# Optimizing a Trainium2 kernel written in Bass

```python
import numpy as np
import jax
import jax.numpy as jnp

def _softmax(x, axis=-1):
    return jax.nn.softmax(x, axis=axis)

def _gelu(x):
    return jax.nn.gelu(x, approximate=True)

def _silu(x):
    return jax.nn.silu(x)

def _sigmoid(x):
    return jax.nn.sigmoid(x)

def _layernorm(x, axis=-1, eps=1e-05):
    m = jnp.mean(x, axis=axis, keepdims=True)
    v = jnp.var(x, axis=axis, keepdims=True)
    return (x - m) / jnp.sqrt(v + eps)

def _scatter_add(tgt, idx, src, axis=0):
    return tgt.at[idx].add(src)

def _segment_sum(src, seg, n):
    return jax.ops.segment_sum(src, seg, n)
kernel_name = 'mk_decoder_preln_d2_seqx_r8_ad5800'

def setup_inputs(seed: int=0):
    np.random.seed(seed)
    _w = jnp.asarray

    def _rec_inputs():
        import jax
        import jax.numpy as jnp
        _rk = jax.random.key(seed)
        x = -0.0002928 + 1 * jax.random.normal(jax.random.fold_in(_rk, 1), (32, 64, 128), jnp.float32)
        _lenS = 64 - jax.random.randint(jax.random.fold_in(_rk, 7), (32,), 0, max(1, 64 // 4) + 1, jnp.int32)
        _lenS2 = 64 - jax.random.randint(jax.random.fold_in(_rk, 8), (32,), 0, max(1, 64 // 4) + 1, jnp.int32)
        _ctx_1024P = jax.random.normal(jax.random.fold_in(_rk, 11), (32, 16, 128), jnp.float32)
        _ctx_1024c = jax.random.dirichlet(jax.random.fold_in(_rk, 511), 0.3 * jnp.ones((16,), jnp.float32), (32, 64))
        _ctx_1024t = jnp.einsum('bsk,bkd->bsd', _ctx_1024c, _ctx_1024P)
        _ctx_1024t = _ctx_1024t * jax.lax.rsqrt(jnp.mean(jnp.square(_ctx_1024t)) + 1e-12) * 0.953939
        ctx_1024 = -1.39393e-06 + 0.999914 * (_ctx_1024t + 0.3 * jax.random.normal(jax.random.fold_in(_rk, 611), (32, 64, 128), jnp.float32))
        _validS = jnp.arange(64)[None, :] < _lenS[:, None]
        _validS2 = jnp.arange(64)[None, :] < _lenS2[:, None]
        _causal = jnp.tril(jnp.ones((64, 64), dtype=bool))
        mask_BxS2_bk0 = jnp.logical_not(jnp.broadcast_to(_validS2[:, :], (32, 64)))
        return (x, ctx_1024, mask_BxS2_bk0)
    x, ctx_1024, mask_BxS2_bk0 = _rec_inputs()

    def _L0_attn_setup():
        import jax, jax.numpy as jnp
        import numpy as np
        D_MODEL = 128
        D_STATE = 16
        D_CONV = 3
        D_INNER = 2 * D_MODEL
        B, S = (4, 256)

        def _mamba_forward(x, in_proj_w, conv_w, conv_b, x_proj_w, dt_proj_w, dt_proj_b, out_proj_w, A_log, D_param):
            combined = x @ in_proj_w
            u, x_gate = jnp.split(combined, 2, axis=-1)
            u_c = jax.lax.conv_general_dilated(u.transpose(0, 2, 1), conv_w, window_strides=(1,), padding='SAME', feature_group_count=D_INNER, dimension_numbers=('NCW', 'OIW', 'NCW'))
            u = jax.nn.silu((u_c + conv_b[None, :, None]).transpose(0, 2, 1))
            x_dbl = u @ x_proj_w
            delta, b, c = jnp.split(x_dbl, [D_INNER, D_INNER + D_STATE], axis=-1)
            delta = jax.nn.softplus(delta @ dt_proj_w + dt_proj_b)
            a = -jnp.exp(A_log)

            def step(h, inp):
                u_t, d_t, b_t, c_t = inp
                h = jnp.exp(d_t[:, :, None] * a) * h + d_t[:, :, None] * b_t[:, None, :] * u_t[:, :, None]
                y_t = jnp.einsum('bds,bs->bd', h, c_t)
                return (h, y_t)
            h0 = jnp.zeros((x.shape[0], D_INNER, D_STATE), x.dtype)
            xs = (u.transpose(1, 0, 2), delta.transpose(1, 0, 2), b.transpose(1, 0, 2), c.transpose(1, 0, 2))
            _, ys = jax.lax.scan(step, h0, xs)
            y = ys.transpose(1, 0, 2)
            y = y + u * D_param
            y = y * jax.nn.silu(x_gate)
            return y @ out_proj_w
        key = jax.random.key(seed)
        ks = jax.random.split(key, 9)
        s = 0.02
        x = jax.random.normal(ks[0], (B, S, D_MODEL), jnp.float32)
        in_proj_w = jax.random.normal(ks[1], (D_MODEL, 2 * D_INNER), jnp.float32) * s
        conv_w = jax.random.normal(ks[2], (D_INNER, 1, D_CONV), jnp.float32) * s
        conv_b = jax.random.normal(ks[3], (D_INNER,), jnp.float32) * s
        x_proj_w = jax.random.normal(ks[4], (D_INNER, D_INNER + 2 * D_STATE), jnp.float32) * s
        dt_proj_w = jax.random.normal(ks[5], (D_INNER, D_INNER), jnp.float32) * s
        dt_proj_b = jax.random.normal(ks[6], (D_INNER,), jnp.float32) * s
        out_proj_w = jax.random.normal(ks[7], (D_INNER, D_MODEL), jnp.float32) * s
        A_log = jnp.tile(jnp.log(jnp.arange(1, D_STATE + 1, dtype=jnp.float32))[None, :], (D_INNER, 1))
        D_param = jnp.ones((D_INNER,), jnp.float32)
        return {'x': x, 'in_proj_w': in_proj_w, 'conv_w': conv_w, 'conv_b': conv_b, 'x_proj_w': x_proj_w, 'dt_proj_w': dt_proj_w, 'dt_proj_b': dt_proj_b, 'out_proj_w': out_proj_w, 'A_log': A_log, 'D_param': D_param}
    _L0_attn_all = _L0_attn_setup()
    _L0_attn_in = {k: v for k, v in _L0_attn_all.items() if k in ('in_proj_w', 'conv_w', 'conv_b', 'x_proj_w', 'dt_proj_w', 'dt_proj_b', 'out_proj_w', 'A_log', 'D_param')}
    del _L0_attn_all

    def _L0_xattn_setup():
        import jax, jax.numpy as jnp
        import numpy as np
        B, N, M, DIM, H, DH = (2, 256, 256, 128, 16, 64)
        INNER = H * DH
        key = jax.random.key(seed)
        ks = jax.random.split(key, 6)
        x = jax.random.normal(ks[0], (B, N, DIM), dtype=jnp.float32)
        cond = jax.random.normal(ks[1], (B, M, DIM), dtype=jnp.float32)
        mask = jax.random.randint(ks[2], (B, M), 0, 2) > 0
        s = 0.02
        Wq = jax.random.normal(ks[3], (DIM, INNER), dtype=jnp.float32) * s
        Wkv = jax.random.normal(ks[4], (DIM, 2 * INNER), dtype=jnp.float32) * s
        Wo = jax.random.normal(ks[5], (INNER, DIM), dtype=jnp.float32) * s
        bo = jnp.zeros((DIM,), dtype=jnp.float32)
        return {'x': x, 'cond': cond, 'mask': mask, 'Wq': Wq, 'Wkv': Wkv, 'Wo': Wo, 'bo': bo}
    _L0_xattn_all = _L0_xattn_setup()
    _L0_xattn_in = {k: v for k, v in _L0_xattn_all.items() if k in ('Wq', 'Wkv', 'Wo', 'bo')}
    del _L0_xattn_all

    def _L0_ffn_setup():
        import jax, jax.numpy as jnp
        import numpy as np
        FF_DIM = 256
        TOP_K = 2
        key = jax.random.key(seed)
        k1, k2, k3, k4 = jax.random.split(key, 4)
        B, S, D, E, F = (2, 256, 128, 8, FF_DIM)
        std = 0.006
        return {'x': jax.random.normal(k1, (B, S, D), dtype=jnp.float32), 'gate_w': jax.random.normal(k2, (D, E), dtype=jnp.float32) * 0.02, 'gate_up_w': jax.random.normal(k3, (E, D, 2 * F), dtype=jnp.float32) * std, 'down_w': jax.random.normal(k4, (E, F, D), dtype=jnp.float32) * std}
    _L0_ffn_all = _L0_ffn_setup()
    _L0_ffn_in = {k: v for k, v in _L0_ffn_all.items() if k in ('gate_w', 'gate_up_w', 'down_w')}
    del _L0_ffn_all

    def _L1_attn_setup():
        import jax, jax.numpy as jnp
        import numpy as np
        ROPE_THETA = 10000.0
        N_HEAD = 16

        def _rope(x, theta):
            T, D = (x.shape[-2], x.shape[-1])
            pos = jnp.arange(T, dtype=jnp.float32)
            inv_freq = 1.0 / theta ** (jnp.arange(0, D, 2, dtype=jnp.float32) / D)
            freqs = pos[:, None] * inv_freq[None, :]
            cos = jnp.cos(freqs).astype(x.dtype)[None, None]
            sin = jnp.sin(freqs).astype(x.dtype)[None, None]
            x_even = x[..., ::2]
            x_odd = x[..., 1::2]
            rot = jnp.stack((x_even * cos - x_odd * sin, x_even * sin + x_odd * cos), axis=-1)
            return rot.reshape(x.shape)
        key = jax.random.key(seed)
        ks = jax.random.split(key, 5)
        B, T, E = (4, 256, 128)
        s = 0.02
        return {'x': jax.random.normal(ks[0], (B, T, E), jnp.float32), 'Wqkv': jax.random.normal(ks[1], (E, 3 * E), jnp.float32) * s, 'bqkv': jax.random.normal(ks[2], (3 * E,), jnp.float32) * s, 'Wproj': jax.random.normal(ks[3], (E, E), jnp.float32) * s, 'bproj': jax.random.normal(ks[4], (E,), jnp.float32) * s}
    _L1_attn_all = _L1_attn_setup()
    _L1_attn_in = {k: v for k, v in _L1_attn_all.items() if k in ('Wqkv', 'bqkv', 'Wproj', 'bproj')}
    del _L1_attn_all

    def _L1_xattn_setup():
        import jax, jax.numpy as jnp
        import numpy as np
        D = 128
        H = 16
        HD = D // H

        def _split_heads(x):
            B, S, _ = x.shape
            return x.reshape(B, S, H, HD).transpose(0, 2, 1, 3)
        key = jax.random.key(seed)
        ks = jax.random.split(key, 11)
        B, S = (4, 256)
        scale = 1.0 / np.sqrt(D)
        inp = {'query': jax.random.normal(ks[0], (B, S, D), jnp.float32), 'key': jax.random.normal(ks[1], (B, S, D), jnp.float32), 'value': jax.random.normal(ks[2], (B, S, D), jnp.float32), 'Wq': jax.random.normal(ks[3], (D, D), jnp.float32) * scale, 'bq': jnp.zeros((D,), jnp.float32), 'Wk': jax.random.normal(ks[4], (D, D), jnp.float32) * scale, 'bk': jnp.zeros((D,), jnp.float32), 'Wv': jax.random.normal(ks[5], (D, D), jnp.float32) * scale, 'bv': jnp.zeros((D,), jnp.float32), 'Wo': jax.random.normal(ks[6], (D, D), jnp.float32) * scale, 'bo': jnp.zeros((D,), jnp.float32)}
        return inp
    _L1_xattn_all = _L1_xattn_setup()
    _L1_xattn_in = {k: v for k, v in _L1_xattn_all.items() if k in ('Wq', 'bq', 'Wk', 'bk', 'Wv', 'bv', 'Wo', 'bo')}
    del _L1_xattn_all

    def _L1_ffn_setup():
        import jax, jax.numpy as jnp
        import numpy as np
        TOP_K = 2

        def _moe(x, Wr, br, W1, b1, W2, b2):
            B, S, D = x.shape
            E = Wr.shape[1]
            xt = x.reshape(-1, D)
            logits = xt @ Wr + br
            top_vals, top_idx = jax.lax.top_k(logits, TOP_K)
            mask = jnp.zeros_like(logits, dtype=bool).at[jnp.arange(xt.shape[0])[:, None], top_idx].set(True)
            sparse_logits = jnp.where(mask, logits, -jnp.inf)
            gate = jax.nn.softmax(sparse_logits, axis=-1)
            h = jax.nn.relu(jnp.einsum('td,edh->teh', xt, W1) + b1)
            y = jnp.einsum('teh,ehd->ted', h, W2) + b2
            out = jnp.einsum('ted,te->td', y, gate)
            return out.reshape(B, S, D)
        key = jax.random.key(seed)
        ks = jax.random.split(key, 5)
        B, S, D, E, H = (2, 256, 128, 8, 512)
        scale = 1.0 / np.sqrt(D)
        return {'x': jax.random.normal(ks[0], (B, S, D), dtype=jnp.float32), 'Wr': jax.random.normal(ks[1], (D, E), dtype=jnp.float32) * scale, 'br': jnp.zeros((E,), dtype=jnp.float32), 'W1': jax.random.normal(ks[2], (E, D, H), dtype=jnp.float32) * scale, 'b1': jnp.zeros((E, H), dtype=jnp.float32), 'W2': jax.random.normal(ks[3], (E, H, D), dtype=jnp.float32) * (1.0 / np.sqrt(H)), 'b2': jnp.zeros((E, D), dtype=jnp.float32)}
    _L1_ffn_all = _L1_ffn_setup()
    _L1_ffn_in = {k: v for k, v in _L1_ffn_all.items() if k in ('Wr', 'br', 'W1', 'b1', 'W2', 'b2')}
    del _L1_ffn_all
    return {'x': x, 'ctx_1024': ctx_1024, 'mask_BxS2_bk0': mask_BxS2_bk0, 'L0_attn_in_proj_w': _L0_attn_in['in_proj_w'], 'L0_attn_conv_w': _L0_attn_in['conv_w'], 'L0_attn_conv_b': _L0_attn_in['conv_b'], 'L0_attn_x_proj_w': _L0_attn_in['x_proj_w'], 'L0_attn_dt_proj_w': _L0_attn_in['dt_proj_w'], 'L0_attn_dt_proj_b': _L0_attn_in['dt_proj_b'], 'L0_attn_out_proj_w': _L0_attn_in['out_proj_w'], 'L0_attn_A_log': _L0_attn_in['A_log'], 'L0_attn_D_param': _L0_attn_in['D_param'], 'L0_xattn_Wq': _L0_xattn_in['Wq'], 'L0_xattn_Wkv': _L0_xattn_in['Wkv'], 'L0_xattn_Wo': _L0_xattn_in['Wo'], 'L0_xattn_bo': _L0_xattn_in['bo'], 'L0_ffn_gate_w': _L0_ffn_in['gate_w'], 'L0_ffn_gate_up_w': _L0_ffn_in['gate_up_w'], 'L0_ffn_down_w': _L0_ffn_in['down_w'], 'L1_attn_Wqkv': _L1_attn_in['Wqkv'], 'L1_attn_bqkv': _L1_attn_in['bqkv'], 'L1_attn_Wproj': _L1_attn_in['Wproj'], 'L1_attn_bproj': _L1_attn_in['bproj'], 'L1_xattn_Wq': _L1_xattn_in['Wq'], 'L1_xattn_bq': _L1_xattn_in['bq'], 'L1_xattn_Wk': _L1_xattn_in['Wk'], 'L1_xattn_bk': _L1_xattn_in['bk'], 'L1_xattn_Wv': _L1_xattn_in['Wv'], 'L1_xattn_bv': _L1_xattn_in['bv'], 'L1_xattn_Wo': _L1_xattn_in['Wo'], 'L1_xattn_bo': _L1_xattn_in['bo'], 'L1_ffn_Wr': _L1_ffn_in['Wr'], 'L1_ffn_br': _L1_ffn_in['br'], 'L1_ffn_W1': _L1_ffn_in['W1'], 'L1_ffn_b1': _L1_ffn_in['b1'], 'L1_ffn_W2': _L1_ffn_in['W2'], 'L1_ffn_b2': _L1_ffn_in['b2']}

def reference(x, ctx_1024, mask_BxS2_bk0, L0_attn_in_proj_w, L0_attn_conv_w, L0_attn_conv_b, L0_attn_x_proj_w, L0_attn_dt_proj_w, L0_attn_dt_proj_b, L0_attn_out_proj_w, L0_attn_A_log, L0_attn_D_param, L0_xattn_Wq, L0_xattn_Wkv, L0_xattn_Wo, L0_xattn_bo, L0_ffn_gate_w, L0_ffn_gate_up_w, L0_ffn_down_w, L1_attn_Wqkv, L1_attn_bqkv, L1_attn_Wproj, L1_attn_bproj, L1_xattn_Wq, L1_xattn_bq, L1_xattn_Wk, L1_xattn_bk, L1_xattn_Wv, L1_xattn_bv, L1_xattn_Wo, L1_xattn_bo, L1_ffn_Wr, L1_ffn_br, L1_ffn_W1, L1_ffn_b1, L1_ffn_W2, L1_ffn_b2):
    import jax
    import jax.numpy as jnp

    def _L0_attn_ref(x, in_proj_w, conv_w, conv_b, x_proj_w, dt_proj_w, dt_proj_b, out_proj_w, A_log, D_param):
        import jax, jax.numpy as jnp
        import numpy as np
        D_MODEL = 128
        D_STATE = 16
        D_CONV = 3
        D_INNER = 2 * D_MODEL
        B, S = (4, 256)

        def _mamba_forward(x, in_proj_w, conv_w, conv_b, x_proj_w, dt_proj_w, dt_proj_b, out_proj_w, A_log, D_param):
            combined = x @ in_proj_w
            u, x_gate = jnp.split(combined, 2, axis=-1)
            u_c = jax.lax.conv_general_dilated(u.transpose(0, 2, 1), conv_w, window_strides=(1,), padding='SAME', feature_group_count=D_INNER, dimension_numbers=('NCW', 'OIW', 'NCW'))
            u = jax.nn.silu((u_c + conv_b[None, :, None]).transpose(0, 2, 1))
            x_dbl = u @ x_proj_w
            delta, b, c = jnp.split(x_dbl, [D_INNER, D_INNER + D_STATE], axis=-1)
            delta = jax.nn.softplus(delta @ dt_proj_w + dt_proj_b)
            a = -jnp.exp(A_log)

            def step(h, inp):
                u_t, d_t, b_t, c_t = inp
                h = jnp.exp(d_t[:, :, None] * a) * h + d_t[:, :, None] * b_t[:, None, :] * u_t[:, :, None]
                y_t = jnp.einsum('bds,bs->bd', h, c_t)
                return (h, y_t)
            h0 = jnp.zeros((x.shape[0], D_INNER, D_STATE), x.dtype)
            xs = (u.transpose(1, 0, 2), delta.transpose(1, 0, 2), b.transpose(1, 0, 2), c.transpose(1, 0, 2))
            _, ys = jax.lax.scan(step, h0, xs)
            y = ys.transpose(1, 0, 2)
            y = y + u * D_param
            y = y * jax.nn.silu(x_gate)
            return y @ out_proj_w
        return _mamba_forward(x, in_proj_w, conv_w, conv_b, x_proj_w, dt_proj_w, dt_proj_b, out_proj_w, A_log, D_param)

    def _L0_xattn_ref(x, cond, mask, Wq, Wkv, Wo, bo):
        import jax, jax.numpy as jnp
        import numpy as np
        B, N, M, DIM, H, DH = (2, 256, 256, 128, 16, 64)
        INNER = H * DH
        b, n, _ = x.shape
        m = cond.shape[1]
        scale = DH ** (-0.5)
        q = (x @ Wq).reshape(b, n, H, DH).transpose(0, 2, 1, 3)
        kv = cond @ Wkv
        k, v = jnp.split(kv, 2, axis=-1)
        k = k.reshape(b, m, H, DH).transpose(0, 2, 1, 3)
        v = v.reshape(b, m, H, DH).transpose(0, 2, 1, 3)
        q = q * scale
        dots = jnp.einsum('bhid,bhjd->bhij', q, k)
        neg = -jnp.finfo(dots.dtype).max
        dots = jnp.where(mask[:, None, None, :], dots, neg)
        causal = jnp.triu(jnp.ones((n, m), dtype=bool), k=m - n + 1)
        dots = jnp.where(causal[None, None, :, :], neg, dots)
        attn = jax.nn.softmax(dots, axis=-1)
        out = jnp.einsum('bhij,bhjd->bhid', attn, v)
        out = out.transpose(0, 2, 1, 3).reshape(b, n, INNER)
        return out @ Wo + bo

    def _L0_ffn_ref(x, gate_w, gate_up_w, down_w):
        import jax, jax.numpy as jnp
        import numpy as np
        FF_DIM = 256
        TOP_K = 2
        B, S, D = x.shape
        E = gate_up_w.shape[0]
        F = down_w.shape[1]
        x_flat = x.reshape(B * S, D)
        router_logits = x_flat @ gate_w
        router_probs = jax.nn.softmax(router_logits, axis=-1)
        top_k_probs, top_k_idx = jax.lax.top_k(router_probs, TOP_K)
        top_k_probs = top_k_probs / jnp.sum(top_k_probs, axis=-1, keepdims=True)
        gate_up = jnp.einsum('nd,edh->enh', x_flat, gate_up_w)
        gate_out = gate_up[..., :F]
        up_out = gate_up[..., F:]
        hidden = jax.nn.silu(gate_out) * up_out
        expert_out = jnp.einsum('enf,efd->end', hidden, down_w)
        out_t = jnp.transpose(expert_out, (1, 0, 2))
        sel = jnp.take_along_axis(out_t, top_k_idx[:, :, None], axis=1)
        output = jnp.sum(sel * top_k_probs[:, :, None], axis=1)
        return output.reshape(B, S, D)

    def _L1_attn_ref(x, Wqkv, bqkv, Wproj, bproj):
        import jax, jax.numpy as jnp
        import numpy as np
        ROPE_THETA = 10000.0
        N_HEAD = 16

        def _rope(x, theta):
            T, D = (x.shape[-2], x.shape[-1])
            pos = jnp.arange(T, dtype=jnp.float32)
            inv_freq = 1.0 / theta ** (jnp.arange(0, D, 2, dtype=jnp.float32) / D)
            freqs = pos[:, None] * inv_freq[None, :]
            cos = jnp.cos(freqs).astype(x.dtype)[None, None]
            sin = jnp.sin(freqs).astype(x.dtype)[None, None]
            x_even = x[..., ::2]
            x_odd = x[..., 1::2]
            rot = jnp.stack((x_even * cos - x_odd * sin, x_even * sin + x_odd * cos), axis=-1)
            return rot.reshape(x.shape)
        B, T, E = x.shape
        H = N_HEAD
        D = E // H
        qkv = x @ Wqkv + bqkv
        q, k, v = jnp.split(qkv, 3, axis=-1)
        q = q.reshape(B, T, H, D).transpose(0, 2, 1, 3)
        k = k.reshape(B, T, H, D).transpose(0, 2, 1, 3)
        v = v.reshape(B, T, H, D).transpose(0, 2, 1, 3)
        q = _rope(q, ROPE_THETA)
        k = _rope(k, ROPE_THETA)
        scores = jnp.einsum('bhqd,bhkd->bhqk', q, k) * D ** (-0.5)
        causal = jnp.tril(jnp.ones((T, T), dtype=bool))
        scores = jnp.where(causal[None, None], scores, -jnp.inf)
        weights = jax.nn.softmax(scores, axis=-1)
        out = jnp.einsum('bhqk,bhkd->bhqd', weights, v)
        out = out.transpose(0, 2, 1, 3).reshape(B, T, E)
        return out @ Wproj + bproj

    def _L1_xattn_ref(query, key, value, Wq, bq, Wk, bk, Wv, bv, Wo, bo):
        import jax, jax.numpy as jnp
        import numpy as np
        D = 128
        H = 16
        HD = D // H

        def _split_heads(x):
            B, S, _ = x.shape
            return x.reshape(B, S, H, HD).transpose(0, 2, 1, 3)
        B, S, _ = query.shape
        q = _split_heads(query @ Wq + bq)
        k = _split_heads(key @ Wk + bk)
        v = _split_heads(value @ Wv + bv)
        scaling = jnp.sqrt(jnp.asarray(HD, jnp.float32))
        attn = jnp.einsum('bhqd,bhkd->bhqk', q, k) / scaling
        causal = 1.0 - jnp.tril(jnp.ones((S, S), jnp.float32))
        attn = attn + causal * -1000000000.0
        probs = jax.nn.softmax(attn, axis=-1)
        out = jnp.einsum('bhqk,bhkd->bhqd', probs, v)
        out = out.transpose(0, 2, 1, 3).reshape(B, S, D)
        return out @ Wo + bo

    def _L1_ffn_ref(x, Wr, br, W1, b1, W2, b2):
        import jax, jax.numpy as jnp
        import numpy as np
        TOP_K = 2

        def _moe(x, Wr, br, W1, b1, W2, b2):
            B, S, D = x.shape
            E = Wr.shape[1]
            xt = x.reshape(-1, D)
            logits = xt @ Wr + br
            top_vals, top_idx = jax.lax.top_k(logits, TOP_K)
            mask = jnp.zeros_like(logits, dtype=bool).at[jnp.arange(xt.shape[0])[:, None], top_idx].set(True)
            sparse_logits = jnp.where(mask, logits, -jnp.inf)
            gate = jax.nn.softmax(sparse_logits, axis=-1)
            h = jax.nn.relu(jnp.einsum('td,edh->teh', xt, W1) + b1)
            y = jnp.einsum('teh,ehd->ted', h, W2) + b2
            out = jnp.einsum('ted,te->td', y, gate)
            return out.reshape(B, S, D)
        return _moe(x, Wr, br, W1, b1, W2, b2)
    x = x + _L0_attn_ref(_layernorm(x, axis=-1), L0_attn_in_proj_w, L0_attn_conv_w, L0_attn_conv_b, L0_attn_x_proj_w, L0_attn_dt_proj_w, L0_attn_dt_proj_b, L0_attn_out_proj_w, L0_attn_A_log, L0_attn_D_param)
    x = x + _L0_xattn_ref(_layernorm(x, axis=-1), ctx_1024, mask_BxS2_bk0, L0_xattn_Wq, L0_xattn_Wkv, L0_xattn_Wo, L0_xattn_bo)
    x = x + _L0_ffn_ref(_layernorm(x, axis=-1), L0_ffn_gate_w, L0_ffn_gate_up_w, L0_ffn_down_w)
    x = x + _L1_attn_ref(_layernorm(x, axis=-1), L1_attn_Wqkv, L1_attn_bqkv, L1_attn_Wproj, L1_attn_bproj)
    x = x + _L1_xattn_ref(_layernorm(x, axis=-1), ctx_1024, ctx_1024, L1_xattn_Wq, L1_xattn_bq, L1_xattn_Wk, L1_xattn_bk, L1_xattn_Wv, L1_xattn_bv, L1_xattn_Wo, L1_xattn_bo)
    x = x + _L1_ffn_ref(_layernorm(x, axis=-1), L1_ffn_Wr, L1_ffn_br, L1_ffn_W1, L1_ffn_b1, L1_ffn_W2, L1_ffn_b2)
    return x

_drawn_inputs = setup_inputs


def setup_inputs(seed=0):
    import zlib

    import numpy as np

    out = dict(_drawn_inputs(seed))
    spreads = {'L0_attn_D_param': (1.0, 0.6),
     'L0_xattn_bo': (0.0, 0.1),
     'L1_xattn_bq': (0.0, 0.492),
     'L1_xattn_bk': (0.0, 2.0),
     'L1_xattn_bv': (0.0, 0.1),
     'L1_xattn_bo': (0.0, 0.1),
     'L1_ffn_br': (0.0, 0.1),
     'L1_ffn_b1': (0.0, 0.545),
     'L1_ffn_b2': (0.0, 0.378)}
    factors = {'L0_attn_in_proj_w': 8.0,
     'L0_attn_conv_w': 8.0,
     'L0_attn_conv_b': 8.0,
     'L0_attn_x_proj_w': 8.0,
     'L0_attn_dt_proj_w': 8.0,
     'L0_attn_dt_proj_b': 8.0,
     'L0_attn_out_proj_w': 7.956,
     'L0_attn_A_log': 8.0,
     'L0_xattn_Wq': 64.0,
     'L0_ffn_gate_w': 7.966,
     'L0_ffn_gate_up_w': 8.0,
     'L0_ffn_down_w': 8.0,
     'L1_attn_bqkv': 19.829,
     'L1_attn_Wqkv': 6.736,
     'L1_attn_Wproj': 4.843,
     'L1_attn_bproj': 4.871}
    for name, (base, spread) in spreads.items():
        noise = np.random.default_rng([zlib.crc32(name.encode()), seed]).standard_normal(out[name].shape)
        drawn = base * np.exp(spread * noise) if base else spread * noise
        out[name] = jnp.asarray(drawn.astype(out[name].dtype))
    for name, factor in factors.items():
        out[name] = (out[name] * factor).astype(out[name].dtype)
    return out
```

```python
from contextlib import ExitStack

import numpy as np

import concourse.bass as bass
from concourse import mybir

F32 = mybir.dt.float32
BF16 = mybir.dt.bfloat16
U8 = mybir.dt.uint8
U32 = mybir.dt.uint32
ALU = mybir.AluOpType
ACT = mybir.ActivationFunctionType
AX = mybir.AxisListType

P = 128
BATCH, S, D = 32, 64, 128
GB = 8
NG = BATCH // GB
T = GB * S
NP = T // P
HEADS = 16
HP = HEADS // 2
DI = 2 * D
NC = DI // P
N = 16
E = 8
F0 = 256
F1 = 512
C0, C1 = F0 // P, F1 // P
HD = D // HEADS
LN_EPS = 1e-5
NEG = -float(np.finfo(np.float32).max)
FAR = 1e28

K_IDENT = 0
K_CAUSAL = K_IDENT + P
K_CAUSAL9 = K_CAUSAL + S
K_COS = K_CAUSAL9 + S
K_SIN = K_COS + S
K_HEAD = K_SIN + S
K_SEL = K_HEAD + HEADS
K_IOTA = K_SEL + 2 * N
K_HALF = K_IOTA + E
K_ALL = K_HALF + NP


def shape_constants():
    k = np.zeros((P, K_ALL), np.float32)
    k[:, K_IDENT:K_CAUSAL] = np.eye(P)
    i = (np.arange(P) % S)[:, None]
    j = np.arange(S)[None, :]
    k[:, K_CAUSAL:K_CAUSAL9] = np.where(j > i, np.float32(NEG), np.float32(0))
    k[:, K_CAUSAL9:K_COS] = np.where(j > i, np.float32(-1e9), np.float32(0))
    inv = (np.float32(1) / np.float32(10000) ** (np.arange(0, HD, 2, dtype=np.float32) / np.float32(HD)))
    freq = (np.arange(S, dtype=np.float32)[:, None] * inv[None, :]).astype(np.float32)
    d = np.arange(P) % HD
    k[:, K_COS:K_SIN] = np.cos(freq)[:, d // 2].T
    k[:, K_SIN:K_HEAD] = np.sin(freq)[:, d // 2].T * np.where(d % 2 == 0, -1, 1)[:, None]
    k[:, K_HEAD:K_SEL] = np.arange(P)[:, None] // HD == np.arange(HEADS)[None, :]
    k[:, K_SEL:K_IOTA] = np.arange(P)[:, None] % (2 * N) == np.arange(2 * N)[None, :]
    k[:, K_IOTA:K_HALF] = np.arange(E)
    k[:, K_HALF:] = -0.5
    return k


class Signal:

    def __init__(self, sem, per_group):
        self.sem, self.per_group = sem, per_group

    def at(self, g, k):
        return g * self.per_group + k


def wait_alone(eng, ready, sem, value):
    value = eng.to_reg(value)
    eng.wait_ge(ready.sem, 1)
    eng.wait_ge(sem, value)


DVE_LINKS = 66
ACT_LINKS = 1


def build(nc, a, out):
    with ExitStack() as ctx:
        def sb(name, shape, dt=F32):
            return ctx.enter_context(nc.sbuf_tensor(name, shape, dt))

        def signal(name, per_group=1):
            return Signal(ctx.enter_context(nc.semaphore(name)), per_group)

        ctx.enter_context(nc.allow_non_contiguous_dma(reason="per-feature vectors"))

        kc = sb("kc", [P, K_ALL])
        ident = kc[:, K_IDENT:K_CAUSAL]
        w_in = sb("w_in", [P, 2 * DI])
        w_conv = sb("w_conv", [P, NC, 3])
        b_conv = sb("b_conv", [P, NC])
        w_xd = sb("w_xd", [P, NC, DI])
        w_xbc = sb("w_xbc", [P, NC, 3, 2 * N])
        w_dt = sb("w_dt", [P, NC, DI])
        b_dt = sb("b_dt", [P, NC])
        w_out = sb("w_out", [P, NC, D])
        a_neg = sb("a_neg", [P, NC, N])
        d_par = sb("d_par", [P, NC])
        sel = sb("sel", [96, 2 * N], BF16)
        w_q0 = sb("w_q0", [P, HP * P])
        w_kv0 = sb("w_kv0", [P, 2 * HP * P])
        w_o0 = sb("w_o0", [P, HP, D])
        bo0 = sb("bo0", [P, D])
        w_r0 = sb("w_r0", [P, E])
        w_gu = sb("w_gu", [P, E, 2 * F0])
        w_dn = sb("w_dn", [P, E, C0, D])
        w_qkv1 = sb("w_qkv1", [P, 3 * D])
        w_sw1 = sb("w_sw1", [P, 2 * D])
        b_qk1 = sb("b_qk1", [P, 2])
        b_sw1 = sb("b_sw1", [P, 2])
        bv1 = sb("bv1", [P, D])
        w_p1 = sb("w_p1", [P, 2, D])
        bo1 = sb("bo1", [P, D])
        w_qkvx = sb("w_qkvx", [P, 3 * D])
        b_qkx = sb("b_qkx", [P, 2])
        bvx = sb("bvx", [P, D])
        w_px = sb("w_px", [P, 2, D])
        box = sb("box", [P, D])
        w_r1 = sb("w_r1", [P, E])
        br1 = sb("br1", [P, E])
        w_1 = sb("w_1", [P, E, F1])
        b_1 = sb("b_1", [P, E, C1])
        w_2 = sb("w_2", [P, E, C1, D])
        b_2 = sb("b_2", [P, NP, D])

        x_in = sb("x_in", [P, NP, D])
        ctx_in = sb("ctx_in", [P, NP, D])
        mask_in = sb("mask_in", [P, T], U8)
        x_res = sb("x_res", [P, NP, D])
        x_out = sb("x_out", [P, NP, D])
        stats = sb("stats", [P, NP, 6])
        mean_var = sb("mean_var", [P, NP, 2])
        var_eps = sb("var_eps", [P, NP])
        rstd = sb("rstd", [P, NP])
        xn = sb("xn", [P, NP, D])
        xT = sb("xT", [P, T])
        ctxT = sb("ctxT", [P, T])
        bias0 = sb("bias0", [P, T])
        kT1 = sb("kT1", [P, T])
        V1 = sb("V1", [P, NP, HP, 18])
        scores = sb("scores", [P, 3, 2 * T])
        row_max = sb("row_max", [P, 3, HP * 2])
        row_sum = sb("row_sum", [P, 3, HP * 2])
        probsT = sb("probsT", [P, 2, HP, P])
        O1 = sb("O1", [P, 2, 2, HP, HD])
        O1T = sb("O1T", [P, NP, 2, S])
        logits = sb("logits", [P, NP, E])
        top = sb("top", [P, NP, 8])
        top_at = sb("top_at", [P, NP, 8], U32)
        top_atf = sb("top_atf", [P, NP, 2])
        top_e = sb("top_e", [P, NP])
        top_w = sb("top_w", [P, NP, 2])
        pick = sb("pick", [P, NP, 2, E])
        gate = sb("gate", [P, NP, 32])
        gateT = sb("gateT", [P, P])
        region = sb("region", [P, 64 * 256])

        def view(at, size, pattern=None, **kw):
            v = region[:, at:at + size]
            return v.rearrange(pattern, **kw) if pattern else v

        def mamba(at):
            return view(at, NC * T, "p (c t) -> p c t", c=NC)
        u_conv, u_act, gate_act = mamba(0), mamba(1024), mamba(2048)
        d_raw, dt_z, dt_e, delta = mamba(3072), mamba(4096), mamba(5120), mamba(6144)
        du, y_gated = mamba(7168), mamba(8192)
        decay = view(9216, 3 * T, "p (r t) -> p r t", r=3)
        bu = view(10752, 3 * T, "p (r t) -> p r t", r=3)
        state = view(12288, 2 * T, "p (r t) -> p r t", r=2)
        hc = view(13312, 3 * T, "p (r t) -> p r t", r=3)
        bc_res = view(14848, T)
        bc_mid = view(15360, T)
        bc_split = sb("bc_split", [96, T], BF16)
        Qd = view(0, HP * GB * P, "p (h b q) -> p h b q", h=HP, b=GB)
        KT = view(8192, HP * T, "p (h t) -> p h t", h=HP)
        V0 = view(12288, NP * HP * P, "p (t f) -> p t f", t=NP)
        q1 = view(8192, T)
        rot_a = view(8704, 2 * T, "p (x t) -> p x t", x=2)
        rot_b = view(9728, 2 * T, "p (x t) -> p x t", x=2)
        hidden = view(0, 2 * 4 * T, "p (s c t) -> p s c t", s=2, c=4)
        silu_g = view(4096, 2 * T, "p (s t) -> p s t", s=2)

        ps = ctx.enter_context(nc.psum_tensor("ps", [P, 8, 512], F32))

        weights = {n: signal(f"w_{n}_loaded") for n in ("mamba", "attn0", "moe0", "attn1", "attnx", "moe1")}
        need = {}
        x_loaded, ctx_loaded, mask_loaded = signal("x_loaded", 16), signal("ctx_loaded", 16), signal("mask_loaded", 16)
        x_stored = signal("x_stored", 16)
        x_free, mask_free, out_free = signal("x_free"), signal("mask_free"), signal("out_free")
        setup = signal("setup")
        a_exp = signal("a_exp")
        zeros_set = signal("zeros_set", NG)
        var_ready, rstd_ready, xn_ready = signal("var_ready", 6), signal("rstd_ready", 6), signal("xn_ready", 6)
        xnT_done, xT_ready = signal("xnT_done", 6), signal("xT_ready", 6)
        ctxT_done, ctxT_ready = signal("ctxT_done"), signal("ctxT_ready")
        biased = signal("biased", 3)
        inproj_done, conv_mid, conv_done, u_ready = signal("inproj_done", 4), signal("conv_mid", 2), signal("conv_done", 2), signal("u_ready", 2)
        gate_ready = signal("gate_ready", 2)
        xproj_done, draw_ready, split_ready = signal("xproj_done", 3), signal("draw_ready", 2), signal("split_ready")
        dt_done, z_ready, nz_ready, ln_ready, delta_ready = signal("dt_done", 2), signal("z_ready", 2), signal("nz_ready"), signal("ln_ready"), signal("delta_ready")
        bc_spread, decay_ready = signal("bc_spread", N), signal("decay_ready", NC * N)
        bu_done, scan_done, hc_done, y_added = signal("bu_done", NC * N), signal("scan_done", NC * N), signal("hc_done", NC * N), signal("y_added", NC * N)
        yg_ready, mamba_done = signal("yg_ready", 2), signal("mamba_done")
        q0_done, q0_top, q0_bottom = signal("q0_done", HP), signal("q0_top", HP), signal("q0_bottom", HP)
        k0_done, k0_even, k0_odd = signal("k0_done", HP), signal("k0_even", HP // 2), signal("k0_odd", HP // 2)
        v0_done, v0_ready = signal("v0_done", NP), signal("v0_ready", NP)
        qd_zero, bias_ready = signal("qd_zero", 2), signal("bias_ready")
        s_done, s_read, s_shifted, exp_done = (signal(n, 3 * NP) for n in ("s_done", "s_read", "s_shifted", "exp_done"))
        sum_ready, normed = signal("sum_ready", NP), signal("normed", NP)
        pT_done, pT_ready, o_done = (signal(n, 3 * NP) for n in ("pT_done", "pT_ready", "o_done"))
        o0_ready = signal("o0_ready", NP)
        o1_ready, o1T_done, o1T_ready = signal("o1_ready", 2 * NP), signal("o1T_done", 2 * NP), signal("o1T_ready", 2 * NP)
        attn_done = signal("attn_done", 3)
        qk1_done, v1_done = signal("qk1_done", 6), signal("v1_done", 2)
        rot_ready, q1_ready, k1_ready, v1_ready = signal("rot_ready", 2), signal("q1_ready", 2), signal("k1_ready", 2), signal("v1_ready", 2)
        qm_dve, qm_act = signal("qm_dve", 2), signal("qm_act", 2)
        route_done, top_ready, tope_ready, gate_w = signal("route_done", 2), signal("top_ready", 2), signal("tope_ready", 2), signal("gate_w", 2)
        gu_done, silu_done, h0_done = signal("gu_done", 2 * E), signal("silu_done", 2 * E), signal("h0_done", 2 * E)
        up_done, h1_act, h1_dve = signal("up_done", C1 * E), signal("h1_act", C1 * E // 2), signal("h1_dve", C1 * E // 2)
        down_done, acc_done = signal("down_done", 2 * E), signal("acc_done", 2 * E)
        gateT_done, gateT_ready, b2_done = signal("gateT_done"), signal("gateT_ready"), signal("b2_done")
        dve_chain, act_chain = signal("dve_chain", DVE_LINKS), signal("act_chain", ACT_LINKS)

        block = ctx.enter_context(nc.Block())

        @block.sync
        def _(sp):
            def load(group, dst, src):
                sp.dma_start(dst, src).then_inc(weights[group].sem, 16)
                need[group] = need.get(group, 0) + 16

            def column(name, n):
                return a[name].rearrange("(c p) -> p c", p=n)

            def row(name):
                return a[name].partition_broadcast(P)

            def load_x(g):
                sp.dma_start(x_in[:], pairs_of(a["x"], g)).then_inc(x_loaded.sem, 16)

            def load_ctx(g):
                sp.dma_start(ctx_in[:], pairs_of(a["ctx_1024"], g)).then_inc(ctx_loaded.sem, 16)

            def load_mask(g):
                src = a["mask_BxS2_bk0"].rearrange("b s -> (b s)")[bass.ds(g * T, T)]
                sp.dma_start(mask_in[:], src.partition_broadcast(P)).then_inc(mask_loaded.sem, 16)

            def store_x(g):
                sp.wait_ge(acc_done.sem, acc_done.at(g, 2 * E))
                sp.dma_start(pairs_of(out, g), x_out[:]).then_inc(x_stored.sem, 16)
                sp.wait_ge(x_stored.sem, x_stored.at(g, 16))
                sp.nop().then_inc(out_free.sem, 1)

            sp.nop().then_inc(out_free.sem, 1)
            load_x(0)
            load("mamba", kc[:], a["shape_constants"])
            load("mamba", w_in[:], a["L0_attn_in_proj_w"])
            load("mamba", w_conv[:], a["L0_attn_conv_w"].rearrange("(c p) a k -> p c (a k)", p=P))
            load("mamba", b_conv[:], column("L0_attn_conv_b", P))
            xp = a["L0_attn_x_proj_w"].rearrange("(c p) n -> p c n", p=P)
            load("mamba", w_xd[:], xp[:, :, 0:DI])
            for k in range(3):
                load("mamba", w_xbc[:, :, k, :], xp[:, :, DI:])
            load("mamba", w_dt[:], a["L0_attn_dt_proj_w"].rearrange("(c p) n -> p c n", p=P))
            load("mamba", b_dt[:], column("L0_attn_dt_proj_b", P))
            load("mamba", a_neg[:], a["L0_attn_A_log"].rearrange("(c p) n -> p c n", p=P))
            load("mamba", d_par[:], column("L0_attn_D_param", P))
            load("mamba", w_out[:], a["L0_attn_out_proj_w"].rearrange("(c p) n -> p c n", p=P))
            load_ctx(0)
            load_mask(0)
            load("attn0", w_q0[:], a["L0_xattn_Wq"])
            load("attn0", w_kv0[:], a["L0_xattn_Wkv"])
            load("attn0", w_o0[:], a["L0_xattn_Wo"].rearrange("(c p) n -> p c n", p=P))
            load("attn0", bo0[:], row("L0_xattn_bo"))
            load("moe0", w_r0[:], a["L0_ffn_gate_w"])
            load("moe0", w_gu[:], a["L0_ffn_gate_up_w"].rearrange("e p f -> p e f"))
            load("moe0", w_dn[:], a["L0_ffn_down_w"].rearrange("e (c p) n -> p e c n", p=P))
            load("attn1", w_qkv1[:], a["L1_attn_Wqkv"])
            bqkv = a["L1_attn_bqkv"]
            load("attn1", b_qk1[:], bqkv[0:2 * D].rearrange("(c p) -> p c", p=P))
            load("attn1", bv1[:], bqkv[2 * D:3 * D].partition_broadcast(P))
            for odd in range(2):
                src = bqkv[0:2 * D].rearrange("(c k two) -> two k c", c=2, two=2)[1 - odd]
                load("attn1", b_sw1[odd:P:2, :], src)
            for name, dst, group in (("L1_attn_Wproj", w_p1, "attn1"), ("L1_xattn_Wo", w_px, "attnx")):
                src = a[name].rearrange("(hp e d) n -> hp d e n", e=2, d=HD)
                for copy in range(2):
                    for hp in range(HP):
                        at = copy * S + hp * HD
                        load(group, dst[at:at + HD, :, :], src[hp])
            load("attn1", bo1[:], row("L1_attn_bproj"))
            for i, n in enumerate("qkv"):
                load("attnx", w_qkvx[:, i * D:(i + 1) * D], a[f"L1_xattn_W{n}"])
            load("attnx", b_qkx[:, 0:1], column("L1_xattn_bq", P))
            load("attnx", b_qkx[:, 1:2], column("L1_xattn_bk", P))
            load("attnx", bvx[:], row("L1_xattn_bv"))
            load("attnx", box[:], row("L1_xattn_bo"))
            load("moe1", w_r1[:], a["L1_ffn_Wr"])
            load("moe1", br1[:], row("L1_ffn_br"))
            load("moe1", w_1[:], a["L1_ffn_W1"].rearrange("e p f -> p e f"))
            load("moe1", b_1[:], a["L1_ffn_b1"].rearrange("e (c p) -> p e c", p=P))
            load("moe1", w_2[:], a["L1_ffn_W2"].rearrange("e (c p) n -> p e c n", p=P))
            sp.wait_ge(zeros_set.sem, 1)
            for t in range(NP):
                load("moe1", b_2[32 * t:32 * t + E, t, :], a["L1_ffn_b2"])
            with sp.Fori(0, NG - 1) as g:
                sp.wait_ge(x_free.sem, x_free.at(g, 1))
                load_x(g + 1)
                sp.wait_ge(ctxT_done.sem, ctxT_done.at(g, 1))
                load_ctx(g + 1)
                wait_alone(sp, zeros_set, mask_free.sem, mask_free.at(g, 1))
                load_mask(g + 1)
                store_x(g)
            store_x(NG - 1)

        @block.tensor
        def _(pe):
            def mm(out_ap, lhsT, rhs, start=True, stop=True, **kw):
                return pe.matmul(out_ap, lhsT, rhs, start=start, stop=stop, **kw)

            def turn_norm(g, l):
                pe.wait_ge(xn_ready.sem, xn_ready.at(g, l + 1))
                for t in range(NP):
                    ins = pe.transpose(ps[:, 7, t * P:(t + 1) * P], xn[:, t, :], ident)
                ins.then_inc(xnT_done.sem, 1)

            def in_proj(g):
                pe.wait_ge(xT_ready.sem, xT_ready.at(g, 1))
                for m in range(2 * NC):
                    mm(ps[:, m, :], w_in[:, m * P:(m + 1) * P], xT[:]).then_inc(inproj_done.sem, 1)

            def turn_ctx(g):
                pe.wait_ge(ctx_loaded.sem, ctx_loaded.at(g, 16))
                for t in range(NP):
                    ins = pe.transpose(ps[:, 6, t * P:(t + 1) * P], ctx_in[:, t, :], ident)
                ins.then_inc(ctxT_done.sem, 1)

            def x_proj(g):
                pe.wait_ge(u_ready.sem, u_ready.at(g, 2))
                for m in range(NC):
                    for c in range(NC):
                        ins = mm(ps[:, 4 + m, :], w_xd[:, c, m * P:(m + 1) * P], u_act[:, c, :], c == 0, c == NC - 1)
                    ins.then_inc(xproj_done.sem, 1)
                pe.wait_ge(ctxT_ready.sem, ctxT_ready.at(g, 1))
                for c in range(NC):
                    ins = mm(ps[0:96, 6, :], w_xbc[:, c, :, :], u_act[:, c, :], c == 0, c == NC - 1)
                ins.then_inc(xproj_done.sem, 1)

            def dt_proj(g):
                pe.wait_ge(draw_ready.sem, draw_ready.at(g, 2))
                for m in range(NC):
                    for c in range(NC):
                        ins = mm(ps[:, m, :], w_dt[:, c, m * P:(m + 1) * P], d_raw[:, c, :], c == 0, c == NC - 1)
                    ins.then_inc(dt_done.sem, 1)

            def spread_bc(g, n):
                if n >= 2:
                    pe.wait_ge(hc_done.sem, hc_done.at(g, NC * (n - 1)))
                mm(ps[:, 2 + n % 2, :], sel[:, n:n + 1].to_broadcast([96, P]), bc_split[:])
                mm(ps[:, 4 + n % 2, :], sel[:, N + n:N + n + 1].to_broadcast([96, P]), bc_split[:]).then_inc(bc_spread.sem, 1)

            def add_y(g, n):
                for c in range(NC):
                    k = NC * n + c
                    pe.wait_ge(hc_done.sem, hc_done.at(g, k + 1))
                    mm(ps[:, c, :], ident, hc[:, k % 3, :], n == 0, n == N - 1).then_inc(y_added.sem, 1)

            def mamba_out(g):
                pe.wait_ge(yg_ready.sem, yg_ready.at(g, 2))
                for t in range(NP):
                    for c in range(NC):
                        ins = mm(ps[:, 6, t * P:(t + 1) * P], y_gated[:, c, t * P:(t + 1) * P], w_out[:, c, :], c == 0, c == NC - 1)
                ins.then_inc(mamba_done.sem, 1)

            def project0(g):
                pe.wait_ge(xT_ready.sem, xT_ready.at(g, 2))
                for h in range(HP):
                    if h >= 4:
                        pe.wait_ge(q0_top.sem, q0_top.at(g, h - 3))
                        pe.wait_ge(q0_bottom.sem, q0_bottom.at(g, h - 3))
                    mm(ps[:, h % 4, :], w_q0[:, h * P:(h + 1) * P], xT[:]).then_inc(q0_done.sem, 1)
                for h in range(HP):
                    if h >= 3:
                        ready = k0_even if (h - 3) % 2 == 0 else k0_odd
                        pe.wait_ge(ready.sem, ready.at(g, (h - 3) // 2 + 1))
                    mm(ps[:, 4 + h % 3, :], w_kv0[:, h * P:(h + 1) * P], ctxT[:]).then_inc(k0_done.sem, 1)
                pe.wait_ge(q0_top.sem, q0_top.at(g, HP))
                pe.wait_ge(q0_bottom.sem, q0_bottom.at(g, HP))
                for t in range(NP):
                    if t >= 2:
                        pe.wait_ge(v0_ready.sem, v0_ready.at(g, t - 1))
                    for half in range(2):
                        cols = w_kv0[:, HP * P + half * 512:HP * P + (half + 1) * 512]
                        ins = mm(ps[:, 2 * (t % 2) + half, :], ctxT[:, t * P:(t + 1) * P], cols)
                    ins.then_inc(v0_done.sem, 1)

            def scores_of(g, k, p, keys):
                if k == 0 and p == 0:
                    pe.wait_ge(k0_even.sem, k0_even.at(g, HP // 2))
                    pe.wait_ge(k0_odd.sem, k0_odd.at(g, HP // 2))
                    pe.wait_ge(v0_ready.sem, v0_ready.at(g, NP))
                if k > 0 and p == 0:
                    pe.wait_ge(qm_dve.sem, qm_dve.at(g, k))
                    pe.wait_ge(qm_act.sem, qm_act.at(g, k))
                    pe.wait_ge(k1_ready.sem, k1_ready.at(g, k))
                    pe.wait_ge(v1_ready.sem, v1_ready.at(g, k))
                if p >= 2:
                    pe.wait_ge(s_read.sem, s_read.at(g, k * NP + p - 1))
                s_ps = ps[:, 2 * (p % 2):2 * (p % 2) + 2, :].rearrange("p k f -> p (k f)")
                for h in range(HP):
                    for s2 in range(2):
                        b = 2 * p + s2
                        at = (2 * h + s2) * S
                        ins = mm(s_ps[:, at:at + S], Qd[:, h, b, :], keys(h)[:, b * S:(b + 1) * S])
                ins.then_inc(s_done.sem, 1)

            def turn_probs(g, k, p):
                if k == 0:
                    pe.wait_ge(normed.sem, normed.at(g, p + 1))
                else:
                    pe.wait_ge(exp_done.sem, exp_done.at(g, k * NP + p + 1))
                if p >= 1:
                    pe.wait_ge(pT_ready.sem, pT_ready.at(g, k * NP + p))
                for h in range(HP):
                    at = h * P
                    ins = pe.transpose(ps[:, 4 + h // 4, (h % 4) * P:(h % 4 + 1) * P], scores[:, p % 3, at:at + P], ident)
                ins.then_inc(pT_done.sem, 1)

            def weigh_values0(g, p):
                if p >= 1:
                    pe.wait_ge(o0_ready.sem, o0_ready.at(g, p))
                wait_alone(pe, weights["attn0"], pT_ready.sem, pT_ready.at(g, p + 1))
                for h in range(HP):
                    for e in range(2):
                        for s2 in range(2):
                            r = slice(s2 * S, s2 * S + S)
                            ins = mm(ps[e * S:(e + 1) * S, 6 + s2, h * S:(h + 1) * S],
                                     V0[r, p, h * P + e * S:h * P + (e + 1) * S],
                                     probsT[r, p % 2, h, e * S:(e + 1) * S])
                ins.then_inc(o_done.sem, 1)

            def attn0_out(g):
                pe.wait_ge(o0_ready.sem, o0_ready.at(g, NP))
                for t in range(NP):
                    for h in range(HP):
                        ins = mm(ps[:, 0, t * P:(t + 1) * P], KT[:, h, t * P:(t + 1) * P], w_o0[:, h, :], h == 0, h == HP - 1)
                ins.then_inc(attn_done.sem, 1)

            def weigh_values1(g, k, p):
                pe.wait_ge(pT_ready.sem, pT_ready.at(g, k * NP + p + 1))
                if p >= 1:
                    pe.wait_ge(o1T_ready.sem, o1T_ready.at(g, (k - 1) * NP + p))
                for h in range(HP):
                    for s2 in range(2):
                        r = slice(s2 * S, s2 * S + S)
                        ins = mm(ps[:, 6 + s2, h * 18:h * 18 + 17], probsT[r, p % 2, h, :], V1[r, p, h, 0:17])
                ins.then_inc(o_done.sem, 1)

            def turn_o1(g, k, p):
                pe.wait_ge(o1_ready.sem, o1_ready.at(g, (k - 1) * NP + p + 1))
                pe.transpose(ps[:, 6, 256:384], O1[:, p % 2].rearrange("p s h d -> p (s h d)"), ident).then_inc(o1T_done.sem, 1)

            def attn1_out(g, k, w_p):
                wait_alone(pe, weights["attn0"], o1T_ready.sem, o1T_ready.at(g, k * NP))
                for t in range(NP):
                    for e in range(2):
                        for s2 in range(2):
                            r = slice(s2 * S, s2 * S + S)
                            ins = mm(ps[r, s2, t * P:(t + 1) * P], O1T[r, t, e, :], w_p[r, e, :], e == 0, e == 1)
                ins.then_inc(attn_done.sem, 1)

            def project1(g, k):
                pe.wait_ge(xT_ready.sem, xT_ready.at(g, 3 + k))
                if k == 1:
                    for c in range(2):
                        mm(ps[:, 2 * c, :], w_qkv1[:, c * D:(c + 1) * D], xT[:]).then_inc(qk1_done.sem, 1)
                        mm(ps[:, 2 * c + 1, :], w_sw1[:, c * D:(c + 1) * D], xT[:]).then_inc(qk1_done.sem, 1)
                    src, w_v = xT, w_qkv1[:, 2 * D:]
                else:
                    mm(ps[:, 0, :], w_qkvx[:, 0:D], xT[:]).then_inc(qk1_done.sem, 1)
                    mm(ps[:, 2, :], w_qkvx[:, D:2 * D], ctxT[:]).then_inc(qk1_done.sem, 1)
                    src, w_v = ctxT, w_qkvx[:, 2 * D:]
                for t in range(NP):
                    ins = mm(ps[:, 4, t * P:(t + 1) * P], src[:, t * P:(t + 1) * P], w_v)
                ins.then_inc(v1_done.sem, 1)

            def attention1(g, k, w_p):
                def keys(h):
                    return kT1
                scores_of(g, k, 0, keys)
                for p in range(NP):
                    if p + 1 < NP:
                        scores_of(g, k, p + 1, keys)
                    turn_probs(g, k, p)
                    weigh_values1(g, k, p)
                    turn_o1(g, k, p)
                attn1_out(g, k, w_p)

            def route(g, m, w_r):
                pe.wait_ge(xT_ready.sem, xT_ready.at(g, 3 if m == 0 else 6))
                for t in range(NP):
                    ins = mm(ps[:, 7, t * E:(t + 1) * E], xT[:, t * P:(t + 1) * P], w_r[:])
                ins.then_inc(route_done.sem, 1)

            def down(g, m, e, chunks, w, ready):
                ready(e)
                if e >= 2:
                    pe.wait_ge(acc_done.sem, acc_done.at(g, m * E + e - 1))
                elif e == 1:
                    pe.wait_ge(top_ready.sem, top_ready.at(g, m + 1))
                for t in range(NP):
                    for c in range(chunks):
                        ins = mm(ps[:, 6 + e % 2, t * P:(t + 1) * P], hidden[:, e % 2, c, t * P:(t + 1) * P], w[:, e, c, :], c == 0, c == chunks - 1)
                ins.then_inc(down_done.sem, 1)

            def experts0(g):
                def ready(e):
                    pe.wait_ge(h0_done.sem, h0_done.at(g, C0 * (e + 1)))
                for e in range(E + 1):
                    for c in range(C0 if e < E else 0):
                        k = e * C0 + c
                        if k >= 3:
                            pe.wait_ge(h0_done.sem, h0_done.at(g, k - 2))
                        q = 2 * (k % 3)
                        mm(ps[:, q, :], w_gu[:, e, c * P:(c + 1) * P], xT[:])
                        mm(ps[:, q + 1, :], w_gu[:, e, F0 + c * P:F0 + (c + 1) * P], xT[:]).then_inc(gu_done.sem, 1)
                    if e >= 1:
                        down(g, 0, e - 1, C0, w_dn, ready)

            def experts1(g):
                def ready(e):
                    pe.wait_ge(h1_act.sem, h1_act.at(g, (e + 1) * C1 // 2))
                    pe.wait_ge(h1_dve.sem, h1_dve.at(g, (e + 1) * C1 // 2))
                for e in range(E + 1):
                    for c in range(C1 if e < E else 0):
                        k = e * C1 + c
                        if k >= 6:
                            by = h1_act if k % 2 == 0 else h1_dve
                            pe.wait_ge(by.sem, by.at(g, (k - 6) // 2 + 1))
                        mm(ps[:, k % 6, :], w_1[:, e, c * P:(c + 1) * P], xT[:]).then_inc(up_done.sem, 1)
                    if e == 0:
                        pe.wait_ge(gate_w.sem, gate_w.at(g, 2))
                        pe.transpose(ps[:, 6, 0:P], gate.rearrange("p t e -> p (t e)"), ident).then_inc(gateT_done.sem, 1)
                        pe.wait_ge(gateT_ready.sem, gateT_ready.at(g, 1))
                        for t in range(NP):
                            ins = mm(ps[:, 7, t * P:(t + 1) * P], gateT[:], b_2[:, t, :])
                        ins.then_inc(b2_done.sem, 1)
                    if e >= 1:
                        down(g, 1, e - 1, C1, w_2, ready)

            pe.wait_ge(weights["mamba"].sem, need["mamba"])
            with pe.Fori(0, NG) as g:
                turn_norm(g, 0)
                in_proj(g)
                turn_ctx(g)
                x_proj(g)
                dt_proj(g)
                pe.wait_ge(split_ready.sem, split_ready.at(g, 1))
                pe.wait_ge(delta_ready.sem, delta_ready.at(g, 1))
                spread_bc(g, 0)
                spread_bc(g, 1)
                for n in range(N):
                    add_y(g, n)
                    if n + 2 < N:
                        spread_bc(g, n + 2)
                mamba_out(g)
                turn_norm(g, 1)
                pe.wait_ge(weights["attn0"].sem, need["attn0"])
                project0(g)
                def keys0(h):
                    return KT[:, h, :]
                scores_of(g, 0, 0, keys0)
                for p in range(NP):
                    if p + 1 < NP:
                        scores_of(g, 0, p + 1, keys0)
                    turn_probs(g, 0, p)
                    weigh_values0(g, p)
                attn0_out(g)
                turn_norm(g, 2)
                pe.wait_ge(weights["moe0"].sem, need["moe0"])
                route(g, 0, w_r0)
                experts0(g)
                turn_norm(g, 3)
                pe.wait_ge(weights["attn1"].sem, need["attn1"])
                project1(g, 1)
                attention1(g, 1, w_p1)
                turn_norm(g, 4)
                pe.wait_ge(weights["attnx"].sem, need["attnx"])
                project1(g, 2)
                attention1(g, 2, w_px)
                turn_norm(g, 5)
                pe.wait_ge(weights["moe1"].sem, need["moe1"])
                route(g, 1, w_r1)
                experts1(g)

        @block.scalar
        def _(act):
            def copy_norm(g, l):
                act.wait_ge(xnT_done.sem, xnT_done.at(g, l + 1))
                act.copy(xT[:], ps[:, 7, :]).then_inc(xT_ready.sem, 1)

            def exps(g, k, p):
                act.wait_ge(s_shifted.sem, s_shifted.at(g, k * NP + p + 1))
                act.activation(scores[:, p % 3, :], scores[:, p % 3, :], ACT.Exp).then_inc(exp_done.sem, 1)

            def copy_probs(g, k, p):
                act.wait_ge(pT_done.sem, pT_done.at(g, k * NP + p + 1))
                if p >= 2:
                    act.wait_ge(o_done.sem, o_done.at(g, k * NP + p - 1))
                act.copy(probsT[:, p % 2].rearrange("p h q -> p (h q)"),
                         ps[:, 4:6, :].rearrange("p k f -> p (k f)")).then_inc(pT_ready.sem, 1)

            act.wait_ge(weights["mamba"].sem, need["mamba"])
            act.activation(a_neg[:], a_neg[:], ACT.Exp).then_inc(a_exp.sem, 1)
            with act.Fori(0, NG) as g:
                copy_norm(g, 0)
                for c in range(NC):
                    act.wait_ge(inproj_done.sem, inproj_done.at(g, c + 1))
                    act.activation(u_conv[:, c, :], ps[:, c, :], ACT.Identity, bias=b_conv[:, c:c + 1],
                                   scale=w_conv[:, c, 1:2]).then_inc(conv_mid.sem, 1)
                for c in range(NC):
                    act.wait_ge(inproj_done.sem, inproj_done.at(g, NC + c + 1))
                    act.activation(gate_act[:, c, :], ps[:, NC + c, :], ACT.Silu).then_inc(gate_ready.sem, 1)
                for c in range(NC):
                    act.wait_ge(conv_done.sem, conv_done.at(g, c + 1))
                    act.activation(u_act[:, c, :], u_conv[:, c, :], ACT.Silu).then_inc(u_ready.sem, 1)
                act.wait_ge(ctxT_done.sem, ctxT_done.at(g, 1))
                act.copy(ctxT[:], ps[:, 6, :]).then_inc(ctxT_ready.sem, 1)
                for c in range(NC):
                    act.wait_ge(xproj_done.sem, xproj_done.at(g, c + 1))
                    act.copy(d_raw[:, c, :], ps[:, 4 + c, :]).then_inc(draw_ready.sem, 1)
                for c in range(NC):
                    act.wait_ge(dt_done.sem, dt_done.at(g, c + 1))
                    act.activation(dt_z[:, c, :], ps[:, c, :], ACT.Identity, bias=b_dt[:, c:c + 1]).then_inc(z_ready.sem, 1)
                act.wait_ge(nz_ready.sem, nz_ready.at(g, 1))
                act.activation(dt_e, dt_e, ACT.Exp).then_inc(act_chain.sem, 1)
                act.wait_ge(act_chain.sem, act_chain.at(g, 1))
                act.activation(dt_e, dt_e, ACT.Ln, bias=1.0).then_inc(ln_ready.sem, 1)
                act.wait_ge(delta_ready.sem, delta_ready.at(g, 1))
                for k in range(NC * N):
                    n, c = k // NC, k % NC
                    if k >= 3:
                        act.wait_ge(scan_done.sem, scan_done.at(g, k - 2))
                    act.activation(decay[:, k % 3, :], delta[:, c, :], ACT.Exp,
                                   scale=a_neg[:, c, n:n + 1]).then_inc(decay_ready.sem, 1)
                copy_norm(g, 1)
                act.wait_ge(qd_zero.sem, qd_zero.at(g, 2))
                for h in range(HP):
                    act.wait_ge(q0_done.sem, q0_done.at(g, h + 1))
                    act.mul(Qd[0:S, h, :, 0:S], ps[0:S, h % 4, :].rearrange("p (b i) -> p b i", b=GB), 0.125).then_inc(q0_top.sem, 1)
                for h in range(0, HP, 2):
                    act.wait_ge(k0_done.sem, k0_done.at(g, h + 1))
                    act.copy(KT[:, h, :], ps[:, 4 + h % 3, :]).then_inc(k0_even.sem, 1)
                for p in range(NP + 1):
                    if p < NP:
                        exps(g, 0, p)
                    if p >= 1:
                        copy_probs(g, 0, p - 1)
                        act.wait_ge(o_done.sem, o_done.at(g, p))
                        act.copy(KT[:, :, (p - 1) * P:p * P].rearrange("p h (s i) -> p s h i", s=2),
                                 ps[:, 6:8, :].rearrange("p s (h i) -> p s h i", h=HP)).then_inc(o0_ready.sem, 1)
                copy_norm(g, 2)
                act.wait_ge(top_ready.sem, top_ready.at(g, 1))
                act.activation(top_e[:], top_e[:], ACT.Exp).then_inc(tope_ready.sem, 1)
                for k in range(E * C0):
                    act.wait_ge(gu_done.sem, gu_done.at(g, k + 1))
                    if k >= 2:
                        act.wait_ge(h0_done.sem, h0_done.at(g, k - 1))
                    act.activation(silu_g[:, k % 2, :], ps[:, 2 * (k % 3), :], ACT.Silu).then_inc(silu_done.sem, 1)
                for k in (1, 2):
                    copy_norm(g, 2 + k)
                    if k == 2:
                        act.wait_ge(qk1_done.sem, qk1_done.at(g, 5))
                        act.activation(q1, ps[:, 0, :], ACT.Identity, bias=b_qkx[:, 0:1]).then_inc(q1_ready.sem, 1)
                        act.wait_ge(qk1_done.sem, qk1_done.at(g, 6))
                        act.activation(kT1[:], ps[:, 2, :], ACT.Identity, bias=b_qkx[:, 1:2]).then_inc(k1_ready.sem, 1)
                    act.wait_ge(q1_ready.sem, q1_ready.at(g, k))
                    for h in range(HEADS - 6, HEADS):
                        ins = act.mul(Qd[:, h // 2, :, (h % 2) * S:(h % 2 + 1) * S], q1.rearrange("p (b i) -> p b i", b=GB),
                                      kc[:, K_HEAD + h:K_HEAD + h + 1])
                    ins.then_inc(qm_act.sem, 1)
                    for p in range(NP + 1):
                        if p < NP:
                            exps(g, k, p)
                        if p >= 1:
                            copy_probs(g, k, p - 1)
                            act.wait_ge(o1T_done.sem, o1T_done.at(g, (k - 1) * NP + p))
                            act.copy(O1T[:, p - 1].rearrange("p e i -> p (e i)"), ps[:, 6, 256:384]).then_inc(o1T_ready.sem, 1)
                copy_norm(g, 5)
                act.wait_ge(top_ready.sem, top_ready.at(g, 2))
                act.activation(top_e[:], top_e[:], ACT.Exp).then_inc(tope_ready.sem, 1)
                for k in range(0, E * C1, 2):
                    if k == 4:
                        act.wait_ge(gateT_done.sem, gateT_done.at(g, 1))
                        act.copy(gateT[:], ps[:, 6, 0:P]).then_inc(gateT_ready.sem, 1)
                    e, c = k // C1, k % C1
                    act.wait_ge(up_done.sem, up_done.at(g, k + 1))
                    if e >= 2 and c == 0:
                        act.wait_ge(down_done.sem, down_done.at(g, E + e - 1))
                    act.activation(hidden[:, e % 2, c, :], ps[:, k % 6, :], ACT.Relu, bias=b_1[:, e, c:c + 1]).then_inc(h1_act.sem, 1)

        @block.gpsimd
        def _(pool):
            def roots(g, l):
                pool.wait_ge(var_ready.sem, var_ready.at(g, l + 1))
                pool.tensor_tensor(rstd[:], var_eps[:], kc[:, K_HALF:K_ALL], ALU.pow).then_inc(rstd_ready.sem, 1)

            def add_bias(g, l, bias):
                pool.wait_ge(xn_ready.sem, xn_ready.at(g, l + 1))
                pool.tensor_tensor(x_res[:], x_res[:], bias[:].unsqueeze(1).to_broadcast([P, NP, D]), ALU.add).then_inc(biased.sem, 1)

            pool.memset(b_2[:], 0.0).then_inc(zeros_set.sem, 1)
            pool.memset(gate[:], 0.0).then_inc(zeros_set.sem, 1)
            pool.memset(V1[:, :, :, 16:18], 1.0).then_inc(zeros_set.sem, 1)
            pool.wait_ge(weights["mamba"].sem, need["mamba"])
            with pool.Fori(0, NG) as g:
                roots(g, 0)
                roots(g, 1)
                wait_alone(pool, zeros_set, rstd_ready.sem, rstd_ready.at(g, 2))
                pool.memset(Qd[0:S, :, :, S:P], 0.0).then_inc(qd_zero.sem, 1)
                wait_alone(pool, zeros_set, qd_zero.sem, qd_zero.at(g, 1))
                pool.memset(Qd[S:P, :, :, 0:S], 0.0).then_inc(qd_zero.sem, 1)
                pool.wait_ge(qd_zero.sem, qd_zero.at(g, 2))
                pool.wait_ge(weights["attn0"].sem, need["attn0"])
                add_bias(g, 1, bo0)
                for p in range(NP):
                    pool.wait_ge(sum_ready.sem, sum_ready.at(g, p + 1))
                    v = scores[:, p % 3, :].rearrange("p (r j) -> p r j", j=S)
                    pool.tensor_tensor(v, v, row_sum[:, p % 3, :].unsqueeze(2).to_broadcast([P, 2 * HP, S]), ALU.mult).then_inc(normed.sem, 1)
                roots(g, 2)
                roots(g, 3)
                pool.wait_ge(weights["attn1"].sem, need["attn1"])
                add_bias(g, 3, bo1)
                roots(g, 4)
                pool.wait_ge(weights["attnx"].sem, need["attnx"])
                add_bias(g, 4, box)
                roots(g, 5)

        @block.vector
        def _(dve):
            links = [0]

            def link(g, ins):
                links[0] += 1
                ins.then_inc(dve_chain.sem, 1)
                dve.wait_ge(dve_chain.sem, dve_chain.at(g, links[0]))

            def link_alone(g, ins):
                links[0] += 1
                ins.then_inc(dve_chain.sem, 1)
                wait_alone(dve, setup, dve_chain.sem, dve_chain.at(g, links[0]))

            def norm(g, l):
                src = x_in if l == 0 else x_res
                if l == 0:
                    dve.wait_ge(x_loaded.sem, x_loaded.at(g, 16))
                for t in range(NP):
                    ins = dve.bn_stats(stats[:, t, :], src[:, t, :])
                link_alone(g, ins)
                for t in range(NP):
                    ins = dve.bn_aggr(mean_var[:, t, :], stats[:, t, :])
                link(g, ins)
                dve.tensor_scalar(var_eps[:], mean_var[:, :, 1], LN_EPS, None, ALU.add).then_inc(var_ready.sem, 1)
                dve.wait_ge(rstd_ready.sem, rstd_ready.at(g, l + 1))
                for t in range(NP):
                    ins = dve.tensor_scalar(xn[:, t, :], src[:, t, :], mean_var[:, t, 0:1], rstd[:, t:t + 1], ALU.subtract, ALU.mult)
                ins.then_inc(xn_ready.sem, 1)

            def scan_steps(g):
                def times_b(k):
                    n, c = k // NC, k % NC
                    dve.wait_ge(bc_spread.sem, bc_spread.at(g, n + 1))
                    if k >= 3:
                        dve.wait_ge(scan_done.sem, scan_done.at(g, k - 2))
                    dve.tensor_tensor(bu[:, k % 3, :], du[:, c, :], ps[:, 2 + n % 2, :], ALU.mult).then_inc(bu_done.sem, 1)

                def scan(k):
                    dve.wait_ge(bu_done.sem, bu_done.at(g, k + 1))
                    dve.wait_ge(decay_ready.sem, decay_ready.at(g, k + 1))
                    if k >= 2:
                        dve.wait_ge(hc_done.sem, hc_done.at(g, k - 1))
                    dve.tensor_tensor_scan(state[:, k % 2, :], decay[:, k % 3, :], bu[:, k % 3, :], 0.0, ALU.mult, ALU.add).then_inc(scan_done.sem, 1)

                def times_c(k):
                    n = k // NC
                    dve.wait_ge(scan_done.sem, scan_done.at(g, k + 1))
                    if k >= 3:
                        dve.wait_ge(y_added.sem, y_added.at(g, k - 2))
                    dve.tensor_tensor(hc[:, k % 3, :], state[:, k % 2, :], ps[:, 4 + n % 2, :], ALU.mult).then_inc(hc_done.sem, 1)

                for k in range(NC * N + 2):
                    if k < NC * N:
                        times_b(k)
                    if 1 <= k <= NC * N:
                        scan(k - 1)
                    if k >= 2:
                        times_c(k - 2)

            def mamba(g):
                for c in range(NC):
                    dve.wait_ge(conv_mid.sem, conv_mid.at(g, c + 1))
                    u = u_conv[:, c, :].rearrange("p (b t) -> p b t", b=GB)
                    raw = ps[:, c, :].rearrange("p (b t) -> p b t", b=GB)
                    link(g, dve.scalar_tensor_tensor(u[:, :, 1:S], raw[:, :, 0:S - 1], w_conv[:, c, 0:1], u[:, :, 1:S], ALU.mult, ALU.add))
                    dve.scalar_tensor_tensor(u[:, :, 0:S - 1], raw[:, :, 1:S], w_conv[:, c, 2:3], u[:, :, 0:S - 1],
                                             ALU.mult, ALU.add).then_inc(conv_done.sem, 1)
                dve.wait_ge(xproj_done.sem, xproj_done.at(g, 3))
                link(g, dve.tensor_copy(bc_split[:], ps[0:96, 6, :]))
                link(g, dve.tensor_tensor(bc_res[0:96, :], ps[0:96, 6, :], bc_split[:], ALU.subtract))
                dve.tensor_copy(bc_split[32:64, :], bc_res[32:64, :])
                bf = bc_mid[64:96, 0:T // 2].bitcast(BF16)
                link(g, dve.tensor_copy(bf, bc_res[64:96, :]))
                dve.tensor_tensor(bc_split[64:96, :], bc_res[64:96, :], bf, ALU.subtract).then_inc(split_ready.sem, 1)
                dve.wait_ge(z_ready.sem, z_ready.at(g, 2))
                dve.scalar_tensor_tensor(dt_e, dt_z, -1.0, dt_z, ALU.mult, ALU.min).then_inc(nz_ready.sem, 1)
                dve.wait_ge(ln_ready.sem, ln_ready.at(g, 1))
                link(g, dve.scalar_tensor_tensor(delta, dt_z, 0.0, dt_e, ALU.max, ALU.add))
                link(g, dve.tensor_tensor(du, delta, u_act, ALU.mult))
                dve.memset(delta.rearrange("p c (b t) -> p (c b) t", t=S)[:, :, 0:1], FAR).then_inc(delta_ready.sem, 1)
                scan_steps(g)
                for c in range(NC):
                    dve.wait_ge(y_added.sem, y_added.at(g, NC * N - (NC - 1 - c)))
                    link(g, dve.scalar_tensor_tensor(u_conv[:, c, :], u_act[:, c, :], d_par[:, c:c + 1], ps[:, c, :], ALU.mult, ALU.add))
                    if c == 0:
                        dve.wait_ge(gate_ready.sem, gate_ready.at(g, 2))
                    dve.tensor_tensor(y_gated[:, c, :], u_conv[:, c, :], gate_act[:, c, :], ALU.mult).then_inc(yg_ready.sem, 1)
                dve.wait_ge(mamba_done.sem, mamba_done.at(g, 1))
                dve.tensor_tensor(x_res.rearrange("p t d -> p (t d)"), x_in.rearrange("p t d -> p (t d)"), ps[:, 6, :],
                                  ALU.add).then_inc(x_free.sem, 1)
                dve.wait_ge(x_free.sem, x_free.at(g, 1))

            def softmax_front(g, k, p):
                dve.wait_ge(s_done.sem, s_done.at(g, k * NP + p + 1))
                s_ps = ps[:, 2 * (p % 2):2 * (p % 2) + 2, :].rearrange("p k f -> p (k f)")
                if p == 3:
                    dve.wait_ge(pT_done.sem, pT_done.at(g, k * NP + 1))
                v = scores[:, p % 3, :]
                if k == 0:
                    bias = bias0[:, p * P:(p + 1) * P].unsqueeze(1).to_broadcast([P, HP, P])
                    ins = dve.tensor_tensor(v.rearrange("p (h j) -> p h j", h=HP), s_ps.rearrange("p (h j) -> p h j", h=HP), bias, ALU.add)
                else:
                    at = K_CAUSAL if k == 1 else K_CAUSAL9
                    bias = kc[:, at:at + S].unsqueeze(1).to_broadcast([P, 2 * HP, S])
                    ins = dve.scalar_tensor_tensor(v.rearrange("p (r j) -> p r j", j=S), s_ps.rearrange("p (r j) -> p r j", j=S),
                                                   HD ** -0.5, bias, ALU.mult, ALU.add)
                ins.then_inc(s_read.sem, 1)
                dve.wait_ge(s_read.sem, s_read.at(g, k * NP + p + 1))
                rows = v.rearrange("p (r j) -> p r j", j=S)
                link(g, dve.reduce_max(row_max[:, p % 3, :], rows, AX.X))
                dve.tensor_tensor(rows, rows, row_max[:, p % 3, :].unsqueeze(2).to_broadcast([P, 2 * HP, S]),
                                  ALU.subtract).then_inc(s_shifted.sem, 1)

            def softmax_sum(g, p):
                dve.wait_ge(exp_done.sem, exp_done.at(g, p + 1))
                link(g, dve.reduce_sum(row_sum[:, p % 3, :], scores[:, p % 3, :].rearrange("p (r j) -> p r j", j=S), AX.X))
                dve.reciprocal(row_sum[:, p % 3, :], row_sum[:, p % 3, :]).then_inc(sum_ready.sem, 1)

            def attention0(g):
                if True:
                    dve.wait_ge(mask_loaded.sem, mask_loaded.at(g, 16))
                    ins = dve.tensor_scalar(bias0[:], mask_in[:], -NEG, NEG, ALU.mult, ALU.add)
                    ins.then_inc(mask_free.sem, 1)
                    dve.wait_ge(mask_free.sem, mask_free.at(g, 1))
                    b3 = bias0.rearrange("p (b j) -> p b j", b=GB)
                    link(g, dve.tensor_tensor(b3, b3, kc[:, K_CAUSAL:K_CAUSAL9].unsqueeze(1).to_broadcast([P, GB, S]), ALU.min))
                dve.wait_ge(qd_zero.sem, qd_zero.at(g, 2))
                for h in range(HP):
                    dve.wait_ge(q0_done.sem, q0_done.at(g, h + 1))
                    dve.tensor_scalar(Qd[S:P, h, :, S:P], ps[S:P, h % 4, :].rearrange("p (b i) -> p b i", b=GB), 0.125, None,
                                      ALU.mult).then_inc(q0_bottom.sem, 1)
                for h in range(1, HP, 2):
                    dve.wait_ge(k0_done.sem, k0_done.at(g, h + 1))
                    dve.tensor_copy(KT[:, h, :], ps[:, 4 + h % 3, :]).then_inc(k0_odd.sem, 1)
                for t in range(NP):
                    dve.wait_ge(v0_done.sem, v0_done.at(g, t + 1))
                    q = 2 * (t % 2)
                    dve.tensor_copy(V0[:, t, :], ps[:, q:q + 2, :].rearrange("p k f -> p (k f)")).then_inc(v0_ready.sem, 1)
                for p in range(NP + 1):
                    if p < NP:
                        softmax_front(g, 0, p)
                    if p >= 1:
                        softmax_sum(g, p - 1)
                dve.wait_ge(attn_done.sem, attn_done.at(g, 1))
                dve.wait_ge(biased.sem, biased.at(g, 1))
                x_flat = x_res.rearrange("p t d -> p (t d)")
                link(g, dve.tensor_tensor(x_flat, x_flat, ps[:, 0, :], ALU.add))

            def attention1(g, k):
                if k == 1:
                    for c in range(2):
                        cos = kc[:, K_COS:K_SIN].unsqueeze(1).to_broadcast([P, GB, S])
                        sin = kc[:, K_SIN:K_HEAD].unsqueeze(1).to_broadcast([P, GB, S])
                        for swapped, table, b, dst in ((0, cos, b_qk1, rot_a), (1, sin, b_sw1, rot_b)):
                            dve.wait_ge(qk1_done.sem, qk1_done.at(g, 2 * c + swapped + 1))
                            ins = dve.scalar_tensor_tensor(dst[:, c, :].rearrange("p (b i) -> p b i", b=GB),
                                                           ps[:, 2 * c + swapped, :].rearrange("p (b i) -> p b i", b=GB),
                                                           b[:, c:c + 1], table, ALU.add, ALU.mult)
                        link(g, ins)
                        dst, ready = (q1, q1_ready) if c == 0 else (kT1[:], k1_ready)
                        dve.tensor_tensor(dst, rot_a[:, c, :], rot_b[:, c, :], ALU.add).then_inc(ready.sem, 1)
                dve.wait_ge(v1_done.sem, v1_done.at(g, k))
                dve.tensor_tensor(V1[:, :, :, 0:16], ps[:, 4, :].rearrange("p (t h d) -> p t h d", t=NP, h=HP),
                                  (bv1 if k == 1 else bvx).rearrange("p (h d) -> p h d", h=HP).unsqueeze(1).to_broadcast([P, NP, HP, 16]),
                                  ALU.add).then_inc(v1_ready.sem, 1)
                dve.wait_ge(q1_ready.sem, q1_ready.at(g, k))
                for h in range(HEADS - 6):
                    ins = dve.tensor_scalar(Qd[:, h // 2, :, (h % 2) * S:(h % 2 + 1) * S], q1.rearrange("p (b i) -> p b i", b=GB),
                                            kc[:, K_HEAD + h:K_HEAD + h + 1], None, ALU.mult)
                ins.then_inc(qm_dve.sem, 1)
                for p in range(NP + 1):
                    if p < NP:
                        softmax_front(g, k, p)
                    if p >= 1:
                        q = p - 1
                        dve.wait_ge(o_done.sem, o_done.at(g, k * NP + q + 1))
                        o_ps = ps[:, 6:8, 0:HP * 18].rearrange("p s (h f) -> p s h f", h=HP)
                        link(g, dve.reciprocal(row_sum[:, q % 3, :].rearrange("p (s h) -> p s h", s=2), o_ps[:, :, :, 16]))
                        for e in range(2):
                            r = slice(e * S, (e + 1) * S)
                            inv = row_sum[r, q % 3, :].rearrange("p (s h) -> p s h", s=2).unsqueeze(3).to_broadcast([S, 2, HP, HD])
                            ins = dve.tensor_tensor(O1[r, q % 2], o_ps[r, :, :, e * HD:(e + 1) * HD], inv, ALU.mult)
                        ins.then_inc(o1_ready.sem, 1)
                dve.wait_ge(attn_done.sem, attn_done.at(g, 1 + k))
                dve.wait_ge(biased.sem, biased.at(g, 1 + k))
                for s2 in range(2):
                    r = slice(s2 * S, (s2 + 1) * S)
                    x_half = x_res[r].rearrange("p t d -> p (t d)")
                    ins = dve.tensor_tensor(x_half, x_half, ps[r, s2, :], ALU.add)
                link(g, ins)

            def routing(g, m):
                dve.wait_ge(route_done.sem, route_done.at(g, m + 1))
                ps_l = ps[:, 7, 0:NP * E].rearrange("p (t e) -> p t e", t=NP)
                if m == 0:
                    link_alone(g, dve.tensor_copy(logits[:], ps_l))
                else:
                    link_alone(g, dve.tensor_tensor(logits[:], ps_l, br1[:].unsqueeze(1).to_broadcast([P, NP, E]), ALU.add))
                for t in range(NP):
                    ins = dve.max(top[:, t, :], logits[:, t, :])
                link_alone(g, ins)
                for t in range(NP):
                    ins = dve.max_index(top_at[:, t, :], top[:, t, :], logits[:, t, :])
                dve.tensor_tensor(top_e[:], top[:, :, 1], top[:, :, 0], ALU.subtract).then_inc(top_ready.sem, 1)
                dve.wait_ge(top_ready.sem, top_ready.at(g, m + 1))
                link(g, dve.tensor_copy(top_atf[:], top_at[:, :, 0:2]))
                iota = kc[:, K_IOTA:K_HALF].unsqueeze(1).to_broadcast([P, NP, E])
                for r in range(2):
                    dve.tensor_tensor(pick[:, :, r, :], iota, top_atf[:, :, r:r + 1].to_broadcast([P, NP, E]), ALU.is_equal)
                dve.wait_ge(tope_ready.sem, tope_ready.at(g, m + 1))
                link(g, dve.tensor_scalar(top_w[:, :, 1], top_e[:], 1.0, None, ALU.add))
                link(g, dve.reciprocal(top_w[:, :, 0], top_w[:, :, 1]))
                link(g, dve.tensor_tensor(top_w[:, :, 1], top_w[:, :, 0], top_e[:], ALU.mult))
                link(g, dve.tensor_tensor(pick[:], pick[:], top_w[:].unsqueeze(3).to_broadcast([P, NP, 2, E]), ALU.mult))
                dve.tensor_tensor(gate[:, :, 0:E], pick[:, :, 0, :], pick[:, :, 1, :], ALU.add).then_inc(gate_w.sem, 1)
                dve.wait_ge(gate_w.sem, gate_w.at(g, m + 1))

            def accumulate(g, m, e):
                dve.wait_ge(down_done.sem, down_done.at(g, m * E + e + 1))
                if e >= 1:
                    dve.wait_ge(acc_done.sem, acc_done.at(g, m * E + e))
                dst = x_res
                if m == 1 and e == E - 1:
                    dve.wait_ge(out_free.sem, out_free.at(g, 1))
                    dst = x_out
                for t in range(NP):
                    ins = dve.scalar_tensor_tensor(dst[:, t, :], ps[:, 6 + e % 2, t * P:(t + 1) * P], gate[:, t, e:e + 1],
                                                   x_res[:, t, :], ALU.mult, ALU.add)
                ins.then_inc(acc_done.sem, 1)

            def experts0(g):
                for e in range(E + 1):
                    for c in range(C0 if e < E else 0):
                        k = e * C0 + c
                        dve.wait_ge(silu_done.sem, silu_done.at(g, k + 1))
                        if e >= 2 and c == 0:
                            dve.wait_ge(down_done.sem, down_done.at(g, e - 1))
                        dve.tensor_tensor(hidden[:, e % 2, c, :], silu_g[:, k % 2, :], ps[:, 2 * (k % 3) + 1, :],
                                          ALU.mult).then_inc(h0_done.sem, 1)
                    if e >= 1:
                        accumulate(g, 0, e - 1)
                dve.wait_ge(acc_done.sem, acc_done.at(g, E))

            def experts1(g):
                for e in range(E + 1):
                    for c in range(1, C1 if e < E else 0, 2):
                        k = e * C1 + c
                        dve.wait_ge(up_done.sem, up_done.at(g, k + 1))
                        if e >= 2 and c == 1:
                            dve.wait_ge(down_done.sem, down_done.at(g, E + e - 1))
                        dve.tensor_scalar(hidden[:, e % 2, c, :], ps[:, k % 6, :], b_1[:, e, c:c + 1], 0.0, ALU.add,
                                          ALU.max).then_inc(h1_dve.sem, 1)
                    if e == 0:
                        dve.wait_ge(b2_done.sem, b2_done.at(g, 1))
                        x_flat = x_res.rearrange("p t d -> p (t d)")
                        link(g, dve.tensor_tensor(x_flat, x_flat, ps[:, 7, :], ALU.add))
                    if e >= 1:
                        accumulate(g, 1, e - 1)

            dve.wait_ge(weights["mamba"].sem, need["mamba"])
            dve.wait_ge(a_exp.sem, 1)
            dve.tensor_scalar(a_neg[:], a_neg[:], -1.0, None, ALU.mult)
            dve.tensor_copy(sel[:], kc[0:96, K_SEL:K_IOTA])
            dve.wait_ge(weights["attn1"].sem, need["attn1"])
            wq = w_qkv1[:, 0:2 * D].rearrange("p (k two) -> p k two", two=2)
            sw = w_sw1[:].rearrange("p (k two) -> p k two", two=2)
            for odd in range(2):
                ins = dve.tensor_copy(sw[:, :, odd], wq[:, :, 1 - odd])
            ins.then_inc(setup.sem, 1)
            dve.wait_ge(setup.sem, 1)
            with dve.Fori(0, NG) as g:
                norm(g, 0)
                mamba(g)
                norm(g, 1)
                attention0(g)
                norm(g, 2)
                routing(g, 0)
                experts0(g)
                norm(g, 3)
                attention1(g, 1)
                norm(g, 4)
                attention1(g, 2)
                norm(g, 5)
                routing(g, 1)
                experts1(g)
            assert links[0] == DVE_LINKS, links[0]


def pairs_of(x, g):
    return x.rearrange("(b s) i d -> (s i) b d", s=2)[:, bass.ds(g * NP, NP), :]


NAMES = """x ctx_1024 mask_BxS2_bk0 L0_attn_in_proj_w L0_attn_conv_w L0_attn_conv_b L0_attn_x_proj_w L0_attn_dt_proj_w
L0_attn_dt_proj_b L0_attn_out_proj_w L0_attn_A_log L0_attn_D_param L0_xattn_Wq L0_xattn_Wkv L0_xattn_Wo L0_xattn_bo
L0_ffn_gate_w L0_ffn_gate_up_w L0_ffn_down_w L1_attn_Wqkv L1_attn_bqkv L1_attn_Wproj L1_attn_bproj L1_xattn_Wq L1_xattn_bq
L1_xattn_Wk L1_xattn_bk L1_xattn_Wv L1_xattn_bv L1_xattn_Wo L1_xattn_bo L1_ffn_Wr L1_ffn_br L1_ffn_W1 L1_ffn_b1
L1_ffn_W2 L1_ffn_b2""".split()


def kernel(**inputs):
    import concourse.bacc as bacc
    from concourse.bass_utils import run_bass_kernel_spmd

    nc = bacc.Bacc("TRN2", target_bir_lowering=False, num_devices=1)
    arrays, aps = {}, {}
    for name in NAMES + ["shape_constants"]:
        v = shape_constants() if name == "shape_constants" else np.ascontiguousarray(inputs[name])
        arrays[f"in_{name}"] = v
        aps[name] = nc.dram_tensor(f"in_{name}", v.shape, mybir.dt.from_np(v.dtype), kind="ExternalInput").ap()
    out = nc.dram_tensor("out_x", (BATCH, S, D), F32, kind="ExternalOutput").ap()
    build(nc, aps, out)
    result = run_bass_kernel_spmd(nc, [arrays], core_ids=[0])
    return result.results[0]["out_x"]
```

```python
from contextlib import ExitStack

import numpy as np

import concourse.bass as bass
from concourse import mybir

F32 = mybir.dt.float32
BF16 = mybir.dt.bfloat16
U8 = mybir.dt.uint8
U32 = mybir.dt.uint32
ALU = mybir.AluOpType
ACT = mybir.ActivationFunctionType
AX = mybir.AxisListType

P = 128
BATCH, S, D = 32, 64, 128
GB = 8
NG = BATCH // GB
T = GB * S
NP = T // P
TH = T // 2
GH, NH = GB // 2, NP // 2
HEADS = 16
HP = HEADS // 2
DI = 2 * D
NC = DI // P
N = 16
E = 8
F0 = 256
F1 = 512
C0, C1 = F0 // P, F1 // P
HD = D // HEADS
LN_EPS = 1e-5
NEG = -float(np.finfo(np.float32).max)
FAR = 1e28

K_IDENT = 0
K_CAUSAL = K_IDENT + P
K_CAUSAL9 = K_CAUSAL + S
K_COS = K_CAUSAL9 + S
K_SIN = K_COS + S
K_HEAD = K_SIN + S
K_SEL = K_HEAD + HEADS
K_IOTA = K_SEL + 2 * N
K_HALF = K_IOTA + E
K_ALL = K_HALF + NP


def shape_constants():
    k = np.zeros((P, K_ALL), np.float32)
    k[:, K_IDENT:K_CAUSAL] = np.eye(P)
    i = (np.arange(P) % S)[:, None]
    j = np.arange(S)[None, :]
    k[:, K_CAUSAL:K_CAUSAL9] = np.where(j > i, np.float32(NEG), np.float32(0))
    k[:, K_CAUSAL9:K_COS] = np.where(j > i, np.float32(-1e9), np.float32(0))
    inv = (np.float32(1) / np.float32(10000) ** (np.arange(0, HD, 2, dtype=np.float32) / np.float32(HD)))
    freq = (np.arange(S, dtype=np.float32)[:, None] * inv[None, :]).astype(np.float32)
    d = np.arange(P) % HD
    k[:, K_COS:K_SIN] = np.cos(freq)[:, d // 2].T
    k[:, K_SIN:K_HEAD] = np.sin(freq)[:, d // 2].T * np.where(d % 2 == 0, -1, 1)[:, None]
    k[:, K_HEAD:K_SEL] = np.arange(P)[:, None] // HD == np.arange(HEADS)[None, :]
    k[:, K_SEL:K_IOTA] = np.arange(P)[:, None] % (2 * N) == np.arange(2 * N)[None, :]
    k[:, K_IOTA:K_HALF] = np.arange(E)
    k[:, K_HALF:] = -0.5
    return k


class Signal:

    def __init__(self, sem, per_group):
        self.sem, self.per_group = sem, per_group

    def at(self, g, k):
        return g * self.per_group + k


def wait_alone(eng, ready, sem, value):
    value = eng.to_reg(value)
    eng.wait_ge(ready.sem, 1)
    eng.wait_ge(sem, value)


MAMBA_LINKS = 11
LAYER_LINKS = 44


def build(nc, a, out):
    with ExitStack() as ctx:
        def sb(name, shape, dt=F32):
            return ctx.enter_context(nc.sbuf_tensor(name, shape, dt))

        def signal(name, per_group=1):
            return Signal(ctx.enter_context(nc.semaphore(name)), per_group)

        ctx.enter_context(nc.allow_non_contiguous_dma(reason="per-feature vectors"))

        kc = sb("kc", [P, K_ALL])
        ident = kc[:, K_IDENT:K_CAUSAL]
        w_in = sb("w_in", [P, 2 * DI])
        w_conv = sb("w_conv", [P, NC, 3])
        b_conv = sb("b_conv", [P, NC])
        w_xd = sb("w_xd", [P, NC, DI])
        w_xbc = sb("w_xbc", [P, NC, 3, 2 * N])
        w_dt = sb("w_dt", [P, NC, DI])
        b_dt = sb("b_dt", [P, NC])
        w_out = sb("w_out", [P, NC, D])
        a_neg = sb("a_neg", [P, NC, N])
        d_par = sb("d_par", [P, NC])
        sel = sb("sel", [96, 2 * N], BF16)
        w_q0 = sb("w_q0", [P, HP * P])
        w_kv0 = sb("w_kv0", [P, 2 * HP * P])
        w_o0 = sb("w_o0", [P, HP, D])
        bo0 = sb("bo0", [P, D])
        w_r0 = sb("w_r0", [P, E])
        w_gu = sb("w_gu", [P, E, 2 * F0])
        w_dn = sb("w_dn", [P, E, C0, D])
        w_qkv1 = sb("w_qkv1", [P, 3 * D])
        w_sw1 = sb("w_sw1", [P, 2 * D])
        b_qk1 = sb("b_qk1", [P, 2])
        b_sw1 = sb("b_sw1", [P, 2])
        bv1 = sb("bv1", [P, D])
        w_p1 = sb("w_p1", [P, 2, D])
        bo1 = sb("bo1", [P, D])
        w_qkvx = sb("w_qkvx", [P, 3 * D])
        b_qkx = sb("b_qkx", [P, 2])
        bvx = sb("bvx", [P, D])
        w_px = sb("w_px", [P, 2, D])
        box = sb("box", [P, D])
        w_r1 = sb("w_r1", [P, E])
        br1 = sb("br1", [P, E])
        w_1 = sb("w_1", [P, E, F1])
        b_1 = sb("b_1", [P, E, C1])
        w_2 = sb("w_2", [P, E, C1, D])
        b_2 = sb("b_2", [P, NP, D])

        x_in = sb("x_in", [P, NP, D])
        x_keep = sb("x_keep", [P, NP, D])
        x_mix = sb("x_mix", [P, NP, D])
        x_res = sb("x_res", [P, NP, D])
        ctx_in = sb("ctx_in", [P, NP, D])
        mask_in = sb("mask_in", [P, T], U8)
        stats = [sb(f"stats{i}", [P, NP, 6]) for i in range(2)]
        mean_var = [sb(f"mean_var{i}", [P, NP, 2]) for i in range(2)]
        var_eps = [sb(f"var_eps{i}", [P, NP]) for i in range(2)]
        rstd = [sb(f"rstd{i}", [P, NP]) for i in range(2)]
        xn = [sb(f"xn{i}", [P, NP, D]) for i in range(2)]
        xT0, xT = sb("xT0", [P, T]), sb("xT", [P, T])
        ctxT = sb("ctxT", [P, T])
        bias0 = sb("bias0", [P, T])
        V1 = sb("V1", [P, NP, HP, 2, 18])
        scores = sb("scores", [P, 3, 2 * T])
        row_max = sb("row_max", [P, 3, HP * 2])
        row_sum = sb("row_sum", [P, 3, HP * 2])
        probsT = sb("probsT", [P, 2, HP, P])
        O1 = sb("O1", [P, 2, 2, HP, HD])
        O1T = sb("O1T", [P, NP, 2, S])
        logits = sb("logits", [P, NP, E])
        top = sb("top", [P, NP, 8])
        top_at = sb("top_at", [P, NP, 8], U32)
        top_atf = sb("top_atf", [P, NP, 2])
        top_e = sb("top_e", [P, NP])
        top_w = sb("top_w", [P, NP, 2])
        pick = sb("pick", [P, NP, 2, E])
        gate = sb("gate", [P, NP, 32])
        gateT = sb("gateT", [P, P])
        gate_act, delta, du, y_sum = (sb(n, [P, NC, T]) for n in ("gate_act", "delta", "du", "y_sum"))
        bc_split = sb("bc_split", [96, T], BF16)

        region = sb("region", [P, 22 * T])

        def view(at, size, pattern, **kw):
            return region[:, at * T:(at + size) * T].rearrange(pattern, **kw)

        Qd = view(0, 8, "p (h b q) -> p h b q", h=HP, b=GH)
        KT = view(8, 8, "p (x h t) -> p x h t", x=2, h=HP)
        V0 = view(16, 4, "p (t f) -> p t f", t=NH)
        Qx = [Qd, view(8, 8, "p (h b q) -> p h b q", h=HP, b=GH)]
        q1, kT1 = region[:, 16 * T:17 * T], region[:, 17 * T:18 * T]
        u_act = view(20, 2, "p (c t) -> p c t", c=NC)
        hidden = view(8, 8, "p (s c t) -> p s c t", s=2, c=4)
        gated, up_copy = hidden[:, :, 2, :], hidden[:, :, 3, :]
        decay = view(16, 3, "p (r t) -> p r t", r=3)
        state = view(19, 3, "p (r t) -> p r t", r=3)
        u_conv = scores[:, 0].rearrange("p (c t) -> p c t", c=NC)
        bc_res, bc_mid = scores[0:96, 0, 0:T], scores[0:96, 0, T:T + T // 2].bitcast(BF16)
        d_raw = scores[:, 2].rearrange("p (c t) -> p c t", c=NC)
        dt_z = probsT[:, 0].rearrange("p h q -> p (h q)").rearrange("p (c t) -> p c t", c=NC)
        dt_e = probsT[:, 1].rearrange("p h q -> p (h q)").rearrange("p (c t) -> p c t", c=NC)

        ps = ctx.enter_context(nc.psum_tensor("ps", [P, 8, 512], F32))

        weights = {n: signal(f"w_{n}_loaded") for n in ("mamba", "attn0", "moe0", "attn1", "attnx", "moe1")}
        need = {}
        x_loaded, ctx_loaded, mask_loaded = signal("x_loaded", 16), signal("ctx_loaded", 16), signal("mask_loaded", 16)
        x_stored = signal("x_stored", 16)
        mask_free, out_free = signal("mask_free"), signal("out_free")
        setup, a_exp, zeros_set, swapped_set = signal("setup"), signal("a_exp"), signal("zeros_set"), signal("swapped_set")
        var_ready, rstd_ready, xn_ready, xnT_done, xT_ready = (
            [signal(f"{n}{i}", (1, 5)[i]) for i in range(2)] for n in ("var_ready", "rstd_ready", "xn_ready", "xnT_done", "xT_ready"))
        ctxT_done, ctxT_ready = signal("ctxT_done"), signal("ctxT_ready")
        biased = signal("biased", 3)
        x_kept, x_mixed = signal("x_kept"), signal("x_mixed")
        inproj_done, conv_mid, conv_done, u_ready = signal("inproj_done", 4), signal("conv_mid", 2), signal("conv_done", 2), signal("u_ready", 2)
        gate_ready = signal("gate_ready", 2)
        xproj_done, draw_ready, split_ready = signal("xproj_done", 3), signal("draw_ready", 2), signal("split_ready")
        dt_done, z_ready, nz_ready, e_ready = signal("dt_done", 2), signal("z_ready", 2), signal("nz_ready"), signal("e_ready")
        ln_ready, delta_ready = signal("ln_ready"), signal("delta_ready")
        bc_spread, decay_ready = signal("bc_spread", N), signal("decay_ready", NC * N)
        bu_done, scan_done, hc_done, y_added = (signal(n, NC * N) for n in ("bu_done", "scan_done", "hc_done", "y_added"))
        yg_ready, mamba_done = signal("yg_ready"), signal("mamba_done")
        q0_done, q0_top, q0_bottom, k0_done, k0_ready = (signal(n, HP) for n in ("q0_done", "q0_top", "q0_bottom", "k0_done", "k0_ready"))
        v0_done, v0_ready, qd_zero = signal("v0_done", NP), signal("v0_ready", NP), signal("qd_zero", 2)
        s_done, s_read, exp_done, pT_done, pT_ready, o_done = (
            signal(n, 3 * NP) for n in ("s_done", "s_read", "exp_done", "pT_done", "pT_ready", "o_done"))
        shifted0, sum_ready, normed, o0_ready = (signal(n, NP) for n in ("shifted0", "sum_ready", "normed", "o0_ready"))
        max_ready, shifted1, o1_ready, o1T_done = (
            signal(n, 2 * NP) for n in ("max_ready", "shifted1", "o1_ready", "o1T_done"))
        o1T_ready = signal("o1T_ready", 2)
        attn_done = signal("attn_done", 3)
        qk1_done, v1_done = signal("qk1_done", 6), signal("v1_done", 2)
        q1_rot, q1_lin, k1_rot, k1_lin = signal("q1_rot"), signal("q1_lin"), signal("k1_rot"), signal("k1_lin")
        v1_ready, qm_dve, qm_act = signal("v1_ready", 2), signal("qm_dve", 4), signal("qm_act", 4)
        route_done, top_ready, tope_ready, gate_w = signal("route_done", 2), signal("top_ready", 2), signal("tope_ready", 2), signal("gate_w", 2)
        gu_done, tanh_done, up_copied, gated_done, h0_done = (
            signal(n, C0 * E) for n in ("gu_done", "tanh_done", "up_copied", "gated_done", "h0_done"))
        up_done, h1_act, h1_dve = signal("up_done", C1 * E), signal("h1_act", C1 * E // 2), signal("h1_dve", C1 * E // 2)
        down_done, acc_done = signal("down_done", 2 * E), signal("acc_done", 2 * E)
        gateT_done, gateT_ready, b2_done, b2_added = (signal(n) for n in ("gateT_done", "gateT_ready", "b2_done", "b2_added"))
        mamba_chain, layer_chain = signal("mamba_chain", MAMBA_LINKS), signal("layer_chain", LAYER_LINKS)

        block = ctx.enter_context(nc.Block())

        @block.sync
        def _(sp):
            def load(group, dst, src):
                sp.dma_start(dst, src).then_inc(weights[group].sem, 16)
                need[group] = need.get(group, 0) + 16

            def column(name, n):
                return a[name].rearrange("(c p) -> p c", p=n)

            def row(name):
                return a[name].partition_broadcast(P)

            def load_x(g):
                sp.dma_start(x_in[:], pairs_of(a["x"], g)).then_inc(x_loaded.sem, 16)

            def load_ctx(g):
                sp.dma_start(ctx_in[:], pairs_of(a["ctx_1024"], g)).then_inc(ctx_loaded.sem, 16)

            def load_mask(g):
                src = a["mask_BxS2_bk0"].rearrange("b s -> (b s)")[bass.ds(g * T, T)]
                sp.dma_start(mask_in[:], src.partition_broadcast(P)).then_inc(mask_loaded.sem, 16)

            def store_x(g):
                sp.wait_ge(acc_done.sem, acc_done.at(g, 2 * E))
                sp.dma_start(pairs_of(out, g), x_res[:]).then_inc(x_stored.sem, 16)
                sp.wait_ge(x_stored.sem, x_stored.at(g, 16))
                sp.nop().then_inc(out_free.sem, 1)

            sp.nop().then_inc(out_free.sem, 1)
            load_x(0)
            load("mamba", kc[:], a["shape_constants"])
            load("mamba", w_in[:], a["L0_attn_in_proj_w"])
            load("mamba", w_conv[:], a["L0_attn_conv_w"].rearrange("(c p) a k -> p c (a k)", p=P))
            load("mamba", b_conv[:], column("L0_attn_conv_b", P))
            xp = a["L0_attn_x_proj_w"].rearrange("(c p) n -> p c n", p=P)
            load("mamba", w_xd[:], xp[:, :, 0:DI])
            for k in range(3):
                load("mamba", w_xbc[:, :, k, :], xp[:, :, DI:])
            load("mamba", w_dt[:], a["L0_attn_dt_proj_w"].rearrange("(c p) n -> p c n", p=P))
            load("mamba", b_dt[:], column("L0_attn_dt_proj_b", P))
            load("mamba", a_neg[:], a["L0_attn_A_log"].rearrange("(c p) n -> p c n", p=P))
            load("mamba", d_par[:], column("L0_attn_D_param", P))
            load("mamba", w_out[:], a["L0_attn_out_proj_w"].rearrange("(c p) n -> p c n", p=P))
            load_ctx(0)
            load_mask(0)
            load("attn0", w_q0[:], a["L0_xattn_Wq"])
            load("attn0", w_kv0[:], a["L0_xattn_Wkv"])
            load("attn0", w_o0[:], a["L0_xattn_Wo"].rearrange("(c p) n -> p c n", p=P))
            load("attn0", bo0[:], row("L0_xattn_bo"))
            load("moe0", w_r0[:], a["L0_ffn_gate_w"])
            load("moe0", w_gu[:], a["L0_ffn_gate_up_w"].rearrange("e p f -> p e f"))
            load("moe0", w_dn[:], a["L0_ffn_down_w"].rearrange("e (c p) n -> p e c n", p=P))
            load("attn1", w_qkv1[:], a["L1_attn_Wqkv"])
            bqkv = a["L1_attn_bqkv"]
            load("attn1", b_qk1[:], bqkv[0:2 * D].rearrange("(c p) -> p c", p=P))
            load("attn1", bv1[:], bqkv[2 * D:3 * D].partition_broadcast(P))
            for odd in range(2):
                src = bqkv[0:2 * D].rearrange("(c k two) -> two k c", c=2, two=2)[1 - odd]
                load("attn1", b_sw1[odd:P:2, :], src)
            for name, dst, group in (("L1_attn_Wproj", w_p1, "attn1"), ("L1_xattn_Wo", w_px, "attnx")):
                src = a[name].rearrange("(hp e d) n -> hp d e n", e=2, d=HD)
                for copy in range(2):
                    for hp in range(HP):
                        at = copy * S + hp * HD
                        load(group, dst[at:at + HD, :, :], src[hp])
            load("attn1", bo1[:], row("L1_attn_bproj"))
            for i, n in enumerate("qkv"):
                load("attnx", w_qkvx[:, i * D:(i + 1) * D], a[f"L1_xattn_W{n}"])
            load("attnx", b_qkx[:, 0:1], column("L1_xattn_bq", P))
            load("attnx", b_qkx[:, 1:2], column("L1_xattn_bk", P))
            load("attnx", bvx[:], row("L1_xattn_bv"))
            load("attnx", box[:], row("L1_xattn_bo"))
            load("moe1", w_r1[:], a["L1_ffn_Wr"])
            load("moe1", br1[:], row("L1_ffn_br"))
            load("moe1", w_1[:], a["L1_ffn_W1"].rearrange("e p f -> p e f"))
            load("moe1", b_1[:], a["L1_ffn_b1"].rearrange("e (c p) -> p e c", p=P))
            load("moe1", w_2[:], a["L1_ffn_W2"].rearrange("e (c p) n -> p e c n", p=P))
            sp.wait_ge(zeros_set.sem, 1)
            for t in range(NP):
                load("moe1", b_2[32 * t:32 * t + E, t, :], a["L1_ffn_b2"])
            with sp.Fori(0, NG - 1) as g:
                sp.wait_ge(x_kept.sem, x_kept.at(g, 1))
                sp.wait_ge(xn_ready[0].sem, xn_ready[0].at(g, 1))
                load_x(g + 1)
                sp.wait_ge(ctxT_done.sem, ctxT_done.at(g, 1))
                load_ctx(g + 1)
                wait_alone(sp, zeros_set, mask_free.sem, mask_free.at(g, 1))
                load_mask(g + 1)
                store_x(g)
            store_x(NG - 1)


        @block.tensor
        def _(pe):
            def mm(out_ap, lhsT, rhs, start=True, stop=True):
                return pe.matmul(out_ap, lhsT, rhs, start=start, stop=stop)

            def turn_norm(g, l):
                i, bank = min(l, 1), 6 if l == 1 else 4
                pe.wait_ge(xn_ready[i].sem, xn_ready[i].at(g, max(l, 1)))
                for t in range(NP):
                    ins = pe.transpose(ps[:, bank, t * P:(t + 1) * P], xn[i][:, t, :], ident)
                ins.then_inc(xnT_done[i].sem, 1)

            def in_proj(g):
                pe.wait_ge(xT_ready[0].sem, xT_ready[0].at(g, 1))
                for m in range(2 * NC):
                    mm(ps[:, 4 + m, :], w_in[:, m * P:(m + 1) * P], xT0[:]).then_inc(inproj_done.sem, 1)

            def x_proj(g):
                pe.wait_ge(u_ready.sem, u_ready.at(g, 2))
                for m in range(NC):
                    for c in range(NC):
                        ins = mm(ps[:, 4 + m, :], w_xd[:, c, m * P:(m + 1) * P], u_act[:, c, :], c == 0, c == NC - 1)
                    ins.then_inc(xproj_done.sem, 1)
                for c in range(NC):
                    ins = mm(ps[0:96, 6, :], w_xbc[:, c, :, :], u_act[:, c, :], c == 0, c == NC - 1)
                ins.then_inc(xproj_done.sem, 1)

            def dt_proj(g):
                pe.wait_ge(draw_ready.sem, draw_ready.at(g, 2))
                for m in range(NC):
                    for c in range(NC):
                        ins = mm(ps[:, 4 + m, :], w_dt[:, c, m * P:(m + 1) * P], d_raw[:, c, :], c == 0, c == NC - 1)
                    ins.then_inc(dt_done.sem, 1)

            def spread_bc(g, n, ring):
                if n >= ring:
                    pe.wait_ge(hc_done.sem, hc_done.at(g, NC * (n - ring + 1)))
                b_bank, c_bank = bc_banks(n, ring)
                mm(ps[:, b_bank, :], sel[:, n:n + 1].to_broadcast([96, P]), bc_split[:])
                mm(ps[:, c_bank, :], sel[:, N + n:N + n + 1].to_broadcast([96, P]), bc_split[:]).then_inc(bc_spread.sem, 1)

            def mamba_out(g):
                pe.wait_ge(yg_ready.sem, yg_ready.at(g, 1))
                for t in range(NP):
                    for c in range(NC):
                        ins = mm(ps[:, 6, t * P:(t + 1) * P], y_sum[:, c, t * P:(t + 1) * P], w_out[:, c, :], c == 0, c == NC - 1)
                ins.then_inc(mamba_done.sem, 1)

            def turn_ctx(g):
                pe.wait_ge(ctx_loaded.sem, ctx_loaded.at(g, 16))
                for t in range(NP):
                    ins = pe.transpose(ps[:, 7, t * P:(t + 1) * P], ctx_in[:, t, :], ident)
                ins.then_inc(ctxT_done.sem, 1)

            def keys0(g, x, units):
                for u in units:
                    if x == 0 and u == 0:
                        pe.wait_ge(ctxT_ready.sem, ctxT_ready.at(g, 1))
                    if x == 1:
                        pe.wait_ge(q0_top.sem, q0_top.at(g, 4 + u + 1))
                        pe.wait_ge(q0_bottom.sem, q0_bottom.at(g, 4 + u + 1))
                    for h in range(2):
                        hp = 2 * u + h
                        ins = mm(ps[:, u, h * TH:(h + 1) * TH], w_kv0[:, hp * P:(hp + 1) * P], ctxT[:, x * TH:(x + 1) * TH])
                    ins.then_inc(k0_done.sem, 1)

            def queries0(g, x):
                if x == 0:
                    pe.wait_ge(xT_ready[1].sem, xT_ready[1].at(g, 1))
                for u in range(4):
                    if x == 0:
                        pe.wait_ge(k0_ready.sem, k0_ready.at(g, u + 1))
                    elif u % 2 == 0:
                        pe.wait_ge(s_read.sem, s_read.at(g, u // 2 + 1))
                    for h in range(2):
                        hp = 2 * u + h
                        ins = mm(ps[:, u, h * TH:(h + 1) * TH], w_q0[:, hp * P:(hp + 1) * P], xT[:, x * TH:(x + 1) * TH])
                    ins.then_inc(q0_done.sem, 1)

            def values0(g, p):
                q = 2 * (p % 2)
                if p < 2:
                    pe.wait_ge(q0_top.sem, q0_top.at(g, q + 2))
                    pe.wait_ge(q0_bottom.sem, q0_bottom.at(g, q + 2))
                else:
                    pe.wait_ge(k0_ready.sem, k0_ready.at(g, 4 + q + 2))
                for half in range(2):
                    cols = w_kv0[:, HP * P + half * 512:HP * P + (half + 1) * 512]
                    ins = mm(ps[:, q + half, :], ctxT[:, p * P:(p + 1) * P], cols)
                ins.then_inc(v0_done.sem, 1)

            def scores_of(g, k, p):
                if k == 0:
                    pe.wait_ge(v0_ready.sem, v0_ready.at(g, p + 1))
                    pe.wait_ge(q0_top.sem, q0_top.at(g, 4 * (p // 2 + 1)))
                    pe.wait_ge(q0_bottom.sem, q0_bottom.at(g, 4 * (p // 2 + 1)))
                    pe.wait_ge(k0_ready.sem, k0_ready.at(g, 4 * (p // 2 + 1)))
                else:
                    if p % 2 == 0:
                        pe.wait_ge(qm_dve.sem, qm_dve.at(g, 2 * (k - 1) + p // 2 + 1))
                        pe.wait_ge(qm_act.sem, qm_act.at(g, 2 * (k - 1) + p // 2 + 1))
                    if p == 0:
                        k1_ready = k1_rot if k == 1 else k1_lin
                        pe.wait_ge(k1_ready.sem, k1_ready.at(g, 1))
                        pe.wait_ge(v1_ready.sem, v1_ready.at(g, k))
                    if p >= 2:
                        pe.wait_ge(s_read.sem, s_read.at(g, k * NP + p - 1))
                s_ps = ps[:, 2 * (p % 2):2 * (p % 2) + 2, :].rearrange("p k f -> p (k f)")
                for h in range(HP):
                    for s2 in range(2):
                        b = 2 * (p % 2) + s2
                        keys = KT[:, p // 2, h, b * S:(b + 1) * S] if k == 0 else kT1[:, (2 * p + s2) * S:(2 * p + s2 + 1) * S]
                        at = (2 * h + s2) * S
                        ins = mm(s_ps[:, at:at + S], (Qd if k == 0 else Qx[p // 2])[:, h, b, :], keys)
                ins.then_inc(s_done.sem, 1)

            def turn_probs(g, k, p):
                if k == 0:
                    pe.wait_ge(normed.sem, normed.at(g, p + 1))
                else:
                    pe.wait_ge(exp_done.sem, exp_done.at(g, k * NP + p + 1))
                bank = probs_bank(k, p)
                if p >= 1 and bank == 4:
                    pe.wait_ge(pT_ready.sem, pT_ready.at(g, k * NP + p))
                for h in range(HP):
                    at = h * P
                    ins = pe.transpose(ps[:, bank + h // 4, (h % 4) * P:(h % 4 + 1) * P], scores[:, p % 3, at:at + P], ident)
                ins.then_inc(pT_done.sem, 1)

            def weigh_values0(g, p):
                if p >= 1:
                    wait_alone(pe, weights["attn0"], o0_ready.sem, o0_ready.at(g, p))
                wait_alone(pe, weights["attn0"], pT_ready.sem, pT_ready.at(g, p + 1))
                for h in range(HP):
                    for e in range(2):
                        for s2 in range(2):
                            r = slice(s2 * S, s2 * S + S)
                            ins = mm(ps[e * S:(e + 1) * S, 6 + s2, h * S:(h + 1) * S],
                                     V0[r, p % 2, h * P + e * S:h * P + (e + 1) * S],
                                     probsT[r, p % 2, h, e * S:(e + 1) * S])
                ins.then_inc(o_done.sem, 1)

            def attn0_out(g):
                pe.wait_ge(o0_ready.sem, o0_ready.at(g, NP))
                for t in range(NP):
                    at = (t % 2) * P
                    for h in range(HP):
                        ins = mm(ps[:, 0, t * P:(t + 1) * P], KT[:, t // 2, h, at:at + P], w_o0[:, h, :], h == 0, h == HP - 1)
                ins.then_inc(attn_done.sem, 1)

            def attention0(g, nxt):
                keys0(g, 0, range(4))
                turn_norm(g, 1)
                queries0(g, 0)
                if nxt is not None:
                    turn_norm(nxt, 0)
                    in_proj(nxt)
                values0(g, 0)
                values0(g, 1)
                scores_of(g, 0, 0)
                if nxt is not None:
                    x_proj(nxt)
                scores_of(g, 0, 1)
                if nxt is not None:
                    dt_proj(nxt)
                queries0(g, 1)
                if nxt is not None:
                    pe.wait_ge(z_ready.sem, z_ready.at(nxt, 2))
                    pe.wait_ge(split_ready.sem, split_ready.at(nxt, 1))
                turn_probs(g, 0, 0)
                keys0(g, 1, (0, 1))
                weigh_values0(g, 0)
                keys0(g, 1, (2, 3))
                turn_probs(g, 0, 1)
                values0(g, 2)
                weigh_values0(g, 1)
                values0(g, 3)
                scores_of(g, 0, 2)
                scores_of(g, 0, 3)
                for p in (2, 3):
                    turn_probs(g, 0, p)
                    weigh_values0(g, p)
                attn0_out(g)

            def project1(g, k):
                if k == 1:
                    turn_norm(g, 3)
                    pe.wait_ge(xT_ready[1].sem, xT_ready[1].at(g, 3))
                    for c in range(2):
                        mm(ps[:, 2 * c, :], w_qkv1[:, c * D:(c + 1) * D], xT[:]).then_inc(qk1_done.sem, 1)
                        mm(ps[:, 2 * c + 1, :], w_sw1[:, c * D:(c + 1) * D], xT[:]).then_inc(qk1_done.sem, 1)
                    src, w_v = xT, w_qkv1[:, 2 * D:]
                else:
                    mm(ps[:, 2, :], w_qkvx[:, D:2 * D], ctxT[:]).then_inc(qk1_done.sem, 1)
                    src, w_v = ctxT, w_qkvx[:, 2 * D:]
                for t in range(NP):
                    ins = mm(ps[:, 5, t * P:(t + 1) * P], src[:, t * P:(t + 1) * P], w_v)
                ins.then_inc(v1_done.sem, 1)
                if k == 2:
                    turn_norm(g, 4)
                    pe.wait_ge(xT_ready[1].sem, xT_ready[1].at(g, 4))
                    mm(ps[:, 0, :], w_qkvx[:, 0:D], xT[:]).then_inc(qk1_done.sem, 1)

            def weigh_values1(g, k, p):
                pe.wait_ge(pT_ready.sem, pT_ready.at(g, k * NP + p + 1))
                if p >= 2:
                    pe.wait_ge(o1_ready.sem, o1_ready.at(g, (k - 1) * NP + p - 1))
                for h in range(HP):
                    ins = mm(ps[:, 6 + p % 2, h * 36:(h + 1) * 36], probsT[:, p % 2, h, :], V1[:, p, h].rearrange("p s f -> p (s f)"))
                ins.then_inc(o_done.sem, 1)

            def turn_o1(g, k, p):
                pe.wait_ge(o1_ready.sem, o1_ready.at(g, (k - 1) * NP + p + 1))
                if p == 0:
                    pe.wait_ge(pT_ready.sem, pT_ready.at(g, k * NP + 2))
                pe.transpose(ps[:, 4, p * P:(p + 1) * P], O1[:, p % 2].rearrange("p s h d -> p (s h d)"), ident).then_inc(o1T_done.sem, 1)

            def attn1_out(g, k, w_p):
                wait_alone(pe, weights["attn0"], o1T_ready.sem, o1T_ready.at(g, k))
                for t in range(NP):
                    for e in range(2):
                        for s2 in range(2):
                            r = slice(s2 * S, s2 * S + S)
                            ins = mm(ps[r, s2, t * P:(t + 1) * P], O1T[r, t, e, :], w_p[r, e, :], e == 0, e == 1)
                ins.then_inc(attn_done.sem, 1)

            def attention1(g, k, w_p):
                for p in range(3):
                    scores_of(g, k, p)
                turn_probs(g, k, 0)
                scores_of(g, k, 3)
                turn_probs(g, k, 1)
                weigh_values1(g, k, 0)
                for p in (1, 2):
                    turn_probs(g, k, p + 1)
                    weigh_values1(g, k, p)
                    turn_o1(g, k, p - 1)
                weigh_values1(g, k, 3)
                turn_o1(g, k, 2)
                turn_o1(g, k, 3)
                attn1_out(g, k, w_p)

            def route(g, m, w_r):
                l = 2 if m == 0 else 5
                turn_norm(g, l)
                pe.wait_ge(xT_ready[1].sem, xT_ready[1].at(g, l))
                for t in range(NP):
                    ins = mm(ps[:, 5, t * E:(t + 1) * E], xT[:, t * P:(t + 1) * P], w_r[:])
                ins.then_inc(route_done.sem, 1)

            def down(g, m, e, chunks, w):
                if m == 0:
                    pe.wait_ge(h0_done.sem, h0_done.at(g, C0 * (e + 1)))
                else:
                    pe.wait_ge(h1_act.sem, h1_act.at(g, (e + 1) * C1 // 2))
                    pe.wait_ge(h1_dve.sem, h1_dve.at(g, (e + 1) * C1 // 2))
                if e >= 2:
                    pe.wait_ge(acc_done.sem, acc_done.at(g, m * E + e - 1))
                elif e == 1 and m == 0:
                    pe.wait_ge(top_ready.sem, top_ready.at(g, 1))
                elif e == 1:
                    pe.wait_ge(b2_added.sem, b2_added.at(g, 1))
                for t in range(NP):
                    for c in range(chunks):
                        ins = mm(ps[:, 4 + e % 2, t * P:(t + 1) * P], hidden[:, e % 2, c, t * P:(t + 1) * P], w[:, e, c, :], c == 0, c == chunks - 1)
                ins.then_inc(down_done.sem, 1)

            def experts0(g, nxt):
                for e in range(E + 1):
                    for c in range(C0 if e < E else 0):
                        k = e * C0 + c
                        if k >= 2:
                            pe.wait_ge(gated_done.sem, gated_done.at(g, k - 1))
                            pe.wait_ge(up_copied.sem, up_copied.at(g, k - 1))
                        q = 2 * (k % 2)
                        mm(ps[:, q, :], w_gu[:, e, c * P:(c + 1) * P], xT[:])
                        mm(ps[:, q + 1, :], w_gu[:, e, F0 + c * P:F0 + (c + 1) * P], xT[:]).then_inc(gu_done.sem, 1)
                    if e < E and nxt is not None:
                        spread_bc(nxt, e, 1)
                    if e >= 1:
                        down(g, 0, e - 1, C0, w_dn)

            def experts1(g, nxt):
                for e in range(E + 1):
                    for c in range(C1 if e < E else 0):
                        k = e * C1 + c
                        if k >= 4:
                            by = h1_act if k % 2 == 0 else h1_dve
                            pe.wait_ge(by.sem, by.at(g, (k - 4) // 2 + 1))
                        mm(ps[:, k % 4, :], w_1[:, e, c * P:(c + 1) * P], xT[:]).then_inc(up_done.sem, 1)
                    if e < E and nxt is not None:
                        spread_bc(nxt, E + e, 1)
                    if e == 0:
                        pe.wait_ge(gate_w.sem, gate_w.at(g, 2))
                        pe.transpose(ps[:, 4, 0:P], gate.rearrange("p t e -> p (t e)"), ident).then_inc(gateT_done.sem, 1)
                        pe.wait_ge(gateT_ready.sem, gateT_ready.at(g, 1))
                        for t in range(NP):
                            ins = mm(ps[:, 5, t * P:(t + 1) * P], gateT[:], b_2[:, t, :])
                        ins.then_inc(b2_done.sem, 1)
                    if e == E and nxt is not None:
                        mamba_out(nxt)
                    if e >= 1:
                        down(g, 1, e - 1, C1, w_2)
                if nxt is not None:
                    turn_ctx(nxt)

            def group(g, nxt):
                pe.wait_ge(weights["attn0"].sem, need["attn0"])
                attention0(g, nxt)
                pe.wait_ge(weights["moe0"].sem, need["moe0"])
                route(g, 0, w_r0)
                experts0(g, nxt)
                pe.wait_ge(weights["attn1"].sem, need["attn1"])
                pe.wait_ge(swapped_set.sem, 1)
                if nxt is not None:
                    pe.wait_ge(hc_done.sem, hc_done.at(nxt, NC * N // 2))
                project1(g, 1)
                attention1(g, 1, w_p1)
                pe.wait_ge(weights["attnx"].sem, need["attnx"])
                project1(g, 2)
                attention1(g, 2, w_px)
                pe.wait_ge(weights["moe1"].sem, need["moe1"])
                route(g, 1, w_r1)
                experts1(g, nxt)

            pe.wait_ge(weights["mamba"].sem, need["mamba"])
            turn_norm(0, 0)
            in_proj(0)
            x_proj(0)
            dt_proj(0)
            pe.wait_ge(split_ready.sem, split_ready.at(0, 1))
            pe.wait_ge(z_ready.sem, z_ready.at(0, 2))
            for n in range(N):
                spread_bc(0, n, 2)
            mamba_out(0)
            turn_ctx(0)
            with pe.Fori(0, NG - 1) as g:
                group(g, g + 1)
            group(NG - 1, None)

        @block.scalar
        def _(act):
            def copy_norm(g, l):
                i, bank = min(l, 1), 6 if l == 1 else 4
                act.wait_ge(xnT_done[i].sem, xnT_done[i].at(g, max(l, 1)))
                act.copy((xT0, xT)[i][:], ps[:, bank, :]).then_inc(xT_ready[i].sem, 1)

            def conv_and_gate(g):
                for c in range(NC):
                    act.wait_ge(inproj_done.sem, inproj_done.at(g, c + 1))
                    act.activation(u_conv[:, c, :], ps[:, 4 + c, :], ACT.Identity, bias=b_conv[:, c:c + 1],
                                   scale=w_conv[:, c, 1:2]).then_inc(conv_mid.sem, 1)
                for c in range(NC):
                    act.wait_ge(inproj_done.sem, inproj_done.at(g, NC + c + 1))
                    act.activation(gate_act[:, c, :], ps[:, 6 + c, :], ACT.Silu).then_inc(gate_ready.sem, 1)
                for c in range(NC):
                    act.wait_ge(conv_done.sem, conv_done.at(g, c + 1))
                    act.activation(u_act[:, c, :], u_conv[:, c, :], ACT.Silu).then_inc(u_ready.sem, 1)

            def copy_d(g):
                for c in range(NC):
                    act.wait_ge(xproj_done.sem, xproj_done.at(g, c + 1))
                    act.copy(d_raw[:, c, :], ps[:, 4 + c, :]).then_inc(draw_ready.sem, 1)

            def add_dt_bias(g):
                for c in range(NC):
                    act.wait_ge(dt_done.sem, dt_done.at(g, c + 1))
                    act.activation(dt_z[:, c, :], ps[:, 4 + c, :], ACT.Identity, bias=b_dt[:, c:c + 1]).then_inc(z_ready.sem, 1)

            def softplus_log(g):
                act.wait_ge(nz_ready.sem, nz_ready.at(g, 1))
                act.activation(dt_e, dt_e, ACT.Exp).then_inc(e_ready.sem, 1)
                act.wait_ge(e_ready.sem, e_ready.at(g, 1))
                act.activation(dt_e, dt_e, ACT.Ln, bias=1.0).then_inc(ln_ready.sem, 1)

            def decays(g, n):
                if n == 0:
                    act.wait_ge(delta_ready.sem, delta_ready.at(g, 1))
                for c in range(NC):
                    k = NC * n + c
                    if k >= 3:
                        act.wait_ge(scan_done.sem, scan_done.at(g, k - 2))
                    act.activation(decay[:, k % 3, :], delta[:, c, :], ACT.Exp,
                                   scale=a_neg[:, c, n:n + 1]).then_inc(decay_ready.sem, 1)

            def copy_ctx(g):
                act.wait_ge(ctxT_done.sem, ctxT_done.at(g, 1))
                act.copy(ctxT[:], ps[:, 7, :]).then_inc(ctxT_ready.sem, 1)

            def copy_keys0(g, x, units):
                for u in units:
                    act.wait_ge(k0_done.sem, k0_done.at(g, 4 * x + u + 1))
                    act.copy(KT[:, x, 2 * u:2 * u + 2, :].rearrange("p h t -> p (h t)"), ps[:, u, :]).then_inc(k0_ready.sem, 1)

            def top_queries0(g, x):
                act.wait_ge(qd_zero.sem, qd_zero.at(g, 2))
                for u in range(4):
                    act.wait_ge(q0_done.sem, q0_done.at(g, 4 * x + u + 1))
                    act.mul(Qd[0:S, 2 * u:2 * u + 2, :, 0:S], ps[0:S, u, :].rearrange("p (h b i) -> p h b i", h=2, b=GH),
                            0.125).then_inc(q0_top.sem, 1)

            def copy_values0(g, p):
                act.wait_ge(v0_done.sem, v0_done.at(g, p + 1))
                q = 2 * (p % 2)
                act.copy(V0[:, p % 2, :], ps[:, q:q + 2, :].rearrange("p k f -> p (k f)")).then_inc(v0_ready.sem, 1)

            def exps(g, k, p):
                if k == 0:
                    act.wait_ge(shifted0.sem, shifted0.at(g, p + 1))
                else:
                    act.wait_ge(shifted1.sem, shifted1.at(g, (k - 1) * NP + p + 1))
                act.activation(scores[:, p % 3, :], scores[:, p % 3, :], ACT.Exp).then_inc(exp_done.sem, 1)

            def copy_probs(g, k, p):
                bank = probs_bank(k, p)
                act.wait_ge(pT_done.sem, pT_done.at(g, k * NP + p + 1))
                if p >= 2:
                    act.wait_ge(o_done.sem, o_done.at(g, k * NP + p - 1))
                act.copy(probsT[:, p % 2].rearrange("p h q -> p (h q)"),
                         ps[:, bank:bank + 2, :].rearrange("p k f -> p (k f)")).then_inc(pT_ready.sem, 1)

            def copy_outputs0(g, p):
                act.wait_ge(o_done.sem, o_done.at(g, p + 1))
                at = (p % 2) * P
                act.copy(KT[:, p // 2, :, at:at + P].rearrange("p h (s i) -> p s h i", s=2),
                         ps[:, 6:8, :].rearrange("p s (h i) -> p s h i", h=HP)).then_inc(o0_ready.sem, 1)

            def attention0(g, nxt):
                copy_keys0(g, 0, range(4))
                copy_norm(g, 1)
                top_queries0(g, 0)
                if nxt is not None:
                    copy_norm(nxt, 0)
                    conv_and_gate(nxt)
                copy_values0(g, 0)
                copy_values0(g, 1)
                if nxt is not None:
                    copy_d(nxt)
                exps(g, 0, 0)
                if nxt is not None:
                    add_dt_bias(nxt)
                top_queries0(g, 1)
                exps(g, 0, 1)
                if nxt is not None:
                    softplus_log(nxt)
                    act.wait_ge(delta_ready.sem, delta_ready.at(nxt, 1))
                copy_probs(g, 0, 0)
                copy_keys0(g, 1, (0, 1))
                copy_keys0(g, 1, (2, 3))
                copy_outputs0(g, 0)
                copy_probs(g, 0, 1)
                copy_values0(g, 2)
                copy_outputs0(g, 1)
                copy_values0(g, 3)
                exps(g, 0, 2)
                exps(g, 0, 3)
                for p in (2, 3):
                    copy_probs(g, 0, p)
                    copy_outputs0(g, p)

            def expand(g, k, x):
                if x == 0:
                    q1_ready = q1_rot if k == 1 else q1_lin
                    act.wait_ge(q1_ready.sem, q1_ready.at(g, 1))
                for h in range(HEADS - 6, HEADS):
                    ins = act.mul(Qx[x][:, h // 2, :, (h % 2) * S:(h % 2 + 1) * S], q1[:, x * TH:(x + 1) * TH].rearrange("p (b i) -> p b i", b=GH),
                                  kc[:, K_HEAD + h:K_HEAD + h + 1])
                ins.then_inc(qm_act.sem, 1)

            def copy_o1(g, k):
                act.wait_ge(o1T_done.sem, o1T_done.at(g, k * NP))
                act.copy(O1T.rearrange("p t e i -> p (t e i)"), ps[:, 4, :]).then_inc(o1T_ready.sem, 1)

            def attention1(g, k):
                if k == 2:
                    act.wait_ge(qk1_done.sem, qk1_done.at(g, 5))
                    act.activation(kT1[:], ps[:, 2, :], ACT.Identity, bias=b_qkx[:, 1:2]).then_inc(k1_lin.sem, 1)
                copy_norm(g, 2 + k)
                if k == 2:
                    act.wait_ge(qk1_done.sem, qk1_done.at(g, 6))
                    act.activation(q1[:], ps[:, 0, :], ACT.Identity, bias=b_qkx[:, 0:1]).then_inc(q1_lin.sem, 1)
                expand(g, k, 0)
                expand(g, k, 1)
                exps(g, k, 0)
                copy_probs(g, k, 0)
                exps(g, k, 1)
                exps(g, k, 2)
                copy_probs(g, k, 1)
                copy_probs(g, k, 2)
                exps(g, k, 3)
                copy_probs(g, k, 3)
                copy_o1(g, k)

            def route(g, m):
                copy_norm(g, 2 if m == 0 else 5)
                act.wait_ge(top_ready.sem, top_ready.at(g, m + 1))
                act.activation(top_e[:], top_e[:], ACT.Exp).then_inc(tope_ready.sem, 1)

            def experts0(g, nxt):
                for e in range(E):
                    if nxt is not None:
                        decays(nxt, e)
                    for c in range(C0):
                        k = e * C0 + c
                        act.wait_ge(gu_done.sem, gu_done.at(g, k + 1))
                        if k >= 2:
                            act.wait_ge(h0_done.sem, h0_done.at(g, k - 1))
                        act.activation(gated[:, k % 2, :], ps[:, 2 * (k % 2), :], ACT.Tanh, scale=0.5).then_inc(tanh_done.sem, 1)
                        act.copy(up_copy[:, k % 2, :], ps[:, 2 * (k % 2) + 1, :]).then_inc(up_copied.sem, 1)

            def experts1(g, nxt):
                for e in range(E):
                    if e == 1:
                        act.wait_ge(gateT_done.sem, gateT_done.at(g, 1))
                        act.copy(gateT[:], ps[:, 4, 0:P]).then_inc(gateT_ready.sem, 1)
                    if nxt is not None:
                        decays(nxt, E + e)
                    for c in range(0, C1, 2):
                        k = e * C1 + c
                        act.wait_ge(up_done.sem, up_done.at(g, k + 1))
                        if e >= 2 and c == 0:
                            act.wait_ge(down_done.sem, down_done.at(g, E + e - 1))
                        act.activation(hidden[:, e % 2, c, :], ps[:, k % 4, :], ACT.Relu, bias=b_1[:, e, c:c + 1]).then_inc(h1_act.sem, 1)
                if nxt is not None:
                    copy_ctx(nxt)

            def group(g, nxt):
                attention0(g, nxt)
                route(g, 0)
                experts0(g, nxt)
                attention1(g, 1)
                attention1(g, 2)
                route(g, 1)
                experts1(g, nxt)

            act.wait_ge(weights["mamba"].sem, need["mamba"])
            act.activation(a_neg[:], a_neg[:], ACT.Exp).then_inc(a_exp.sem, 1)
            copy_norm(0, 0)
            conv_and_gate(0)
            copy_d(0)
            add_dt_bias(0)
            softplus_log(0)
            for n in range(N):
                decays(0, n)
            copy_ctx(0)
            with act.Fori(0, NG - 1) as g:
                group(g, g + 1)
            group(NG - 1, None)

        @block.gpsimd
        def _(pool):
            def root(g, l):
                i = min(l, 1)
                pool.wait_ge(var_ready[i].sem, var_ready[i].at(g, max(l, 1)))
                pool.tensor_tensor(rstd[i][:], var_eps[i][:], kc[:, K_HALF:K_ALL], ALU.pow).then_inc(rstd_ready[i].sem, 1)

            def keep_x(g, last):
                if last is not None:
                    pool.wait_ge(x_mixed.sem, x_mixed.at(last, 1))
                    wait_alone(pool, zeros_set, x_loaded.sem, x_loaded.at(g, 16))
                else:
                    pool.wait_ge(x_loaded.sem, x_loaded.at(g, 16))
                pool.tensor_copy(x_keep[:], x_in[:]).then_inc(x_kept.sem, 1)

            def add_bias(g, l, x, bias):
                pool.wait_ge(xn_ready[1].sem, xn_ready[1].at(g, l))
                pool.tensor_tensor(x[:], x[:], bias[:].unsqueeze(1).to_broadcast([P, NP, D]), ALU.add).then_inc(biased.sem, 1)

            def add_y(g, n):
                for c in range(NC):
                    k = NC * n + c
                    pool.wait_ge(hc_done.sem, hc_done.at(g, k + 1))
                    if k >= 2:
                        pool.wait_ge(y_added.sem, y_added.at(g, k - 1))
                    pool.tensor_tensor(y_sum[:, c, :], y_sum[:, c, :], state[:, k % 3, :], ALU.add).then_inc(y_added.sem, 1)

            def normalise(g, p):
                pool.wait_ge(sum_ready.sem, sum_ready.at(g, p + 1))
                v = scores[:, p % 3, :].rearrange("p (r j) -> p r j", j=S)
                pool.tensor_tensor(v, v, row_sum[:, p % 3, :].unsqueeze(2).to_broadcast([P, 2 * HP, S]), ALU.mult).then_inc(normed.sem, 1)

            def shift(g, k, p):
                pool.wait_ge(max_ready.sem, max_ready.at(g, (k - 1) * NP + p + 1))
                v = scores[:, p % 3, :].rearrange("p (r j) -> p r j", j=S)
                pool.tensor_tensor(v, v, row_max[:, p % 3, :].unsqueeze(2).to_broadcast([P, 2 * HP, S]), ALU.subtract).then_inc(shifted1.sem, 1)

            def zero_qd(g, last):
                if last is not None:
                    wait_alone(pool, zeros_set, s_done.sem, s_done.at(last, 3 * NP))
                pool.memset(Qd[0:S, :, :, S:P], 0.0).then_inc(qd_zero.sem, 1)
                if last is None:
                    pool.wait_ge(qd_zero.sem, qd_zero.at(g, 1))
                else:
                    wait_alone(pool, zeros_set, qd_zero.sem, qd_zero.at(g, 1))
                pool.memset(Qd[S:P, :, :, 0:S], 0.0).then_inc(qd_zero.sem, 1)
                pool.wait_ge(qd_zero.sem, qd_zero.at(g, 2))

            def experts0(g, nxt):
                for e in range(E):
                    for c in range(C0):
                        k = e * C0 + c
                        pool.wait_ge(gated_done.sem, gated_done.at(g, k + 1))
                        pool.wait_ge(up_copied.sem, up_copied.at(g, k + 1))
                        if e >= 2 and c == 0:
                            pool.wait_ge(down_done.sem, down_done.at(g, e - 1))
                        pool.tensor_tensor(hidden[:, e % 2, c, :], gated[:, k % 2, :], up_copy[:, k % 2, :],
                                           ALU.mult).then_inc(h0_done.sem, 1)
                    if nxt is not None:
                        add_y(nxt, e)

            def group(g, nxt):
                pool.wait_ge(weights["attn0"].sem, need["attn0"])
                add_bias(g, 1, x_mix, bo0)
                if nxt is not None:
                    keep_x(nxt, g)
                    root(nxt, 0)
                for p in range(NP):
                    normalise(g, p)
                root(g, 2)
                experts0(g, nxt)
                root(g, 3)
                pool.wait_ge(weights["attn1"].sem, need["attn1"])
                add_bias(g, 3, x_res, bo1)
                for p in range(NP):
                    shift(g, 1, p)
                root(g, 4)
                pool.wait_ge(weights["attnx"].sem, need["attnx"])
                add_bias(g, 4, x_res, box)
                for p in range(NP):
                    shift(g, 2, p)
                root(g, 5)
                if nxt is not None:
                    zero_qd(nxt, g)
                    for n in range(E, N):
                        add_y(nxt, n)
                    root(nxt, 1)

            pool.memset(b_2[:], 0.0)
            pool.memset(gate[:], 0.0)
            pool.memset(V1[:], 0.0).then_inc(zeros_set.sem, 1)
            for s2 in range(2):
                pool.wait_ge(zeros_set.sem, 1 + s2)
                pool.memset(V1[s2 * S:(s2 + 1) * S, :, :, s2, 16:18], 1.0).then_inc(zeros_set.sem, 1)
            pool.wait_ge(zeros_set.sem, 3)
            pool.wait_ge(weights["mamba"].sem, need["mamba"])
            keep_x(0, None)
            root(0, 0)
            zero_qd(0, None)
            for n in range(N):
                add_y(0, n)
            root(0, 1)
            with pool.Fori(0, NG - 1) as g:
                group(g, g + 1)
            group(NG - 1, None)

        @block.vector
        def _(dve):
            links = {mamba_chain: 0, layer_chain: 0}

            def link(chain, g, ins):
                links[chain] += 1
                ins.then_inc(chain.sem, 1)
                dve.wait_ge(chain.sem, chain.at(g, links[chain]))

            def link_alone(chain, g, ins):
                links[chain] += 1
                ins.then_inc(chain.sem, 1)
                wait_alone(dve, setup, chain.sem, chain.at(g, links[chain]))

            def norm(g, l):
                src = (x_in, x_mix)[l] if l < 2 else x_res
                chain = mamba_chain if l < 2 else layer_chain
                i = min(l, 1)
                if l == 0:
                    dve.wait_ge(x_loaded.sem, x_loaded.at(g, 16))
                for t in range(NP):
                    ins = dve.bn_stats(stats[i][:, t, :], src[:, t, :])
                link_alone(chain, g, ins)
                for t in range(NP):
                    ins = dve.bn_aggr(mean_var[i][:, t, :], stats[i][:, t, :])
                link(chain, g, ins)
                dve.tensor_scalar(var_eps[i][:], mean_var[i][:, :, 1], LN_EPS, None, ALU.add).then_inc(var_ready[i].sem, 1)
                dve.wait_ge(rstd_ready[i].sem, rstd_ready[i].at(g, max(l, 1)))
                for t in range(NP):
                    ins = dve.tensor_scalar(xn[i][:, t, :], src[:, t, :], mean_var[i][:, t, 0:1], rstd[i][:, t:t + 1], ALU.subtract, ALU.mult)
                ins.then_inc(xn_ready[i].sem, 1)

            def conv(g):
                for c in range(NC):
                    dve.wait_ge(conv_mid.sem, conv_mid.at(g, c + 1))
                    u = u_conv[:, c, :].rearrange("p (b t) -> p b t", b=GB)
                    raw = ps[:, 4 + c, :].rearrange("p (b t) -> p b t", b=GB)
                    link(mamba_chain, g, dve.scalar_tensor_tensor(u[:, :, 1:S], raw[:, :, 0:S - 1], w_conv[:, c, 0:1], u[:, :, 1:S], ALU.mult, ALU.add))
                    dve.scalar_tensor_tensor(u[:, :, 0:S - 1], raw[:, :, 1:S], w_conv[:, c, 2:3], u[:, :, 0:S - 1],
                                             ALU.mult, ALU.add).then_inc(conv_done.sem, 1)

            def split_bc(g):
                dve.wait_ge(xproj_done.sem, xproj_done.at(g, 3))
                link(mamba_chain, g, dve.tensor_copy(bc_split[:], ps[0:96, 6, :]))
                link(mamba_chain, g, dve.tensor_tensor(bc_res, ps[0:96, 6, :], bc_split[:], ALU.subtract))
                dve.tensor_copy(bc_split[32:64, :], bc_res[32:64, :])
                link(mamba_chain, g, dve.tensor_copy(bc_mid[64:96, :], bc_res[64:96, :]))
                dve.tensor_tensor(bc_split[64:96, :], bc_res[64:96, :], bc_mid[64:96, :], ALU.subtract).then_inc(split_ready.sem, 1)

            def minus_abs(g):
                dve.wait_ge(z_ready.sem, z_ready.at(g, 2))
                dve.scalar_tensor_tensor(dt_e, dt_z, -1.0, dt_z, ALU.mult, ALU.min).then_inc(nz_ready.sem, 1)

            def find_delta(g):
                dve.wait_ge(ln_ready.sem, ln_ready.at(g, 1))
                link(mamba_chain, g, dve.scalar_tensor_tensor(delta[:], dt_z, 0.0, dt_e, ALU.max, ALU.add))
                for c in range(NC):
                    dve.tensor_scalar(y_sum[:, c, :], u_act[:, c, :], d_par[:, c:c + 1], None, ALU.mult)
                link(mamba_chain, g, dve.tensor_tensor(du[:], delta[:], u_act, ALU.mult))
                dve.memset(delta.rearrange("p c (b t) -> p (c b) t", t=S)[:, :, 0:1], FAR).then_inc(delta_ready.sem, 1)

            def scan_step(g, n, ring):
                b_bank, c_bank = bc_banks(n, ring)
                dve.wait_ge(bc_spread.sem, bc_spread.at(g, n + 1))
                for c in range(NC):
                    k = NC * n + c
                    if k >= 3:
                        dve.wait_ge(y_added.sem, y_added.at(g, k - 2))
                    dve.tensor_tensor(state[:, k % 3, :], du[:, c, :], ps[:, b_bank, :], ALU.mult).then_inc(bu_done.sem, 1)
                for c in range(NC):
                    k = NC * n + c
                    dve.wait_ge(bu_done.sem, bu_done.at(g, k + 1))
                    dve.wait_ge(decay_ready.sem, decay_ready.at(g, k + 1))
                    dve.tensor_tensor_scan(state[:, k % 3, :], decay[:, k % 3, :], state[:, k % 3, :], 0.0, ALU.mult, ALU.add).then_inc(scan_done.sem, 1)
                for c in range(NC):
                    k = NC * n + c
                    dve.wait_ge(scan_done.sem, scan_done.at(g, k + 1))
                    dve.tensor_tensor(state[:, k % 3, :], state[:, k % 3, :], ps[:, c_bank, :], ALU.mult).then_inc(hc_done.sem, 1)

            def gate_y(g):
                dve.wait_ge(y_added.sem, y_added.at(g, NC * N))
                dve.wait_ge(gate_ready.sem, gate_ready.at(g, 2))
                dve.tensor_tensor(y_sum[:], y_sum[:], gate_act[:], ALU.mult).then_inc(yg_ready.sem, 1)

            def mix_x(g):
                dve.wait_ge(mamba_done.sem, mamba_done.at(g, 1))
                dve.wait_ge(x_kept.sem, x_kept.at(g, 1))
                dve.tensor_tensor(x_mix.rearrange("p t d -> p (t d)"), x_keep.rearrange("p t d -> p (t d)"), ps[:, 6, :],
                                  ALU.add).then_inc(x_mixed.sem, 1)
                dve.wait_ge(x_mixed.sem, x_mixed.at(g, 1))

            def softmax_front(g, k, p):
                dve.wait_ge(s_done.sem, s_done.at(g, k * NP + p + 1))
                s_ps = ps[:, 2 * (p % 2):2 * (p % 2) + 2, :].rearrange("p k f -> p (k f)")
                if p == 3:
                    dve.wait_ge(pT_done.sem, pT_done.at(g, k * NP + 1))
                v = scores[:, p % 3, :]
                if k == 0:
                    bias = bias0[:, p * P:(p + 1) * P].unsqueeze(1).to_broadcast([P, HP, P])
                    ins = dve.tensor_tensor(v.rearrange("p (h j) -> p h j", h=HP), s_ps.rearrange("p (h j) -> p h j", h=HP), bias, ALU.add)
                else:
                    at = K_CAUSAL if k == 1 else K_CAUSAL9
                    bias = kc[:, at:at + S].unsqueeze(1).to_broadcast([P, 2 * HP, S])
                    ins = dve.scalar_tensor_tensor(v.rearrange("p (r j) -> p r j", j=S), s_ps.rearrange("p (r j) -> p r j", j=S),
                                                   HD ** -0.5, bias, ALU.mult, ALU.add)
                ins.then_inc(s_read.sem, 1)
                dve.wait_ge(s_read.sem, s_read.at(g, k * NP + p + 1))
                rows = v.rearrange("p (r j) -> p r j", j=S)
                ins = dve.reduce_max(row_max[:, p % 3, :], rows, AX.X)
                if k == 0:
                    link(layer_chain, g, ins)
                    dve.tensor_tensor(rows, rows, row_max[:, p % 3, :].unsqueeze(2).to_broadcast([P, 2 * HP, S]),
                                      ALU.subtract).then_inc(shifted0.sem, 1)
                else:
                    ins.then_inc(max_ready.sem, 1)

            def softmax_sum(g, p):
                dve.wait_ge(exp_done.sem, exp_done.at(g, p + 1))
                link(layer_chain, g, dve.reduce_sum(row_sum[:, p % 3, :], scores[:, p % 3, :].rearrange("p (r j) -> p r j", j=S), AX.X))
                dve.reciprocal(row_sum[:, p % 3, :], row_sum[:, p % 3, :]).then_inc(sum_ready.sem, 1)

            def bottom_queries0(g, x):
                dve.wait_ge(qd_zero.sem, qd_zero.at(g, 2))
                for u in range(4):
                    dve.wait_ge(q0_done.sem, q0_done.at(g, 4 * x + u + 1))
                    dve.tensor_scalar(Qd[S:P, 2 * u:2 * u + 2, :, S:P], ps[S:P, u, :].rearrange("p (h b i) -> p h b i", h=2, b=GH), 0.125, None,
                                      ALU.mult).then_inc(q0_bottom.sem, 1)

            def mask_bias(g):
                dve.wait_ge(mask_loaded.sem, mask_loaded.at(g, 16))
                dve.tensor_scalar(bias0[:], mask_in[:], -NEG, NEG, ALU.mult, ALU.add).then_inc(mask_free.sem, 1)
                dve.wait_ge(mask_free.sem, mask_free.at(g, 1))
                b3 = bias0.rearrange("p (b j) -> p b j", b=GB)
                link(layer_chain, g, dve.tensor_tensor(b3, b3, kc[:, K_CAUSAL:K_CAUSAL9].unsqueeze(1).to_broadcast([P, GB, S]), ALU.min))

            def attention0(g, nxt):
                mask_bias(g)
                if nxt is not None:
                    norm(nxt, 0)
                bottom_queries0(g, 0)
                if nxt is not None:
                    conv(nxt)
                    dve.wait_ge(u_ready.sem, u_ready.at(nxt, 2))
                    split_bc_first(nxt)
                softmax_front(g, 0, 0)
                softmax_front(g, 0, 1)
                if nxt is not None:
                    minus_abs(nxt)
                bottom_queries0(g, 1)
                softmax_sum(g, 0)
                softmax_sum(g, 1)
                if nxt is not None:
                    find_delta(nxt)
                softmax_front(g, 0, 2)
                softmax_front(g, 0, 3)
                softmax_sum(g, 2)
                softmax_sum(g, 3)
                dve.wait_ge(attn_done.sem, attn_done.at(g, 1))
                dve.wait_ge(biased.sem, biased.at(g, 1))
                dve.wait_ge(out_free.sem, out_free.at(g, 1))
                link(layer_chain, g, dve.tensor_tensor(x_res.rearrange("p t d -> p (t d)"), x_mix.rearrange("p t d -> p (t d)"), ps[:, 0, :], ALU.add))

            def split_bc_first(g):
                split_bc(g)
                dve.wait_ge(split_ready.sem, split_ready.at(g, 1))

            def rotate(g):
                for c in range(2):
                    cos = kc[:, K_COS:K_SIN].unsqueeze(1).to_broadcast([P, GB, S])
                    sin = kc[:, K_SIN:K_HEAD].unsqueeze(1).to_broadcast([P, GB, S])
                    part = scores[:, c, :].rearrange("p (x t) -> p x t", x=2)
                    for swapped, table, b in ((0, cos, b_qk1), (1, sin, b_sw1)):
                        dve.wait_ge(qk1_done.sem, qk1_done.at(g, 2 * c + swapped + 1))
                        ins = dve.scalar_tensor_tensor(part[:, swapped, :].rearrange("p (b i) -> p b i", b=GB),
                                                       ps[:, 2 * c + swapped, :].rearrange("p (b i) -> p b i", b=GB),
                                                       b[:, c:c + 1], table, ALU.add, ALU.mult)
                    link(layer_chain, g, ins)
                    dst, ready = (q1, q1_rot) if c == 0 else (kT1, k1_rot)
                    dve.tensor_tensor(dst[:], part[:, 0, :], part[:, 1, :], ALU.add).then_inc(ready.sem, 1)

            def add_value_bias(g, k):
                dve.wait_ge(v1_done.sem, v1_done.at(g, k))
                for s2 in range(2):
                    r = slice(s2 * S, (s2 + 1) * S)
                    bias = (bv1 if k == 1 else bvx)[r].rearrange("p (h d) -> p h d", h=HP).unsqueeze(1).to_broadcast([S, NP, HP, 16])
                    ins = dve.tensor_tensor(V1[r, :, :, s2, 0:16], ps[r, 5, :].rearrange("p (t h d) -> p t h d", t=NP, h=HP), bias, ALU.add)
                ins.then_inc(v1_ready.sem, 1)

            def expand(g, k, x):
                if x == 0:
                    q1_ready = q1_rot if k == 1 else q1_lin
                    dve.wait_ge(q1_ready.sem, q1_ready.at(g, 1))
                for h in range(HEADS - 6):
                    ins = dve.tensor_scalar(Qx[x][:, h // 2, :, (h % 2) * S:(h % 2 + 1) * S], q1[:, x * TH:(x + 1) * TH].rearrange("p (b i) -> p b i", b=GH),
                                            kc[:, K_HEAD + h:K_HEAD + h + 1], None, ALU.mult)
                ins.then_inc(qm_dve.sem, 1)

            def scale_outputs(g, k, p):
                dve.wait_ge(o_done.sem, o_done.at(g, k * NP + p + 1))
                o_ps = ps[:, 6 + p % 2, 0:HP * 36].rearrange("p (h s f) -> p s h f", h=HP, s=2)
                link(layer_chain, g, dve.reciprocal(row_sum[:, p % 3, :].rearrange("p (s h) -> p s h", s=2), o_ps[:, :, :, 16]))
                for e in range(2):
                    r = slice(e * S, (e + 1) * S)
                    inv = row_sum[r, p % 3, :].rearrange("p (s h) -> p s h", s=2).unsqueeze(3).to_broadcast([S, 2, HP, HD])
                    ins = dve.tensor_tensor(O1[r, p % 2], o_ps[r, :, :, e * HD:(e + 1) * HD], inv, ALU.mult)
                ins.then_inc(o1_ready.sem, 1)

            def attention1(g, k):
                if k == 1:
                    norm(g, 3)
                    rotate(g)
                    add_value_bias(g, 1)
                else:
                    norm(g, 4)
                    add_value_bias(g, 2)
                expand(g, k, 0)
                if k == 1:
                    dve.wait_ge(k1_rot.sem, k1_rot.at(g, 1))
                softmax_front(g, k, 0)
                expand(g, k, 1)
                for p in range(1, NP):
                    softmax_front(g, k, p)
                for p in range(NP):
                    scale_outputs(g, k, p)
                dve.wait_ge(attn_done.sem, attn_done.at(g, 1 + k))
                dve.wait_ge(biased.sem, biased.at(g, 1 + k))
                for s2 in range(2):
                    r = slice(s2 * S, (s2 + 1) * S)
                    x_half = x_res[r].rearrange("p t d -> p (t d)")
                    ins = dve.tensor_tensor(x_half, x_half, ps[r, s2, :], ALU.add)
                link(layer_chain, g, ins)

            def routing(g, m):
                dve.wait_ge(route_done.sem, route_done.at(g, m + 1))
                ps_l = ps[:, 5, 0:NP * E].rearrange("p (t e) -> p t e", t=NP)
                if m == 0:
                    link_alone(layer_chain, g, dve.tensor_copy(logits[:], ps_l))
                else:
                    link_alone(layer_chain, g, dve.tensor_tensor(logits[:], ps_l, br1[:].unsqueeze(1).to_broadcast([P, NP, E]), ALU.add))
                for t in range(NP):
                    ins = dve.max(top[:, t, :], logits[:, t, :])
                link_alone(layer_chain, g, ins)
                for t in range(NP):
                    ins = dve.max_index(top_at[:, t, :], top[:, t, :], logits[:, t, :])
                dve.tensor_tensor(top_e[:], top[:, :, 1], top[:, :, 0], ALU.subtract).then_inc(top_ready.sem, 1)
                dve.wait_ge(top_ready.sem, top_ready.at(g, m + 1))
                link(layer_chain, g, dve.tensor_copy(top_atf[:], top_at[:, :, 0:2]))
                iota = kc[:, K_IOTA:K_HALF].unsqueeze(1).to_broadcast([P, NP, E])
                for r in range(2):
                    dve.tensor_tensor(pick[:, :, r, :], iota, top_atf[:, :, r:r + 1].to_broadcast([P, NP, E]), ALU.is_equal)
                dve.wait_ge(tope_ready.sem, tope_ready.at(g, m + 1))
                link(layer_chain, g, dve.tensor_scalar(top_w[:, :, 1], top_e[:], 1.0, 2.0 if m == 0 else 1.0, ALU.add, ALU.mult))
                link(layer_chain, g, dve.reciprocal(top_w[:, :, 0], top_w[:, :, 1]))
                link(layer_chain, g, dve.tensor_tensor(top_w[:, :, 1], top_w[:, :, 0], top_e[:], ALU.mult))
                link(layer_chain, g, dve.tensor_tensor(pick[:], pick[:], top_w[:].unsqueeze(3).to_broadcast([P, NP, 2, E]), ALU.mult))
                dve.tensor_tensor(gate[:, :, 0:E], pick[:, :, 0, :], pick[:, :, 1, :], ALU.add).then_inc(gate_w.sem, 1)

            def accumulate(g, m, e):
                dve.wait_ge(down_done.sem, down_done.at(g, m * E + e + 1))
                if e == 0:
                    dve.wait_ge(gate_w.sem, gate_w.at(g, m + 1))
                if e >= 1:
                    dve.wait_ge(acc_done.sem, acc_done.at(g, m * E + e))
                for t in range(NP):
                    ins = dve.scalar_tensor_tensor(x_res[:, t, :], ps[:, 4 + e % 2, t * P:(t + 1) * P], gate[:, t, e:e + 1],
                                                   x_res[:, t, :], ALU.mult, ALU.add)
                ins.then_inc(acc_done.sem, 1)

            def experts0(g, nxt):
                for e in range(E + 1):
                    for c in range(C0 if e < E else 0):
                        k = e * C0 + c
                        dve.wait_ge(tanh_done.sem, tanh_done.at(g, k + 1))
                        dve.scalar_tensor_tensor(gated[:, k % 2, :], gated[:, k % 2, :], 1.0, ps[:, 2 * (k % 2), :],
                                                 ALU.add, ALU.mult).then_inc(gated_done.sem, 1)
                    if e < E and nxt is not None:
                        scan_step(nxt, e, 1)
                    if e >= 1:
                        accumulate(g, 0, e - 1)
                dve.wait_ge(acc_done.sem, acc_done.at(g, E))

            def experts1(g, nxt):
                for e in range(E + 1):
                    for c in range(1, C1 if e < E else 0, 2):
                        k = e * C1 + c
                        dve.wait_ge(up_done.sem, up_done.at(g, k + 1))
                        if e >= 2 and c == 1:
                            dve.wait_ge(down_done.sem, down_done.at(g, E + e - 1))
                        dve.tensor_scalar(hidden[:, e % 2, c, :], ps[:, k % 4, :], b_1[:, e, c:c + 1], 0.0, ALU.add,
                                          ALU.max).then_inc(h1_dve.sem, 1)
                    if e < E and nxt is not None:
                        scan_step(nxt, E + e, 1)
                    if e == 0:
                        dve.wait_ge(b2_done.sem, b2_done.at(g, 1))
                        x_flat = x_res.rearrange("p t d -> p (t d)")
                        dve.tensor_tensor(x_flat, x_flat, ps[:, 5, :], ALU.add).then_inc(b2_added.sem, 1)
                        dve.wait_ge(b2_added.sem, b2_added.at(g, 1))
                    if e == E and nxt is not None:
                        gate_y(nxt)
                        mix_x(nxt)
                        norm(nxt, 1)
                    if e >= 1:
                        accumulate(g, 1, e - 1)

            def group(g, nxt):
                links.update({mamba_chain: 0, layer_chain: 0})
                attention0(g, nxt)
                norm(g, 2)
                routing(g, 0)
                experts0(g, nxt)
                attention1(g, 1)
                attention1(g, 2)
                norm(g, 5)
                routing(g, 1)
                experts1(g, nxt)
                assert links == {mamba_chain: 0 if nxt is None else MAMBA_LINKS, layer_chain: LAYER_LINKS}, list(links.values())

            dve.wait_ge(weights["mamba"].sem, need["mamba"])
            dve.wait_ge(a_exp.sem, 1)
            dve.tensor_scalar(a_neg[:], a_neg[:], -1.0, None, ALU.mult)
            dve.tensor_copy(sel[:], kc[0:96, K_SEL:K_IOTA]).then_inc(setup.sem, 1)
            dve.wait_ge(setup.sem, 1)
            norm(0, 0)
            conv(0)
            split_bc(0)
            minus_abs(0)
            find_delta(0)
            for n in range(N):
                scan_step(0, n, 2)
            gate_y(0)
            mix_x(0)
            norm(0, 1)
            assert links[mamba_chain] == MAMBA_LINKS, links[mamba_chain]
            dve.wait_ge(weights["attn1"].sem, need["attn1"])
            wq = w_qkv1[:, 0:2 * D].rearrange("p (k two) -> p k two", two=2)
            sw = w_sw1[:].rearrange("p (k two) -> p k two", two=2)
            for odd in range(2):
                ins = dve.tensor_copy(sw[:, :, odd], wq[:, :, 1 - odd])
            ins.then_inc(swapped_set.sem, 1)
            with dve.Fori(0, NG - 1) as g:
                group(g, g + 1)
            group(NG - 1, None)


def probs_bank(k, p):
    return 4 if k == 0 or p < 2 else 2 * (p % 2)


def bc_banks(n, ring):
    return (6, 7) if ring == 1 else (4 + n % 2, 6 + n % 2)


def pairs_of(x, g):
    return x.rearrange("(b s) i d -> (s i) b d", s=2)[:, bass.ds(g * NP, NP), :]


NAMES = """x ctx_1024 mask_BxS2_bk0 L0_attn_in_proj_w L0_attn_conv_w L0_attn_conv_b L0_attn_x_proj_w L0_attn_dt_proj_w
L0_attn_dt_proj_b L0_attn_out_proj_w L0_attn_A_log L0_attn_D_param L0_xattn_Wq L0_xattn_Wkv L0_xattn_Wo L0_xattn_bo
L0_ffn_gate_w L0_ffn_gate_up_w L0_ffn_down_w L1_attn_Wqkv L1_attn_bqkv L1_attn_Wproj L1_attn_bproj L1_xattn_Wq L1_xattn_bq
L1_xattn_Wk L1_xattn_bk L1_xattn_Wv L1_xattn_bv L1_xattn_Wo L1_xattn_bo L1_ffn_Wr L1_ffn_br L1_ffn_W1 L1_ffn_b1
L1_ffn_W2 L1_ffn_b2""".split()


def kernel(**inputs):
    import concourse.bacc as bacc
    from concourse.bass_utils import run_bass_kernel_spmd

    nc = bacc.Bacc("TRN2", target_bir_lowering=False, num_devices=1)
    arrays, aps = {}, {}
    for name in NAMES + ["shape_constants"]:
        v = shape_constants() if name == "shape_constants" else np.ascontiguousarray(inputs[name])
        arrays[f"in_{name}"] = v
        aps[name] = nc.dram_tensor(f"in_{name}", v.shape, mybir.dt.from_np(v.dtype), kind="ExternalInput").ap()
    out = nc.dram_tensor("out_x", (BATCH, S, D), F32, kind="ExternalOutput").ap()
    build(nc, aps, out)
    result = run_bass_kernel_spmd(nc, [arrays], core_ids=[0])
    return result.results[0]["out_x"]
```

```python
from contextlib import ExitStack

import numpy as np

import concourse.bass as bass
from concourse import mybir

F32 = mybir.dt.float32
BF16 = mybir.dt.bfloat16
U8 = mybir.dt.uint8
U32 = mybir.dt.uint32
ALU = mybir.AluOpType
ACT = mybir.ActivationFunctionType
AX = mybir.AxisListType

P = 128
BATCH, S, D = 32, 64, 128
GB = 8
NG = BATCH // GB
T = GB * S
NP = T // P
TH = T // 2
GH, NH = GB // 2, NP // 2
HEADS = 16
HP = HEADS // 2
DI = 2 * D
NC = DI // P
N = 16
E = 8
F0 = 256
F1 = 512
C0, C1 = F0 // P, F1 // P
HD = D // HEADS
LN_EPS = 1e-5
NEG = -float(np.finfo(np.float32).max)
FAR = 1e28

K_IDENT = 0
K_CAUSAL = K_IDENT + P
K_CAUSAL9 = K_CAUSAL + S
K_COS = K_CAUSAL9 + S
K_SIN = K_COS + S
K_HEAD = K_SIN + S
K_SEL = K_HEAD + HEADS
K_IOTA = K_SEL + 2 * N
K_HALF = K_IOTA + E
K_ALL = K_HALF + NP


def shape_constants():
    k = np.zeros((P, K_ALL), np.float32)
    k[:, K_IDENT:K_CAUSAL] = np.eye(P)
    i = (np.arange(P) % S)[:, None]
    j = np.arange(S)[None, :]
    k[:, K_CAUSAL:K_CAUSAL9] = np.where(j > i, np.float32(NEG), np.float32(0))
    k[:, K_CAUSAL9:K_COS] = np.where(j > i, np.float32(-1e9), np.float32(0))
    inv = (np.float32(1) / np.float32(10000) ** (np.arange(0, HD, 2, dtype=np.float32) / np.float32(HD)))
    freq = (np.arange(S, dtype=np.float32)[:, None] * inv[None, :]).astype(np.float32)
    d = np.arange(P) % HD
    k[:, K_COS:K_SIN] = np.cos(freq)[:, d // 2].T
    k[:, K_SIN:K_HEAD] = np.sin(freq)[:, d // 2].T * np.where(d % 2 == 0, -1, 1)[:, None]
    k[:, K_HEAD:K_SEL] = np.arange(P)[:, None] // HD == np.arange(HEADS)[None, :]
    k[:, K_SEL:K_IOTA] = np.arange(P)[:, None] % (2 * N) == np.arange(2 * N)[None, :]
    k[:, K_IOTA:K_HALF] = np.arange(E)
    k[:, K_HALF:] = -0.5
    return k


class Signal:

    def __init__(self, sem, per_group):
        self.sem, self.per_group = sem, per_group

    def at(self, g, k):
        return g * self.per_group + k


def wait_alone(eng, ready, sem, value):
    value = eng.to_reg(value)
    eng.wait_ge(ready.sem, 1)
    eng.wait_ge(sem, value)


MAMBA_LINKS = 11
LAYER_LINKS = 44


def build(nc, a, out):
    with ExitStack() as ctx:
        def sb(name, shape, dt=F32):
            return ctx.enter_context(nc.sbuf_tensor(name, shape, dt))

        def signal(name, per_group=1):
            return Signal(ctx.enter_context(nc.semaphore(name)), per_group)

        ctx.enter_context(nc.allow_non_contiguous_dma(reason="per-feature vectors"))

        kc = sb("kc", [P, K_ALL])
        ident = kc[:, K_IDENT:K_CAUSAL]
        w_in = sb("w_in", [P, 2 * DI])
        w_conv = sb("w_conv", [P, NC, 3])
        b_conv = sb("b_conv", [P, NC])
        w_xd = sb("w_xd", [P, NC, DI])
        w_xbc = sb("w_xbc", [P, NC, 3, 2 * N])
        w_dt = sb("w_dt", [P, NC, DI])
        b_dt = sb("b_dt", [P, NC])
        w_out = sb("w_out", [P, NC, D])
        a_neg = sb("a_neg", [P, NC, N])
        d_par = sb("d_par", [P, NC])
        sel = sb("sel", [96, 2 * N], BF16)
        w_q0 = sb("w_q0", [P, HP * P])
        w_kv0 = sb("w_kv0", [P, 2 * HP * P])
        w_o0 = sb("w_o0", [P, HP, D])
        bo0 = sb("bo0", [P, D])
        w_r0 = sb("w_r0", [P, E])
        w_gu = sb("w_gu", [P, E, 2 * F0])
        w_dn = sb("w_dn", [P, E, C0, D])
        w_qkv1 = sb("w_qkv1", [P, 3 * D])
        w_sw1 = sb("w_sw1", [P, 2 * D])
        b_qk1 = sb("b_qk1", [P, 2])
        b_sw1 = sb("b_sw1", [P, 2])
        bv1 = sb("bv1", [P, D])
        w_p1 = sb("w_p1", [P, D])
        bo1 = sb("bo1", [P, D])
        w_qkvx = sb("w_qkvx", [P, 3 * D])
        b_qkx = sb("b_qkx", [P, 2])
        bvx = sb("bvx", [P, D])
        w_px = sb("w_px", [P, D])
        box = sb("box", [P, D])
        w_r1 = sb("w_r1", [P, E])
        br1 = sb("br1", [P, E])
        w_1 = sb("w_1", [P, E, F1])
        b_1 = sb("b_1", [P, E, C1])
        w_2 = sb("w_2", [P, E, C1, D])
        b_2 = sb("b_2", [P, NP, D])

        x_in = sb("x_in", [P, NP, D])
        x_keep = sb("x_keep", [P, NP, D])
        x_mix = sb("x_mix", [P, NP, D])
        x_res = sb("x_res", [P, NP, D])
        ctx_in = sb("ctx_in", [P, NP, D])
        mask_in = sb("mask_in", [P, T], U8)
        stats = [sb(f"stats{i}", [P, NP, 6]) for i in range(2)]
        mean_var = [sb(f"mean_var{i}", [P, NP, 2]) for i in range(2)]
        var_eps = [sb(f"var_eps{i}", [P, NP]) for i in range(2)]
        rstd = [sb(f"rstd{i}", [P, NP]) for i in range(2)]
        xn = [sb(f"xn{i}", [P, NP, D]) for i in range(2)]
        xT0, xT = sb("xT0", [P, T]), sb("xT", [P, T])
        ctxT = sb("ctxT", [P, T])
        bias0 = sb("bias0", [P, T])
        q1, kT1 = sb("q1", [P, T]), bias0
        V1 = sb("V1", [P, GB, HP, 2, HD + 1])
        scores = sb("scores", [P, 3, 2 * T])
        row_max = sb("row_max", [P, 3, HP * 2])
        row_sum = sb("row_sum", [P, 3, HP * 2])
        probsT = sb("probsT", [P, 2, HP, P])
        O1 = sb("O1", [P, 2, D])
        O1T = sb("O1T", [P, T])
        logits = sb("logits", [P, NP, E])
        top = sb("top", [P, NP, 8])
        top_at = sb("top_at", [P, NP, 8], U32)
        top_atf = sb("top_atf", [P, NP, 2])
        top_e = sb("top_e", [P, NP])
        top_w = sb("top_w", [P, NP, 2])
        pick = sb("pick", [P, NP, 2, E])
        gate = sb("gate", [P, NP, 32])
        gateT = sb("gateT", [P, P])
        gate_act, delta, du, y_sum = (sb(n, [P, NC, T]) for n in ("gate_act", "delta", "du", "y_sum"))
        bc_split = sb("bc_split", [96, T], BF16)

        region = sb("region", [P, 22 * T])

        def view(at, size, pattern, **kw):
            return region[:, at * T:(at + size) * T].rearrange(pattern, **kw)

        QT, KT = (view(8 * i, 8, "p (x h t) -> p x h t", x=2, h=HP) for i in range(2))
        V0 = [view(at, 4, "p (t f) -> p t f", t=NH) for at in (16, 0)]
        Kx = [view(8 * x, 8, "p (b h j) -> p b h j", b=GH, h=HEADS) for x in range(2)]
        u_act = view(20, 2, "p (c t) -> p c t", c=NC)
        hidden = view(8, 8, "p (s c t) -> p s c t", s=2, c=4)
        gated, up_copy = hidden[:, :, 2, :], hidden[:, :, 3, :]
        decay = view(16, 3, "p (r t) -> p r t", r=3)
        state = view(19, 3, "p (r t) -> p r t", r=3)
        weighed, c_copy = view(8, 4, "p (r t) -> p r t", r=4), view(12, 2, "p (r t) -> p r t", r=2)
        u_conv, d_raw, dt_z, dt_e = y_sum, du, delta, du
        bc_res, bc_mid = O1T[0:96, :], O1[0:96].rearrange("p s f -> p (s f)").bitcast(BF16)

        ps = ctx.enter_context(nc.psum_tensor("ps", [P, 8, 512], F32))

        weights = {n: signal(f"w_{n}_loaded") for n in ("mamba", "attn0", "moe0", "attn1", "attnx", "moe1")}
        need = {}
        x_loaded, ctx_loaded, mask_loaded = signal("x_loaded", 16), signal("ctx_loaded", 16), signal("mask_loaded", 16)
        x_stored = signal("x_stored", 16)
        mask_free, out_free = signal("mask_free"), signal("out_free")
        setup, a_exp, zeros_set, swapped_set = signal("setup"), signal("a_exp"), signal("zeros_set"), signal("swapped_set")
        var_ready, rstd_ready, xn_ready, xnT_done, xT_ready = (
            [signal(f"{n}{i}", (1, 5)[i]) for i in range(2)] for n in ("var_ready", "rstd_ready", "xn_ready", "xnT_done", "xT_ready"))
        ctxT_done, ctxT_ready = signal("ctxT_done"), signal("ctxT_ready")
        biased = signal("biased", 3)
        x_kept, x_mixed = signal("x_kept"), signal("x_mixed")
        inproj_done, conv_mid, conv_done, u_ready = signal("inproj_done", 4), signal("conv_mid", 2), signal("conv_done", 2), signal("u_ready", 2)
        gate_ready = signal("gate_ready", 2)
        xproj_done, draw_ready, split_ready = signal("xproj_done", 3), signal("draw_ready", 2), signal("split_ready")
        dt_done, z_ready, nz_ready, e_ready = signal("dt_done", 2), signal("z_ready", 2), signal("nz_ready"), signal("e_ready")
        ln_ready, delta_ready = signal("ln_ready"), signal("delta_ready")
        bc_spread, decay_ready = signal("bc_spread", N), signal("decay_ready", NC * N)
        bu_done, scan_done, hc_done, y_added = (signal(n, NC * N) for n in ("bu_done", "scan_done", "hc_done", "y_added"))
        c_copied = signal("c_copied", N)
        y0_ready = signal("y0_ready")
        yg_ready, mamba_done = signal("yg_ready"), signal("mamba_done")
        q0_done, k0_done, k0_ready = (signal(n, HP) for n in ("q0_done", "k0_done", "k0_ready"))
        q0_ready = [signal(f"q0_ready{x}", HP // 2) for x in range(2)]
        v0_done, v0_ready = signal("v0_done", NP), signal("v0_ready", NP)
        s_done, s_read, exp_done, pT_done, pT_ready, o_done = (
            signal(n, 3 * NP) for n in ("s_done", "s_read", "exp_done", "pT_done", "pT_ready", "o_done"))
        shifted0, sum_ready, normed, o0_ready = (signal(n, NP) for n in ("shifted0", "sum_ready", "normed", "o0_ready"))
        max_ready, shifted1, o1_ready, o1T_done = (
            signal(n, 2 * NP) for n in ("max_ready", "shifted1", "o1_ready", "o1T_done"))
        o1T_ready = signal("o1T_ready", 4)
        attn_done = signal("attn_done", 3)
        qk1_done, v1_done = signal("qk1_done", 6), signal("v1_done", 2)
        q1_rot, q1_lin, k1_rot, k1_lin = signal("q1_rot"), signal("q1_lin"), signal("k1_rot"), signal("k1_lin")
        v1_ready = signal("v1_ready", 2)
        kx_dve, kx_act, kx_pool = signal("kx_dve", 2), signal("kx_act", 4), signal("kx_pool", 4)
        route_done, top_ready, tope_ready, gate_w = signal("route_done", 2), signal("top_ready", 2), signal("tope_ready", 2), signal("gate_w", 2)
        gu_done, tanh_done, up_copied, gated_done, h0_done = (
            signal(n, C0 * e) for n, e in (("gu_done", E), ("tanh_done", E), ("up_copied", E - 1), ("gated_done", E), ("h0_done", E - 1)))
        h0_last = signal("h0_last", C0)
        up_done, h1_act, h1_dve = signal("up_done", C1 * E), signal("h1_act", C1 * E // 2), signal("h1_dve", C1 * E // 2)
        down_done, acc_done = signal("down_done", 2 * E), signal("acc_done", 2 * E)
        gateT_done, gateT_ready, b2_done, b2_added = (signal(n) for n in ("gateT_done", "gateT_ready", "b2_done", "b2_added"))
        mamba_chain, layer_chain = signal("mamba_chain", MAMBA_LINKS), signal("layer_chain", LAYER_LINKS)

        block = ctx.enter_context(nc.Block())

        @block.sync
        def _(sp):
            def load(group, dst, src):
                sp.dma_start(dst, src).then_inc(weights[group].sem, 16)
                need[group] = need.get(group, 0) + 16

            def column(name, n):
                return a[name].rearrange("(c p) -> p c", p=n)

            def row(name):
                return a[name].partition_broadcast(P)

            def load_x(g):
                sp.dma_start(x_in[:], pairs_of(a["x"], g)).then_inc(x_loaded.sem, 16)

            def load_ctx(g):
                sp.dma_start(ctx_in[:], pairs_of(a["ctx_1024"], g)).then_inc(ctx_loaded.sem, 16)

            def load_mask(g):
                src = a["mask_BxS2_bk0"].rearrange("b s -> (b s)")[bass.ds(g * T, T)]
                sp.dma_start(mask_in[:], src.partition_broadcast(P)).then_inc(mask_loaded.sem, 16)

            def store_x(g):
                sp.wait_ge(acc_done.sem, acc_done.at(g, 2 * E))
                sp.dma_start(pairs_of(out, g), x_res[:]).then_inc(x_stored.sem, 16)
                sp.wait_ge(x_stored.sem, x_stored.at(g, 16))
                sp.nop().then_inc(out_free.sem, 1)

            sp.nop().then_inc(out_free.sem, 1)
            load_x(0)
            load("mamba", kc[:], a["shape_constants"])
            load("mamba", w_in[:], a["L0_attn_in_proj_w"])
            load("mamba", w_conv[:], a["L0_attn_conv_w"].rearrange("(c p) a k -> p c (a k)", p=P))
            load("mamba", b_conv[:], column("L0_attn_conv_b", P))
            xp = a["L0_attn_x_proj_w"].rearrange("(c p) n -> p c n", p=P)
            load("mamba", w_xd[:], xp[:, :, 0:DI])
            for k in range(3):
                load("mamba", w_xbc[:, :, k, :], xp[:, :, DI:])
            load("mamba", w_dt[:], a["L0_attn_dt_proj_w"].rearrange("(c p) n -> p c n", p=P))
            load("mamba", b_dt[:], column("L0_attn_dt_proj_b", P))
            load("mamba", a_neg[:], a["L0_attn_A_log"].rearrange("(c p) n -> p c n", p=P))
            load("mamba", d_par[:], column("L0_attn_D_param", P))
            load("mamba", w_out[:], a["L0_attn_out_proj_w"].rearrange("(c p) n -> p c n", p=P))
            load_ctx(0)
            load_mask(0)
            load("attn0", w_q0[:], a["L0_xattn_Wq"])
            load("attn0", w_kv0[:], a["L0_xattn_Wkv"])
            load("attn0", w_o0[:], a["L0_xattn_Wo"].rearrange("(c p) n -> p c n", p=P))
            load("attn0", bo0[:], row("L0_xattn_bo"))
            load("moe0", w_r0[:], a["L0_ffn_gate_w"])
            load("moe0", w_gu[:], a["L0_ffn_gate_up_w"].rearrange("e p f -> p e f"))
            load("moe0", w_dn[:], a["L0_ffn_down_w"].rearrange("e (c p) n -> p e c n", p=P))
            load("attn1", w_qkv1[:], a["L1_attn_Wqkv"])
            bqkv = a["L1_attn_bqkv"]
            load("attn1", b_qk1[:], bqkv[0:2 * D].rearrange("(c p) -> p c", p=P))
            load("attn1", bv1[:], bqkv[2 * D:3 * D].partition_broadcast(P))
            for odd in range(2):
                src = bqkv[0:2 * D].rearrange("(c k two) -> two k c", c=2, two=2)[1 - odd]
                load("attn1", b_sw1[odd:P:2, :], src)
            load("attn1", w_p1[:], a["L1_attn_Wproj"])
            load("attn1", bo1[:], row("L1_attn_bproj"))
            for i, n in enumerate("qkv"):
                load("attnx", w_qkvx[:, i * D:(i + 1) * D], a[f"L1_xattn_W{n}"])
            load("attnx", w_px[:], a["L1_xattn_Wo"])
            load("attnx", b_qkx[:, 0:1], column("L1_xattn_bq", P))
            load("attnx", b_qkx[:, 1:2], column("L1_xattn_bk", P))
            load("attnx", bvx[:], row("L1_xattn_bv"))
            load("attnx", box[:], row("L1_xattn_bo"))
            load("moe1", w_r1[:], a["L1_ffn_Wr"])
            load("moe1", br1[:], row("L1_ffn_br"))
            load("moe1", w_1[:], a["L1_ffn_W1"].rearrange("e p f -> p e f"))
            load("moe1", b_1[:], a["L1_ffn_b1"].rearrange("e (c p) -> p e c", p=P))
            load("moe1", w_2[:], a["L1_ffn_W2"].rearrange("e (c p) n -> p e c n", p=P))
            sp.wait_ge(zeros_set.sem, 1)
            for t in range(NP):
                load("moe1", b_2[32 * t:32 * t + E, t, :], a["L1_ffn_b2"])
            def load_next(g):
                sp.wait_ge(ctxT_done.sem, ctxT_done.at(g, 1))
                load_ctx(g + 1)
                wait_alone(sp, zeros_set, mask_free.sem, mask_free.at(g, 1))
                load_mask(g + 1)

            def load_x_after(g):
                wait_alone(sp, zeros_set, x_kept.sem, x_kept.at(g, 1))
                wait_alone(sp, zeros_set, xn_ready[0].sem, xn_ready[0].at(g, 1))
                load_x(g + 1)

            load_x_after(0)
            with sp.Fori(0, NG - 2) as g:
                load_next(g)
                load_x_after(g + 1)
                store_x(g)
            load_next(NG - 2)
            store_x(NG - 2)
            store_x(NG - 1)

        @block.tensor
        def _(pe):
            def mm(out_ap, lhsT, rhs, start=True, stop=True):
                return pe.matmul(out_ap, lhsT, rhs, start=start, stop=stop)

            def turn_norm(g, l):
                i, bank = min(l, 1), 6 if l == 1 else 4
                pe.wait_ge(xn_ready[i].sem, xn_ready[i].at(g, max(l, 1)))
                for t in range(NP):
                    ins = pe.transpose(ps[:, bank, t * P:(t + 1) * P], xn[i][:, t, :], ident)
                ins.then_inc(xnT_done[i].sem, 1)

            def in_proj(g):
                pe.wait_ge(xT_ready[0].sem, xT_ready[0].at(g, 1))
                for m in range(2 * NC):
                    mm(ps[:, 4 + m, :], w_in[:, m * P:(m + 1) * P], xT0[:]).then_inc(inproj_done.sem, 1)

            def x_proj(g):
                pe.wait_ge(u_ready.sem, u_ready.at(g, 2))
                for c in range(NC):
                    ins = mm(ps[0:96, 6, :], w_xbc[:, c, :, :], u_act[:, c, :], c == 0, c == NC - 1)
                ins.then_inc(xproj_done.sem, 1)
                for m in range(NC):
                    for c in range(NC):
                        ins = mm(ps[:, 4 + m, :], w_xd[:, c, m * P:(m + 1) * P], u_act[:, c, :], c == 0, c == NC - 1)
                    ins.then_inc(xproj_done.sem, 1)

            def dt_proj(g):
                pe.wait_ge(draw_ready.sem, draw_ready.at(g, 2))
                pe.wait_ge(split_ready.sem, split_ready.at(g, 1))
                for m in range(NC):
                    for c in range(NC):
                        ins = mm(ps[:, 6 + m, :], w_dt[:, c, m * P:(m + 1) * P], d_raw[:, c, :], c == 0, c == NC - 1)
                    ins.then_inc(dt_done.sem, 1)

            def spread_bc(g, n, ring):
                if ring == 1 and n >= 1:
                    pe.wait_ge(hc_done.sem, hc_done.at(g, NC * n))
                if ring == 2 and n >= 2:
                    pe.wait_ge(bu_done.sem, bu_done.at(g, NC * (n - 1)))
                    pe.wait_ge(c_copied.sem, c_copied.at(g, n - 1))
                b_bank, c_bank = bc_banks(n, ring)
                mm(ps[:, b_bank, :], sel[:, n:n + 1].to_broadcast([96, P]), bc_split[:])
                mm(ps[:, c_bank, :], sel[:, N + n:N + n + 1].to_broadcast([96, P]), bc_split[:]).then_inc(bc_spread.sem, 1)

            def mamba_out(g):
                pe.wait_ge(yg_ready.sem, yg_ready.at(g, 1))
                for t in range(NP):
                    for c in range(NC):
                        ins = mm(ps[:, 6, t * P:(t + 1) * P], y_sum[:, c, t * P:(t + 1) * P], w_out[:, c, :], c == 0, c == NC - 1)
                ins.then_inc(mamba_done.sem, 1)

            def turn_ctx(g):
                pe.wait_ge(ctx_loaded.sem, ctx_loaded.at(g, 16))
                for t in range(NP):
                    ins = pe.transpose(ps[:, 7, t * P:(t + 1) * P], ctx_in[:, t, :], ident)
                ins.then_inc(ctxT_done.sem, 1)

            def keys0(g, x, units):
                for u in units:
                    if x == 0 and u == 0:
                        pe.wait_ge(ctxT_ready.sem, ctxT_ready.at(g, 1))
                    if x == 1:
                        pe.wait_ge(q0_ready[1].sem, q0_ready[1].at(g, u + 1))
                    for h in range(2):
                        hp = 2 * u + h
                        ins = mm(ps[:, u, h * TH:(h + 1) * TH], w_kv0[:, hp * P:(hp + 1) * P], ctxT[:, x * TH:(x + 1) * TH])
                    ins.then_inc(k0_done.sem, 1)

            def queries0(g, x):
                if x == 0:
                    pe.wait_ge(xT_ready[1].sem, xT_ready[1].at(g, 1))
                for u in range(4):
                    if x == 0:
                        pe.wait_ge(k0_ready.sem, k0_ready.at(g, u + 1))
                    elif u % 2 == 0:
                        pe.wait_ge(s_read.sem, s_read.at(g, u // 2 + 1))
                    for h in range(2):
                        hp = 2 * u + h
                        ins = mm(ps[:, u, h * TH:(h + 1) * TH], w_q0[:, hp * P:(hp + 1) * P], xT[:, x * TH:(x + 1) * TH])
                    ins.then_inc(q0_done.sem, 1)

            def values0(g, p):
                q = 2 * (p % 2)
                if p < 2:
                    pe.wait_ge(q0_ready[0].sem, q0_ready[0].at(g, q + 2))
                else:
                    pe.wait_ge(k0_ready.sem, k0_ready.at(g, 4 + q + 2))
                for half in range(2):
                    cols = w_kv0[:, HP * P + half * 512:HP * P + (half + 1) * 512]
                    ins = mm(ps[:, q + half, :], ctxT[:, p * P:(p + 1) * P], cols)
                ins.then_inc(v0_done.sem, 1)

            def scores_of(g, k, p):
                if k == 0:
                    x = p // 2
                    wait_alone(pe, weights["attn0"], v0_ready.sem, v0_ready.at(g, p + 1))
                    wait_alone(pe, weights["attn0"], q0_ready[x].sem, q0_ready[x].at(g, HP // 2))
                    wait_alone(pe, weights["attn0"], k0_ready.sem, k0_ready.at(g, 4 * (x + 1)))
                else:
                    if p % 2 == 0:
                        pe.wait_ge(kx_pool.sem, kx_pool.at(g, 2 * (k - 1) + p // 2 + 1))
                        pe.wait_ge(kx_act.sem, kx_act.at(g, 2 * (k - 1) + p // 2 + 1))
                    if p == 0:
                        pe.wait_ge(kx_dve.sem, kx_dve.at(g, k))
                        q1_ready = q1_rot if k == 1 else q1_lin
                        pe.wait_ge(q1_ready.sem, q1_ready.at(g, 1))
                    if p >= 2:
                        pe.wait_ge(s_read.sem, s_read.at(g, k * NP + p - 1))
                bank = 2 * (p % 2)
                s_ps = ps[:, bank:bank + 2, :].rearrange("p k f -> p (k f)")
                for s2 in range(2):
                    b = 2 * (p % 2) + s2
                    if k == 0:
                        for h in range(HP):
                            at = (2 * h + s2) * S
                            for e in range(2):
                                r = slice(e * S, (e + 1) * S)
                                ins = mm(s_ps[r, at:at + S], QT[r, x, h, b * S:(b + 1) * S], KT[r, x, h, b * S:(b + 1) * S])
                    else:
                        for x in range(2):
                            ins = mm(ps[s2 * S:(s2 + 1) * S, bank + x, :], q1[:, (2 * p + s2) * S:(2 * p + s2 + 1) * S],
                                     Kx[p // 2][:, b, x * HP:(x + 1) * HP, :].rearrange("p h j -> p (h j)"))
                ins.then_inc(s_done.sem, 1)

            def turn_probs(g, k, p):
                if k == 0:
                    pe.wait_ge(normed.sem, normed.at(g, p + 1))
                else:
                    if p == 0:
                        pe.wait_ge(v1_ready.sem, v1_ready.at(g, k))
                    pe.wait_ge(exp_done.sem, exp_done.at(g, k * NP + p + 1))
                bank = probs_bank(k, p)
                if p >= 1 and bank == 4:
                    pe.wait_ge(pT_ready.sem, pT_ready.at(g, k * NP + p))
                for h in range(HP):
                    at = h * P
                    ins = pe.transpose(ps[:, bank + h // 4, (h % 4) * P:(h % 4 + 1) * P], scores[:, p % 3, at:at + P], ident)
                ins.then_inc(pT_done.sem, 1)

            def weigh_values0(g, p):
                if p >= 1:
                    wait_alone(pe, weights["attn0"], o0_ready.sem, o0_ready.at(g, p))
                wait_alone(pe, weights["attn0"], pT_ready.sem, pT_ready.at(g, p + 1))
                for h in range(HP):
                    for e in range(2):
                        for s2 in range(2):
                            r = slice(s2 * S, s2 * S + S)
                            ins = mm(ps[e * S:(e + 1) * S, 6 + s2, h * S:(h + 1) * S],
                                     V0[p // 2][r, p % 2, h * P + e * S:h * P + (e + 1) * S],
                                     probsT[r, p % 2, h, e * S:(e + 1) * S])
                ins.then_inc(o_done.sem, 1)

            def attn0_out(g, t):
                if t == 0:
                    pe.wait_ge(s_read.sem, s_read.at(g, 3))
                pe.wait_ge(o0_ready.sem, o0_ready.at(g, t + 1))
                at = (t % 2) * P
                for h in range(HP):
                    ins = mm(ps[:, 0, t * P:(t + 1) * P], KT[:, t // 2, h, at:at + P], w_o0[:, h, :], h == 0, h == HP - 1)
                if t == NP - 1:
                    ins.then_inc(attn_done.sem, 1)

            def attention0(g, nxt):
                keys0(g, 0, range(4))
                turn_norm(g, 1)
                queries0(g, 0)
                if nxt is not None:
                    turn_norm(nxt, 0)
                    in_proj(nxt)
                values0(g, 0)
                values0(g, 1)
                scores_of(g, 0, 0)
                if nxt is not None:
                    x_proj(nxt)
                scores_of(g, 0, 1)
                queries0(g, 1)
                if nxt is not None:
                    dt_proj(nxt)
                turn_probs(g, 0, 0)
                if nxt is not None:
                    pe.wait_ge(z_ready.sem, z_ready.at(nxt, 2))
                keys0(g, 1, (0, 1))
                weigh_values0(g, 0)
                keys0(g, 1, (2, 3))
                values0(g, 2)
                turn_probs(g, 0, 1)
                values0(g, 3)
                scores_of(g, 0, 2)
                weigh_values0(g, 1)
                scores_of(g, 0, 3)
                turn_probs(g, 0, 2)
                attn0_out(g, 0)
                weigh_values0(g, 2)
                attn0_out(g, 1)
                turn_probs(g, 0, 3)
                attn0_out(g, 2)
                weigh_values0(g, 3)
                attn0_out(g, 3)

            def project1(g):
                turn_norm(g, 3)
                pe.wait_ge(xT_ready[1].sem, xT_ready[1].at(g, 3))
                for c in (1, 0):
                    mm(ps[:, 2 * c, :], w_qkv1[:, c * D:(c + 1) * D], xT[:]).then_inc(qk1_done.sem, 1)
                    mm(ps[:, 2 * c + 1, :], w_sw1[:, c * D:(c + 1) * D], xT[:]).then_inc(qk1_done.sem, 1)
                values1(xT, w_qkv1)

            def values1(src, w):
                w_v = w[:, 2 * D:].rearrange("p (h e d) -> p e h d", e=2, d=HD)
                for b in range(GB):
                    for e in range(2):
                        ins = mm(ps[e * S:(e + 1) * S, 5, b * S:(b + 1) * S], src[:, b * S:(b + 1) * S], w_v[:, e])
                ins.then_inc(v1_done.sem, 1)

            def keys_x(g):
                pe.wait_ge(pT_ready.sem, pT_ready.at(g, NP + 2))
                mm(ps[:, 5, :], w_qkvx[:, D:2 * D], ctxT[:]).then_inc(qk1_done.sem, 1)

            def queries_x(g):
                pe.wait_ge(k1_lin.sem, k1_lin.at(g, 1))
                values1(ctxT, w_qkvx)
                turn_norm(g, 4)
                pe.wait_ge(xT_ready[1].sem, xT_ready[1].at(g, 4))
                mm(ps[:, 0, :], w_qkvx[:, 0:D], xT[:]).then_inc(qk1_done.sem, 1)

            def weigh_values1(g, k, p):
                pe.wait_ge(pT_ready.sem, pT_ready.at(g, k * NP + p + 1))
                if p >= 2:
                    pe.wait_ge(o1_ready.sem, o1_ready.at(g, (k - 1) * NP + p - 1))
                for h in range(HP):
                    for s2 in range(2):
                        f = 2 * (HD + 1)
                        ins = mm(ps[s2 * S:(s2 + 1) * S, 6 + p % 2, h * f:(h + 1) * f], probsT[:, p % 2, h, s2 * S:(s2 + 1) * S],
                                 V1[:, 2 * p + s2, h].rearrange("p e f -> p (e f)"))
                ins.then_inc(o_done.sem, 1)

            def turn_o1(g, k, p):
                pe.wait_ge(o1_ready.sem, o1_ready.at(g, (k - 1) * NP + p + 1))
                if p == 0:
                    pe.wait_ge(pT_ready.sem, pT_ready.at(g, k * NP + 2))
                if p == NP - 1 and k == 1:
                    pe.wait_ge(k1_lin.sem, k1_lin.at(g, 1))
                at = p * P if p < NP - 1 else 0
                pe.transpose(ps[:, 4 + p // (NP - 1), at:at + P], O1[:, p % 2], ident).then_inc(o1T_done.sem, 1)

            def attn1_out(g, k, w_p, tiles):
                pe.wait_ge(o1T_ready.sem, o1T_ready.at(g, 2 * (k - 1) + (1 if NP - 1 not in tiles else 2)))
                for t in tiles:
                    ins = mm(ps[:, 0, t * P:(t + 1) * P], O1T[:, t * P:(t + 1) * P], w_p[:])
                if NP - 1 in tiles:
                    ins.then_inc(attn_done.sem, 1)

            def attention1(g, k, w_p, nxt):
                for p in range(3):
                    scores_of(g, k, p)
                turn_probs(g, k, 0)
                scores_of(g, k, 3)
                turn_probs(g, k, 1)
                if nxt is not None:
                    pe.wait_ge(hc_done.sem, hc_done.at(nxt, NC * (STEP_AT_NORM[2 + k] + 1)))
                weigh_values1(g, k, 0)
                for p in (1, 2):
                    turn_probs(g, k, p + 1)
                    weigh_values1(g, k, p)
                    if k == 1 and p == 1:
                        keys_x(g)
                    turn_o1(g, k, p - 1)
                weigh_values1(g, k, 3)
                turn_o1(g, k, 2)
                turn_o1(g, k, 3)
                attn1_out(g, k, w_p, range(NP - 1))
                attn1_out(g, k, w_p, (NP - 1,))

            def route(g, m, w_r):
                for t in range(NP):
                    ins = mm(ps[:, 5, t * E:(t + 1) * E], xT[:, t * P:(t + 1) * P], w_r[:])
                ins.then_inc(route_done.sem, 1)

            def down(g, m, e, chunks, w):
                if m == 0 and e == E - 1:
                    pe.wait_ge(h0_last.sem, h0_last.at(g, C0))
                elif m == 0:
                    pe.wait_ge(h0_done.sem, h0_done.at(g, C0 * (e + 1)))
                else:
                    pe.wait_ge(h1_act.sem, h1_act.at(g, (e + 1) * C1 // 2))
                    pe.wait_ge(h1_dve.sem, h1_dve.at(g, (e + 1) * C1 // 2))
                if e >= 2:
                    pe.wait_ge(acc_done.sem, acc_done.at(g, m * E + e - 1))
                elif e == 1 and m == 0:
                    pe.wait_ge(top_ready.sem, top_ready.at(g, 1))
                elif e == 1:
                    pe.wait_ge(b2_added.sem, b2_added.at(g, 1))
                for t in range(NP):
                    for c in range(chunks):
                        ins = mm(ps[:, 4 + e % 2, t * P:(t + 1) * P], hidden[:, e % 2, c, t * P:(t + 1) * P], w[:, e, c, :], c == 0, c == chunks - 1)
                ins.then_inc(down_done.sem, 1)

            def experts0(g, nxt):
                turn_norm(g, 2)
                pe.wait_ge(xT_ready[1].sem, xT_ready[1].at(g, 2))
                for e in range(E + 1):
                    for c in range(C0 if e < E else 0):
                        k = e * C0 + c
                        if k >= 2:
                            pe.wait_ge(gated_done.sem, gated_done.at(g, k - 1))
                            pe.wait_ge(up_copied.sem, up_copied.at(g, k - 1))
                        q = 2 * (k % 2)
                        mm(ps[:, q, :], w_gu[:, e, c * P:(c + 1) * P], xT[:])
                        mm(ps[:, q + 1, :], w_gu[:, e, F0 + c * P:F0 + (c + 1) * P], xT[:]).then_inc(gu_done.sem, 1)
                    if e == 0:
                        route(g, 0, w_r0)
                    if e >= 1:
                        down(g, 0, e - 1, C0, w_dn)
                    if 1 <= e <= STEPS_MOE[0] and nxt is not None:
                        spread_bc(nxt, step_in_moe(0, e), 1)

            def experts1(g, nxt):
                turn_norm(g, 5)
                pe.wait_ge(xT_ready[1].sem, xT_ready[1].at(g, 5))
                for e in range(E + 1):
                    for c in range(C1 if e < E else 0):
                        k = e * C1 + c
                        if k >= 4:
                            by = h1_act if k % 2 == 0 else h1_dve
                            pe.wait_ge(by.sem, by.at(g, (k - 4) // 2 + 1))
                        mm(ps[:, k % 4, :], w_1[:, e, c * P:(c + 1) * P], xT[:]).then_inc(up_done.sem, 1)
                    if 1 <= e <= STEPS_MOE[1] and nxt is not None:
                        spread_bc(nxt, step_in_moe(1, e), 1)
                    if e == 0:
                        route(g, 1, w_r1)
                    if e == 1:
                        pe.wait_ge(gate_w.sem, gate_w.at(g, 2))
                        pe.transpose(ps[:, 4, 0:P], gate.rearrange("p t e -> p (t e)"), ident).then_inc(gateT_done.sem, 1)
                        pe.wait_ge(gateT_ready.sem, gateT_ready.at(g, 1))
                        for t in range(NP):
                            ins = mm(ps[:, 5, t * P:(t + 1) * P], gateT[:], b_2[:, t, :])
                        ins.then_inc(b2_done.sem, 1)
                    if e >= 1:
                        down(g, 1, e - 1, C1, w_2)
                    if e == E and nxt is not None:
                        pe.wait_ge(hc_done.sem, hc_done.at(nxt, NC * N))
                        turn_ctx(nxt)
                        mamba_out(nxt)

            def group(g, nxt):
                pe.wait_ge(weights["attn0"].sem, need["attn0"])
                attention0(g, nxt)
                pe.wait_ge(weights["moe0"].sem, need["moe0"])
                if nxt is not None:
                    spread_bc(nxt, STEP_AT_NORM[2], 1)
                experts0(g, nxt)
                pe.wait_ge(weights["attn1"].sem, need["attn1"])
                pe.wait_ge(swapped_set.sem, 1)
                if nxt is not None:
                    spread_bc(nxt, STEP_AT_NORM[3], 1)
                project1(g)
                pe.wait_ge(weights["attnx"].sem, need["attnx"])
                attention1(g, 1, w_p1, nxt)
                if nxt is not None:
                    spread_bc(nxt, STEP_AT_NORM[4], 1)
                queries_x(g)
                attention1(g, 2, w_px, nxt)
                pe.wait_ge(weights["moe1"].sem, need["moe1"])
                if nxt is not None:
                    spread_bc(nxt, STEP_AT_NORM[5], 1)
                experts1(g, nxt)

            pe.wait_ge(weights["mamba"].sem, need["mamba"])
            turn_norm(0, 0)
            in_proj(0)
            x_proj(0)
            dt_proj(0)
            pe.wait_ge(z_ready.sem, z_ready.at(0, 2))
            spread_bc(0, 0, 2)
            spread_bc(0, 1, 2)
            for n in range(N):
                if n + 2 < N:
                    spread_bc(0, n + 2, 2)
                for c in range(NC):
                    k = NC * n + c
                    pe.wait_ge(hc_done.sem, hc_done.at(0, k + 1))
                    mm(ps[:, c, :], ident, weighed[:, k % 4, :], n == 0, n == N - 1).then_inc(y_added.sem, 1)
            mamba_out(0)
            turn_ctx(0)
            with pe.Fori(0, NG - 1) as g:
                group(g, g + 1)
            group(NG - 1, None)

        @block.scalar
        def _(act):
            def copy_norm(g, l):
                i, bank = min(l, 1), 6 if l == 1 else 4
                act.wait_ge(xnT_done[i].sem, xnT_done[i].at(g, max(l, 1)))
                act.copy((xT0, xT)[i][:], ps[:, bank, :]).then_inc(xT_ready[i].sem, 1)

            def conv_and_gate(g):
                for c in range(NC):
                    act.wait_ge(inproj_done.sem, inproj_done.at(g, c + 1))
                    act.activation(u_conv[:, c, :], ps[:, 4 + c, :], ACT.Identity, bias=b_conv[:, c:c + 1],
                                   scale=w_conv[:, c, 1:2]).then_inc(conv_mid.sem, 1)
                for c in range(NC):
                    act.wait_ge(inproj_done.sem, inproj_done.at(g, NC + c + 1))
                    act.activation(gate_act[:, c, :], ps[:, 6 + c, :], ACT.Silu).then_inc(gate_ready.sem, 1)
                for c in range(NC):
                    act.wait_ge(conv_done.sem, conv_done.at(g, c + 1))
                    act.activation(u_act[:, c, :], u_conv[:, c, :], ACT.Silu).then_inc(u_ready.sem, 1)

            def copy_d(g):
                for c in range(NC):
                    act.wait_ge(xproj_done.sem, xproj_done.at(g, c + 2))
                    act.copy(d_raw[:, c, :], ps[:, 4 + c, :]).then_inc(draw_ready.sem, 1)

            def add_dt_bias(g):
                for c in range(NC):
                    act.wait_ge(dt_done.sem, dt_done.at(g, c + 1))
                    act.activation(dt_z[:, c, :], ps[:, 6 + c, :], ACT.Identity, bias=b_dt[:, c:c + 1]).then_inc(z_ready.sem, 1)

            def softplus_log(g):
                act.wait_ge(nz_ready.sem, nz_ready.at(g, 1))
                act.activation(dt_e[:], dt_e[:], ACT.Exp).then_inc(e_ready.sem, 1)
                act.wait_ge(e_ready.sem, e_ready.at(g, 1))
                act.activation(dt_e[:], dt_e[:], ACT.Ln, bias=1.0).then_inc(ln_ready.sem, 1)

            def decays(g, n):
                if n == 0:
                    act.wait_ge(delta_ready.sem, delta_ready.at(g, 1))
                for c in range(NC):
                    k = NC * n + c
                    if k >= 3:
                        act.wait_ge(scan_done.sem, scan_done.at(g, k - 2))
                    act.activation(decay[:, k % 3, :], delta[:, c, :], ACT.Exp,
                                   scale=a_neg[:, c, n:n + 1]).then_inc(decay_ready.sem, 1)

            def copy_ctx(g):
                act.wait_ge(ctxT_done.sem, ctxT_done.at(g, 1))
                act.copy(ctxT[:], ps[:, 7, :]).then_inc(ctxT_ready.sem, 1)

            def copy_keys0(g, x, units):
                for u in units:
                    act.wait_ge(k0_done.sem, k0_done.at(g, 4 * x + u + 1))
                    act.copy(KT[:, x, 2 * u:2 * u + 2, :].rearrange("p h t -> p (h t)"), ps[:, u, :]).then_inc(k0_ready.sem, 1)

            def copy_queries0(g):
                for u in range(4):
                    act.wait_ge(q0_done.sem, q0_done.at(g, u + 1))
                    act.mul(QT[:, 0, 2 * u:2 * u + 2, :].rearrange("p h t -> p (h t)"), ps[:, u, :], 0.125).then_inc(q0_ready[0].sem, 1)

            def copy_values0(g, p):
                act.wait_ge(v0_done.sem, v0_done.at(g, p + 1))
                q = 2 * (p % 2)
                act.copy(V0[p // 2][:, p % 2, :], ps[:, q:q + 2, :].rearrange("p k f -> p (k f)")).then_inc(v0_ready.sem, 1)

            def exps(g, k, p):
                if k == 0:
                    act.wait_ge(shifted0.sem, shifted0.at(g, p + 1))
                else:
                    act.wait_ge(shifted1.sem, shifted1.at(g, (k - 1) * NP + p + 1))
                act.activation(scores[:, p % 3, :], scores[:, p % 3, :], ACT.Exp).then_inc(exp_done.sem, 1)

            def copy_probs(g, k, p):
                bank = probs_bank(k, p)
                act.wait_ge(pT_done.sem, pT_done.at(g, k * NP + p + 1))
                if p >= 2:
                    act.wait_ge(o_done.sem, o_done.at(g, k * NP + p - 1))
                act.copy(probsT[:, p % 2].rearrange("p h q -> p (h q)"),
                         ps[:, bank:bank + 2, :].rearrange("p k f -> p (k f)")).then_inc(pT_ready.sem, 1)

            def copy_outputs0(g, p):
                act.wait_ge(o_done.sem, o_done.at(g, p + 1))
                at = (p % 2) * P
                act.copy(KT[:, p // 2, :, at:at + P].rearrange("p h (s i) -> p s h i", s=2),
                         ps[:, 6:8, :].rearrange("p s (h i) -> p s h i", h=HP)).then_inc(o0_ready.sem, 1)

            def attention0(g, nxt):
                copy_keys0(g, 0, range(4))
                copy_norm(g, 1)
                copy_queries0(g)
                if nxt is not None:
                    copy_norm(nxt, 0)
                    conv_and_gate(nxt)
                copy_values0(g, 0)
                copy_values0(g, 1)
                exps(g, 0, 0)
                if nxt is not None:
                    copy_d(nxt)
                exps(g, 0, 1)
                if nxt is not None:
                    add_dt_bias(nxt)
                copy_probs(g, 0, 0)
                if nxt is not None:
                    softplus_log(nxt)
                copy_keys0(g, 1, (0, 1))
                copy_keys0(g, 1, (2, 3))
                copy_outputs0(g, 0)
                copy_values0(g, 2)
                copy_probs(g, 0, 1)
                copy_values0(g, 3)
                copy_outputs0(g, 1)
                exps(g, 0, 2)
                copy_probs(g, 0, 2)
                exps(g, 0, 3)
                copy_outputs0(g, 2)
                copy_probs(g, 0, 3)
                copy_outputs0(g, 3)

            def expand(g, k, x):
                if x == 0:
                    k1_ready = k1_rot if k == 1 else k1_lin
                    act.wait_ge(k1_ready.sem, k1_ready.at(g, 1))
                if k == 2:
                    act.wait_ge(s_done.sem, s_done.at(g, k * NP - 2 + 2 * x))
                for h in ACT_HEADS[x]:
                    ins = act.mul(Kx[x][:, :, h, :], kT1[:, x * TH:(x + 1) * TH].rearrange("p (b j) -> p b j", b=GH),
                                  kc[:, K_HEAD + h:K_HEAD + h + 1])
                ins.then_inc(kx_act.sem, 1)

            def copy_o1(g, k):
                first = (NP - 1) * P
                act.wait_ge(o1T_done.sem, o1T_done.at(g, k * NP - 1))
                act.copy(O1T[:, 0:first], ps[:, 4, 0:first]).then_inc(o1T_ready.sem, 1)
                act.wait_ge(o1T_done.sem, o1T_done.at(g, k * NP))
                act.copy(O1T[:, first:T], ps[:, 5, 0:P]).then_inc(o1T_ready.sem, 1)

            def attention1(g, k, nxt):
                if k == 2:
                    expand(g, 2, 0)
                if nxt is not None:
                    decays(nxt, STEP_AT_NORM[2 + k])
                copy_norm(g, 2 + k)
                if k == 1:
                    expand(g, 1, 0)
                    expand(g, 1, 1)
                else:
                    act.wait_ge(qk1_done.sem, qk1_done.at(g, 6))
                    act.activation(q1[:], ps[:, 0, :], ACT.Identity, bias=b_qkx[:, 0:1]).then_inc(q1_lin.sem, 1)
                    expand(g, 2, 1)
                exps(g, k, 0)
                copy_probs(g, k, 0)
                exps(g, k, 1)
                exps(g, k, 2)
                copy_probs(g, k, 1)
                copy_probs(g, k, 2)
                exps(g, k, 3)
                if k == 1:
                    act.wait_ge(qk1_done.sem, qk1_done.at(g, 5))
                    act.activation(kT1[:], ps[:, 5, :], ACT.Identity, bias=b_qkx[:, 1:2]).then_inc(k1_lin.sem, 1)
                copy_probs(g, k, 3)
                copy_o1(g, k)

            def exp_top(g, m):
                act.wait_ge(top_ready.sem, top_ready.at(g, m + 1))
                act.activation(top_e[:], top_e[:], ACT.Exp).then_inc(tope_ready.sem, 1)

            def before_experts(g, m, nxt):
                l = 2 if m == 0 else 5
                if nxt is not None:
                    decays(nxt, STEP_AT_NORM[l])
                copy_norm(g, l)

            def experts0(g, nxt):
                for e in range(E):
                    if 1 <= e <= STEPS_MOE[0] and nxt is not None:
                        decays(nxt, step_in_moe(0, e))
                    for c in range(C0):
                        k = e * C0 + c
                        act.wait_ge(gu_done.sem, gu_done.at(g, k + 1))
                        if k >= 2:
                            act.wait_ge(h0_done.sem, h0_done.at(g, k - 1))
                        act.activation(gated[:, k % 2, :], ps[:, 2 * (k % 2), :], ACT.Tanh, scale=0.5).then_inc(tanh_done.sem, 1)
                        if e < E - 1:
                            act.copy(up_copy[:, k % 2, :], ps[:, 2 * (k % 2) + 1, :]).then_inc(up_copied.sem, 1)
                    if e == 0:
                        exp_top(g, 0)

            def experts1(g, nxt):
                for e in range(E):
                    if 1 <= e <= STEPS_MOE[1] and nxt is not None:
                        decays(nxt, step_in_moe(1, e))
                    for c in range(0, C1, 2):
                        k = e * C1 + c
                        act.wait_ge(up_done.sem, up_done.at(g, k + 1))
                        if e >= 2 and c == 0:
                            act.wait_ge(down_done.sem, down_done.at(g, E + e - 1))
                        act.activation(hidden[:, e % 2, c, :], ps[:, k % 4, :], ACT.Relu, bias=b_1[:, e, c:c + 1]).then_inc(h1_act.sem, 1)
                    if e == 0:
                        exp_top(g, 1)
                    if e == 1:
                        act.wait_ge(gateT_done.sem, gateT_done.at(g, 1))
                        act.copy(gateT[:], ps[:, 4, 0:P]).then_inc(gateT_ready.sem, 1)
                if nxt is not None:
                    copy_ctx(nxt)

            def group(g, nxt):
                attention0(g, nxt)
                before_experts(g, 0, nxt)
                experts0(g, nxt)
                attention1(g, 1, nxt)
                attention1(g, 2, nxt)
                before_experts(g, 1, nxt)
                experts1(g, nxt)

            act.wait_ge(weights["mamba"].sem, need["mamba"])
            act.activation(a_neg[:], a_neg[:], ACT.Exp).then_inc(a_exp.sem, 1)
            copy_norm(0, 0)
            conv_and_gate(0)
            copy_d(0)
            add_dt_bias(0)
            softplus_log(0)
            for n in range(N):
                decays(0, n)
                act.wait_ge(bc_spread.sem, bc_spread.at(0, n + 1))
                if n >= 2:
                    act.wait_ge(hc_done.sem, hc_done.at(0, NC * (n - 1)))
                act.copy(c_copy[:, n % 2, :], ps[:, bc_banks(n, 2)[1], :]).then_inc(c_copied.sem, 1)
            copy_ctx(0)
            with act.Fori(0, NG - 1) as g:
                group(g, g + 1)
            group(NG - 1, None)

        @block.gpsimd
        def _(pool):
            def root(g, l):
                i = min(l, 1)
                pool.wait_ge(var_ready[i].sem, var_ready[i].at(g, max(l, 1)))
                pool.tensor_tensor(rstd[i][:], var_eps[i][:], kc[:, K_HALF:K_ALL], ALU.pow).then_inc(rstd_ready[i].sem, 1)

            def keep_x(g, last):
                if last is not None:
                    pool.wait_ge(x_mixed.sem, x_mixed.at(last, 1))
                    wait_alone(pool, zeros_set, x_loaded.sem, x_loaded.at(g, 16))
                else:
                    pool.wait_ge(x_loaded.sem, x_loaded.at(g, 16))
                pool.tensor_copy(x_keep[:], x_in[:]).then_inc(x_kept.sem, 1)

            def add_bias(g, l, x, bias):
                pool.wait_ge(xn_ready[1].sem, xn_ready[1].at(g, l))
                pool.tensor_tensor(x[:], x[:], bias[:].unsqueeze(1).to_broadcast([P, NP, D]), ALU.add).then_inc(biased.sem, 1)

            def add_y(g, n):
                for c in range(NC):
                    k = NC * n + c
                    pool.wait_ge(hc_done.sem, hc_done.at(g, k + 1))
                    if k >= 2:
                        pool.wait_ge(y_added.sem, y_added.at(g, k - 1))
                    pool.tensor_tensor(y_sum[:, c, :], y_sum[:, c, :], state[:, k % 3, :], ALU.add).then_inc(y_added.sem, 1)

            def normalise(g, p):
                pool.wait_ge(sum_ready.sem, sum_ready.at(g, p + 1))
                v = scores[:, p % 3, :].rearrange("p (r j) -> p r j", j=S)
                pool.tensor_tensor(v, v, row_sum[:, p % 3, :].unsqueeze(2).to_broadcast([P, 2 * HP, S]), ALU.mult).then_inc(normed.sem, 1)

            def shift(g, k, p):
                pool.wait_ge(max_ready.sem, max_ready.at(g, (k - 1) * NP + p + 1))
                v = scores[:, p % 3, :].rearrange("p (r j) -> p r j", j=S)
                pool.tensor_tensor(v, v, row_max[:, p % 3, :].unsqueeze(2).to_broadcast([P, 2 * HP, S]), ALU.subtract).then_inc(shifted1.sem, 1)

            def expand(g, k, x):
                if x == 0:
                    k1_ready = k1_rot if k == 1 else k1_lin
                    pool.wait_ge(k1_ready.sem, k1_ready.at(g, 1))
                if k == 2:
                    pool.wait_ge(s_done.sem, s_done.at(g, k * NP - 2 + 2 * x))
                first, n = POOL_HEADS[x].start, len(POOL_HEADS[x])
                heads = kc[:, K_HEAD + first:K_HEAD + first + n].unsqueeze(1).unsqueeze(3).to_broadcast([P, GH, n, S])
                keys = kT1[:, x * TH:(x + 1) * TH].rearrange("p (b j) -> p b j", b=GH).unsqueeze(2).to_broadcast([P, GH, n, S])
                pool.tensor_tensor(Kx[x][:, :, first:first + n, :], keys, heads, ALU.mult).then_inc(kx_pool.sem, 1)

            def experts0(g, nxt):
                for e in range(E - 1):
                    for c in range(C0):
                        k = e * C0 + c
                        pool.wait_ge(gated_done.sem, gated_done.at(g, k + 1))
                        pool.wait_ge(up_copied.sem, up_copied.at(g, k + 1))
                        if e >= 2 and c == 0:
                            pool.wait_ge(down_done.sem, down_done.at(g, e - 1))
                        pool.tensor_tensor(hidden[:, e % 2, c, :], gated[:, k % 2, :], up_copy[:, k % 2, :],
                                           ALU.mult).then_inc(h0_done.sem, 1)
                    if 1 <= e <= STEPS_MOE[0] and nxt is not None:
                        add_y(nxt, step_in_moe(0, e))

            def group(g, nxt):
                pool.wait_ge(weights["attn0"].sem, need["attn0"])
                add_bias(g, 1, x_mix, bo0)
                if nxt is not None:
                    root(nxt, 0)
                    keep_x(nxt, g)
                for p in range(NP):
                    normalise(g, p)
                root(g, 2)
                if nxt is not None:
                    add_y(nxt, STEP_AT_NORM[2])
                experts0(g, nxt)
                for k, name, bias in ((1, "attn1", bo1), (2, "attnx", box)):
                    root(g, 2 + k)
                    pool.wait_ge(weights[name].sem, need[name])
                    add_bias(g, 2 + k, x_res, bias)
                    if nxt is not None:
                        add_y(nxt, STEP_AT_NORM[2 + k])
                    if k == 1:
                        expand(g, 1, 0)
                        expand(g, 1, 1)
                    for p in range(NP):
                        shift(g, k, p)
                    if k == 1:
                        expand(g, 2, 0)
                        expand(g, 2, 1)
                root(g, 5)
                if nxt is not None:
                    add_y(nxt, STEP_AT_NORM[5])
                    for e in range(1, STEPS_MOE[1] + 1):
                        add_y(nxt, step_in_moe(1, e))
                    root(nxt, 1)

            pool.memset(b_2[:], 0.0)
            pool.memset(gate[:], 0.0)
            pool.memset(V1[:], 0.0).then_inc(zeros_set.sem, 1)
            for e in range(2):
                pool.wait_ge(zeros_set.sem, 1 + e)
                pool.memset(V1[e * S:(e + 1) * S, :, :, e, HD:], 1.0).then_inc(zeros_set.sem, 1)
            pool.wait_ge(zeros_set.sem, 3)
            pool.wait_ge(weights["mamba"].sem, need["mamba"])
            keep_x(0, None)
            root(0, 0)
            for k in range(NC * N):
                pool.wait_ge(scan_done.sem, scan_done.at(0, k + 1))
                pool.wait_ge(c_copied.sem, c_copied.at(0, k // NC + 1))
                if k >= 4:
                    pool.wait_ge(y_added.sem, y_added.at(0, k - 3))
                pool.tensor_tensor(weighed[:, k % 4, :], state[:, k % 3, :], c_copy[:, k // NC % 2, :], ALU.mult).then_inc(hc_done.sem, 1)
            root(0, 1)
            with pool.Fori(0, NG - 1) as g:
                group(g, g + 1)
            group(NG - 1, None)

        @block.vector
        def _(dve):
            links = {mamba_chain: 0, layer_chain: 0}

            def link(chain, g, ins):
                links[chain] += 1
                ins.then_inc(chain.sem, 1)
                dve.wait_ge(chain.sem, chain.at(g, links[chain]))

            def link_alone(chain, g, ins):
                links[chain] += 1
                ins.then_inc(chain.sem, 1)
                wait_alone(dve, setup, chain.sem, chain.at(g, links[chain]))

            def norm(g, l):
                src = (x_in, x_mix)[l] if l < 2 else x_res
                chain = mamba_chain if l < 2 else layer_chain
                i = min(l, 1)
                if l == 0:
                    dve.wait_ge(x_loaded.sem, x_loaded.at(g, 16))
                for t in range(NP):
                    ins = dve.bn_stats(stats[i][:, t, :], src[:, t, :])
                link_alone(chain, g, ins)
                for t in range(NP):
                    ins = dve.bn_aggr(mean_var[i][:, t, :], stats[i][:, t, :])
                link(chain, g, ins)
                dve.tensor_scalar(var_eps[i][:], mean_var[i][:, :, 1], LN_EPS, None, ALU.add).then_inc(var_ready[i].sem, 1)
                dve.wait_ge(rstd_ready[i].sem, rstd_ready[i].at(g, max(l, 1)))
                for t in range(NP):
                    ins = dve.tensor_scalar(xn[i][:, t, :], src[:, t, :], mean_var[i][:, t, 0:1], rstd[i][:, t:t + 1], ALU.subtract, ALU.mult)
                ins.then_inc(xn_ready[i].sem, 1)

            def conv(g):
                for c in range(NC):
                    dve.wait_ge(conv_mid.sem, conv_mid.at(g, c + 1))
                    u = u_conv[:, c, :].rearrange("p (b t) -> p b t", b=GB)
                    raw = ps[:, 4 + c, :].rearrange("p (b t) -> p b t", b=GB)
                    link(mamba_chain, g, dve.scalar_tensor_tensor(u[:, :, 1:S], raw[:, :, 0:S - 1], w_conv[:, c, 0:1], u[:, :, 1:S], ALU.mult, ALU.add))
                    dve.scalar_tensor_tensor(u[:, :, 0:S - 1], raw[:, :, 1:S], w_conv[:, c, 2:3], u[:, :, 0:S - 1],
                                             ALU.mult, ALU.add).then_inc(conv_done.sem, 1)

            def split_bc(g):
                dve.wait_ge(xproj_done.sem, xproj_done.at(g, 1))
                link(mamba_chain, g, dve.tensor_copy(bc_split[:], ps[0:96, 6, :]))
                link(mamba_chain, g, dve.tensor_tensor(bc_res, ps[0:96, 6, :], bc_split[:], ALU.subtract))
                dve.tensor_copy(bc_split[32:64, :], bc_res[32:64, :])
                link(mamba_chain, g, dve.tensor_copy(bc_mid[64:96, :], bc_res[64:96, :]))
                dve.tensor_tensor(bc_split[64:96, :], bc_res[64:96, :], bc_mid[64:96, :], ALU.subtract).then_inc(split_ready.sem, 1)

            def minus_abs(g):
                dve.wait_ge(z_ready.sem, z_ready.at(g, 2))
                dve.scalar_tensor_tensor(dt_e[:], dt_z[:], -1.0, dt_z[:], ALU.mult, ALU.min).then_inc(nz_ready.sem, 1)

            def find_delta(g):
                dve.wait_ge(ln_ready.sem, ln_ready.at(g, 1))
                link(mamba_chain, g, dve.scalar_tensor_tensor(delta[:], dt_z[:], 0.0, dt_e[:], ALU.max, ALU.add))
                for c in range(NC):
                    dve.tensor_scalar(y_sum[:, c, :], u_act[:, c, :], d_par[:, c:c + 1], None, ALU.mult)
                link(mamba_chain, g, dve.tensor_tensor(du[:], delta[:], u_act, ALU.mult))
                dve.memset(delta.rearrange("p c (b t) -> p (c b) t", t=S)[:, :, 0:1], FAR).then_inc(delta_ready.sem, 1)

            def start_step(g, n, b_bank, free):
                dve.wait_ge(bc_spread.sem, bc_spread.at(g, n + 1))
                for c in range(NC):
                    k = NC * n + c
                    if k >= 3:
                        dve.wait_ge(free.sem, free.at(g, k - 2))
                    dve.tensor_tensor(state[:, k % 3, :], du[:, c, :], ps[:, b_bank, :], ALU.mult).then_inc(bu_done.sem, 1)
                for c in range(NC):
                    k = NC * n + c
                    dve.wait_ge(bu_done.sem, bu_done.at(g, k + 1))
                    dve.wait_ge(decay_ready.sem, decay_ready.at(g, k + 1))
                    dve.tensor_tensor_scan(state[:, k % 3, :], decay[:, k % 3, :], state[:, k % 3, :], 0.0, ALU.mult, ALU.add).then_inc(scan_done.sem, 1)

            def scan_step(g, n):
                b_bank, c_bank = bc_banks(n, 1)
                start_step(g, n, b_bank, y_added)
                for c in range(NC):
                    k = NC * n + c
                    dve.wait_ge(scan_done.sem, scan_done.at(g, k + 1))
                    dve.tensor_tensor(state[:, k % 3, :], state[:, k % 3, :], ps[:, c_bank, :], ALU.mult).then_inc(hc_done.sem, 1)

            def gate_y(g):
                dve.wait_ge(y_added.sem, y_added.at(g, NC * N))
                dve.wait_ge(gate_ready.sem, gate_ready.at(g, 2))
                dve.tensor_tensor(y_sum[:], y_sum[:], gate_act[:], ALU.mult).then_inc(yg_ready.sem, 1)

            def mix_x(g):
                dve.wait_ge(mamba_done.sem, mamba_done.at(g, 1))
                dve.wait_ge(x_kept.sem, x_kept.at(g, 1))
                dve.tensor_tensor(x_mix.rearrange("p t d -> p (t d)"), x_keep.rearrange("p t d -> p (t d)"), ps[:, 6, :],
                                  ALU.add).then_inc(x_mixed.sem, 1)
                dve.wait_ge(x_mixed.sem, x_mixed.at(g, 1))

            def softmax_front(g, k, p):
                dve.wait_ge(s_done.sem, s_done.at(g, k * NP + p + 1))
                s_ps = ps[:, 2 * (p % 2):2 * (p % 2) + 2, :].rearrange("p k f -> p (k f)")
                if p == 3:
                    dve.wait_ge(pT_done.sem, pT_done.at(g, k * NP + 1))
                v = scores[:, p % 3, :]
                if k == 0:
                    bias = bias0[:, p * P:(p + 1) * P].unsqueeze(1).to_broadcast([P, HP, P])
                    ins = dve.tensor_tensor(v.rearrange("p (h j) -> p h j", h=HP), s_ps.rearrange("p (h j) -> p h j", h=HP), bias, ALU.add)
                else:
                    at = K_CAUSAL if k == 1 else K_CAUSAL9
                    bias = kc[:, at:at + S].unsqueeze(1).to_broadcast([P, 2 * HP, S])
                    ins = dve.scalar_tensor_tensor(v.rearrange("p (r j) -> p r j", j=S), s_ps.rearrange("p (r j) -> p r j", j=S),
                                                   HD ** -0.5, bias, ALU.mult, ALU.add)
                ins.then_inc(s_read.sem, 1)
                dve.wait_ge(s_read.sem, s_read.at(g, k * NP + p + 1))
                rows = v.rearrange("p (r j) -> p r j", j=S)
                ins = dve.reduce_max(row_max[:, p % 3, :], rows, AX.X)
                if k == 0:
                    link(layer_chain, g, ins)
                    dve.tensor_tensor(rows, rows, row_max[:, p % 3, :].unsqueeze(2).to_broadcast([P, 2 * HP, S]),
                                      ALU.subtract).then_inc(shifted0.sem, 1)
                else:
                    ins.then_inc(max_ready.sem, 1)

            def softmax_sum(g, p):
                dve.wait_ge(exp_done.sem, exp_done.at(g, p + 1))
                link(layer_chain, g, dve.reduce_sum(row_sum[:, p % 3, :], scores[:, p % 3, :].rearrange("p (r j) -> p r j", j=S), AX.X))
                dve.reciprocal(row_sum[:, p % 3, :], row_sum[:, p % 3, :]).then_inc(sum_ready.sem, 1)

            def copy_queries0(g):
                for u in range(4):
                    dve.wait_ge(q0_done.sem, q0_done.at(g, 4 + u + 1))
                    dve.tensor_scalar(QT[:, 1, 2 * u:2 * u + 2, :].rearrange("p h t -> p (h t)"), ps[:, u, :], 0.125, None,
                                      ALU.mult).then_inc(q0_ready[1].sem, 1)

            def mask_bias(g):
                dve.wait_ge(mask_loaded.sem, mask_loaded.at(g, 16))
                dve.tensor_scalar(bias0[:], mask_in[:], -NEG, NEG, ALU.mult, ALU.add).then_inc(mask_free.sem, 1)
                dve.wait_ge(mask_free.sem, mask_free.at(g, 1))
                b3 = bias0.rearrange("p (b j) -> p b j", b=GB)
                link(layer_chain, g, dve.tensor_tensor(b3, b3, kc[:, K_CAUSAL:K_CAUSAL9].unsqueeze(1).to_broadcast([P, GB, S]), ALU.min))

            def attention0(g, nxt):
                mask_bias(g)
                if nxt is not None:
                    norm(nxt, 0)
                if nxt is not None:
                    conv(nxt)
                softmax_front(g, 0, 0)
                if nxt is not None:
                    split_bc(nxt)
                softmax_front(g, 0, 1)
                softmax_sum(g, 0)
                copy_queries0(g)
                softmax_sum(g, 1)
                if nxt is not None:
                    minus_abs(nxt)
                    find_delta(nxt)
                for p in (2, 3):
                    softmax_front(g, 0, p)
                    softmax_sum(g, p)
                dve.wait_ge(attn_done.sem, attn_done.at(g, 1))
                dve.wait_ge(biased.sem, biased.at(g, 1))
                dve.wait_ge(out_free.sem, out_free.at(g, 1))
                link(layer_chain, g, dve.tensor_tensor(x_res.rearrange("p t d -> p (t d)"), x_mix.rearrange("p t d -> p (t d)"), ps[:, 0, :], ALU.add))

            def rotate(g, c):
                cos = kc[:, K_COS:K_SIN].unsqueeze(1).to_broadcast([P, GB, S])
                sin = kc[:, K_SIN:K_HEAD].unsqueeze(1).to_broadcast([P, GB, S])
                part = scores[:, c, :].rearrange("p (x t) -> p x t", x=2)
                for swapped, table, b in ((0, cos, b_qk1), (1, sin, b_sw1)):
                    dve.wait_ge(qk1_done.sem, qk1_done.at(g, 2 * (1 - c) + swapped + 1))
                    ins = dve.scalar_tensor_tensor(part[:, swapped, :].rearrange("p (b i) -> p b i", b=GB),
                                                   ps[:, 2 * c + swapped, :].rearrange("p (b i) -> p b i", b=GB),
                                                   b[:, c:c + 1], table, ALU.add, ALU.mult)
                link(layer_chain, g, ins)
                dst, ready = (q1, q1_rot) if c == 0 else (kT1, k1_rot)
                dve.tensor_tensor(dst[:], part[:, 0, :], part[:, 1, :], ALU.add).then_inc(ready.sem, 1)

            def add_value_bias(g, k):
                dve.wait_ge(v1_done.sem, v1_done.at(g, k))
                for e in range(2):
                    r = slice(e * S, (e + 1) * S)
                    bias = (bv1 if k == 1 else bvx)[r].rearrange("p (h e d) -> p e h d", h=HP, e=2)[:, e].unsqueeze(1).to_broadcast([S, GB, HP, HD])
                    ins = dve.tensor_tensor(V1[r, :, :, e, 0:HD], ps[r, 5, :].rearrange("p (b h d) -> p b h d", b=GB, h=HP), bias, ALU.add)
                ins.then_inc(v1_ready.sem, 1)

            def expand(g, k):
                k1_ready = k1_rot if k == 1 else k1_lin
                dve.wait_ge(k1_ready.sem, k1_ready.at(g, 1))
                if k == 2:
                    dve.wait_ge(s_done.sem, s_done.at(g, k * NP - 2))
                for h in DVE_HEADS:
                    ins = dve.tensor_scalar(Kx[0][:, :, h, :], kT1[:, 0:TH].rearrange("p (b j) -> p b j", b=GH),
                                            kc[:, K_HEAD + h:K_HEAD + h + 1], None, ALU.mult)
                ins.then_inc(kx_dve.sem, 1)

            def scale_outputs(g, k, p):
                dve.wait_ge(o_done.sem, o_done.at(g, k * NP + p + 1))
                o_ps = ps[:, 6 + p % 2, 0:HEADS * (HD + 1)].rearrange("p (h f) -> p h f", h=HEADS)
                link(layer_chain, g, dve.reciprocal(row_sum[:, p % 3, :], o_ps[:, :, HD]))
                dve.tensor_tensor(O1[:, p % 2].rearrange("p (h d) -> p h d", h=HEADS), o_ps[:, :, 0:HD],
                                  row_sum[:, p % 3, :].unsqueeze(2).to_broadcast([P, HEADS, HD]), ALU.mult).then_inc(o1_ready.sem, 1)

            def attention1(g, k, nxt):
                norm(g, 2 + k)
                if nxt is not None:
                    scan_step(nxt, STEP_AT_NORM[2 + k])
                if k == 1:
                    rotate(g, 1)
                    expand(g, 1)
                    rotate(g, 0)
                    add_value_bias(g, 1)
                    dve.wait_ge(q1_rot.sem, q1_rot.at(g, 1))
                softmax_front(g, k, 0)
                if k == 2:
                    add_value_bias(g, 2)
                for p in range(1, NP):
                    softmax_front(g, k, p)
                for p in range(NP):
                    scale_outputs(g, k, p)
                if k == 1:
                    expand(g, 2)
                dve.wait_ge(attn_done.sem, attn_done.at(g, 1 + k))
                dve.wait_ge(biased.sem, biased.at(g, 1 + k))
                x_flat = x_res.rearrange("p t d -> p (t d)")
                link(layer_chain, g, dve.tensor_tensor(x_flat, x_flat, ps[:, 0, :], ALU.add))

            def routing(g, m):
                dve.wait_ge(route_done.sem, route_done.at(g, m + 1))
                ps_l = ps[:, 5, 0:NP * E].rearrange("p (t e) -> p t e", t=NP)
                if m == 0:
                    link_alone(layer_chain, g, dve.tensor_copy(logits[:], ps_l))
                else:
                    link_alone(layer_chain, g, dve.tensor_tensor(logits[:], ps_l, br1[:].unsqueeze(1).to_broadcast([P, NP, E]), ALU.add))
                for t in range(NP):
                    ins = dve.max(top[:, t, :], logits[:, t, :])
                link_alone(layer_chain, g, ins)
                for t in range(NP):
                    ins = dve.max_index(top_at[:, t, :], top[:, t, :], logits[:, t, :])
                dve.tensor_tensor(top_e[:], top[:, :, 1], top[:, :, 0], ALU.subtract).then_inc(top_ready.sem, 1)
                dve.wait_ge(top_ready.sem, top_ready.at(g, m + 1))
                link(layer_chain, g, dve.tensor_copy(top_atf[:], top_at[:, :, 0:2]))
                iota = kc[:, K_IOTA:K_HALF].unsqueeze(1).to_broadcast([P, NP, E])
                for r in range(2):
                    dve.tensor_tensor(pick[:, :, r, :], iota, top_atf[:, :, r:r + 1].to_broadcast([P, NP, E]), ALU.is_equal)
                dve.wait_ge(tope_ready.sem, tope_ready.at(g, m + 1))
                link(layer_chain, g, dve.tensor_scalar(top_w[:, :, 1], top_e[:], 1.0, 2.0 if m == 0 else 1.0, ALU.add, ALU.mult))
                link(layer_chain, g, dve.reciprocal(top_w[:, :, 0], top_w[:, :, 1]))
                link(layer_chain, g, dve.tensor_tensor(top_w[:, :, 1], top_w[:, :, 0], top_e[:], ALU.mult))
                link(layer_chain, g, dve.tensor_tensor(pick[:], pick[:], top_w[:].unsqueeze(3).to_broadcast([P, NP, 2, E]), ALU.mult))
                dve.tensor_tensor(gate[:, :, 0:E], pick[:, :, 0, :], pick[:, :, 1, :], ALU.add).then_inc(gate_w.sem, 1)

            def accumulate(g, m, e):
                dve.wait_ge(down_done.sem, down_done.at(g, m * E + e + 1))
                if e == 0:
                    dve.wait_ge(gate_w.sem, gate_w.at(g, m + 1))
                if e >= 1:
                    dve.wait_ge(acc_done.sem, acc_done.at(g, m * E + e))
                for t in range(NP):
                    ins = dve.scalar_tensor_tensor(x_res[:, t, :], ps[:, 4 + e % 2, t * P:(t + 1) * P], gate[:, t, e:e + 1],
                                                   x_res[:, t, :], ALU.mult, ALU.add)
                ins.then_inc(acc_done.sem, 1)

            def experts0(g, nxt):
                for e in range(E + 1):
                    for c in range(C0 if e < E else 0):
                        k = e * C0 + c
                        dve.wait_ge(tanh_done.sem, tanh_done.at(g, k + 1))
                        dve.scalar_tensor_tensor(gated[:, k % 2, :], gated[:, k % 2, :], 1.0, ps[:, 2 * (k % 2), :],
                                                 ALU.add, ALU.mult).then_inc(gated_done.sem, 1)
                        if e == E - 1:
                            dve.wait_ge(gated_done.sem, gated_done.at(g, k + 1))
                            if c == 0:
                                dve.wait_ge(down_done.sem, down_done.at(g, e - 1))
                            dve.tensor_tensor(hidden[:, e % 2, c, :], gated[:, k % 2, :], ps[:, 2 * (k % 2) + 1, :],
                                              ALU.mult).then_inc(h0_last.sem, 1)
                    if e == 0:
                        routing(g, 0)
                    if 1 <= e <= STEPS_MOE[0] and nxt is not None:
                        scan_step(nxt, step_in_moe(0, e))
                    if e >= 1:
                        accumulate(g, 0, e - 1)
                dve.wait_ge(acc_done.sem, acc_done.at(g, E))

            def experts1(g, nxt):
                for e in range(E + 1):
                    for c in range(1, C1 if e < E else 0, 2):
                        k = e * C1 + c
                        dve.wait_ge(up_done.sem, up_done.at(g, k + 1))
                        if e >= 2 and c == 1:
                            dve.wait_ge(down_done.sem, down_done.at(g, E + e - 1))
                        dve.tensor_scalar(hidden[:, e % 2, c, :], ps[:, k % 4, :], b_1[:, e, c:c + 1], 0.0, ALU.add,
                                          ALU.max).then_inc(h1_dve.sem, 1)
                    if e == 0:
                        routing(g, 1)
                    if 1 <= e <= STEPS_MOE[1] and nxt is not None:
                        scan_step(nxt, step_in_moe(1, e))
                    if e == 1:
                        dve.wait_ge(b2_done.sem, b2_done.at(g, 1))
                        x_flat = x_res.rearrange("p t d -> p (t d)")
                        dve.tensor_tensor(x_flat, x_flat, ps[:, 5, :], ALU.add).then_inc(b2_added.sem, 1)
                        dve.wait_ge(b2_added.sem, b2_added.at(g, 1))
                    if e == E and nxt is not None:
                        gate_y(nxt)
                    if e >= 1:
                        accumulate(g, 1, e - 1)
                    if e == E and nxt is not None:
                        mix_x(nxt)
                        norm(nxt, 1)

            def group(g, nxt):
                links.update({mamba_chain: 0, layer_chain: 0})
                attention0(g, nxt)
                norm(g, 2)
                if nxt is not None:
                    scan_step(nxt, STEP_AT_NORM[2])
                experts0(g, nxt)
                attention1(g, 1, nxt)
                attention1(g, 2, nxt)
                norm(g, 5)
                if nxt is not None:
                    scan_step(nxt, STEP_AT_NORM[5])
                experts1(g, nxt)
                assert links == {mamba_chain: 0 if nxt is None else MAMBA_LINKS, layer_chain: LAYER_LINKS}, list(links.values())

            dve.wait_ge(weights["mamba"].sem, need["mamba"])
            dve.wait_ge(a_exp.sem, 1)
            dve.tensor_scalar(a_neg[:], a_neg[:], -1.0, None, ALU.mult)
            dve.tensor_copy(sel[:], kc[0:96, K_SEL:K_IOTA]).then_inc(setup.sem, 1)
            dve.wait_ge(setup.sem, 1)
            norm(0, 0)
            conv(0)
            split_bc(0)
            minus_abs(0)
            find_delta(0)
            for n in range(N):
                start_step(0, n, bc_banks(n, 2)[0], hc_done)
            dve.wait_ge(y_added.sem, y_added.at(0, NC * N))
            dve.tensor_tensor(y_sum[:], y_sum[:], ps[:, 0:NC, :], ALU.add).then_inc(y0_ready.sem, 1)
            dve.wait_ge(y0_ready.sem, 1)
            gate_y(0)
            mix_x(0)
            norm(0, 1)
            assert links[mamba_chain] == MAMBA_LINKS, links[mamba_chain]
            dve.wait_ge(weights["attn1"].sem, need["attn1"])
            wq = w_qkv1[:, 0:2 * D].rearrange("p (k two) -> p k two", two=2)
            sw = w_sw1[:].rearrange("p (k two) -> p k two", two=2)
            for odd in range(2):
                ins = dve.tensor_copy(sw[:, :, odd], wq[:, :, 1 - odd])
            ins.then_inc(swapped_set.sem, 1)
            with dve.Fori(0, NG - 1) as g:
                group(g, g + 1)
            group(NG - 1, None)


DVE_HEADS = range(4)
POOL_HEADS = range(4, 9), range(10, HEADS)
ACT_HEADS = range(9, HEADS), range(10)


def probs_bank(k, p):
    return 4 if k == 0 or p < 2 else 2 * (p % 2)


STEP_AT_NORM = {2: 0, 3: 6, 4: 7, 5: 8}
STEPS_MOE = 5, 7


def step_in_moe(m, e):
    return (1, 9)[m] + e - 1


def bc_banks(n, ring):
    return (6, 7) if ring == 1 else (4 + n % 2, 6 + n % 2)


def pairs_of(x, g):
    return x.rearrange("(b s) i d -> (s i) b d", s=2)[:, bass.ds(g * NP, NP), :]


NAMES = """x ctx_1024 mask_BxS2_bk0 L0_attn_in_proj_w L0_attn_conv_w L0_attn_conv_b L0_attn_x_proj_w L0_attn_dt_proj_w
L0_attn_dt_proj_b L0_attn_out_proj_w L0_attn_A_log L0_attn_D_param L0_xattn_Wq L0_xattn_Wkv L0_xattn_Wo L0_xattn_bo
L0_ffn_gate_w L0_ffn_gate_up_w L0_ffn_down_w L1_attn_Wqkv L1_attn_bqkv L1_attn_Wproj L1_attn_bproj L1_xattn_Wq L1_xattn_bq
L1_xattn_Wk L1_xattn_bk L1_xattn_Wv L1_xattn_bv L1_xattn_Wo L1_xattn_bo L1_ffn_Wr L1_ffn_br L1_ffn_W1 L1_ffn_b1
L1_ffn_W2 L1_ffn_b2""".split()


def kernel(**inputs):
    import concourse.bacc as bacc
    from concourse.bass_utils import run_bass_kernel_spmd

    nc = bacc.Bacc("TRN2", target_bir_lowering=False, num_devices=1)
    arrays, aps = {}, {}
    for name in NAMES + ["shape_constants"]:
        v = shape_constants() if name == "shape_constants" else np.ascontiguousarray(inputs[name])
        arrays[f"in_{name}"] = v
        aps[name] = nc.dram_tensor(f"in_{name}", v.shape, mybir.dt.from_np(v.dtype), kind="ExternalInput").ap()
    out = nc.dram_tensor("out_x", (BATCH, S, D), F32, kind="ExternalOutput").ap()
    build(nc, aps, out)
    result = run_bass_kernel_spmd(nc, [arrays], core_ids=[0])
    return result.results[0]["out_x"]
```
